# Optimizing a Trainium2 kernel written in Bass

```python
import numpy as np
import jax
import jax.numpy as jnp

def _softmax(x, axis=-1):
    return jax.nn.softmax(x, axis=axis)

def _gelu(x):
    return jax.nn.gelu(x, approximate=True)

def _silu(x):
    return jax.nn.silu(x)

def _sigmoid(x):
    return jax.nn.sigmoid(x)

def _layernorm(x, axis=-1, eps=1e-05):
    m = jnp.mean(x, axis=axis, keepdims=True)
    v = jnp.var(x, axis=axis, keepdims=True)
    return (x - m) / jnp.sqrt(v + eps)

def _scatter_add(tgt, idx, src, axis=0):
    return tgt.at[idx].add(src)

def _segment_sum(src, seg, n):
    return jax.ops.segment_sum(src, seg, n)
kernel_name = 'mk_sandwich_d1_jaxref_r4_e68805'

def setup_inputs(seed: int=0):
    np.random.seed(seed)
    _w = jnp.asarray

    def _L0_attn_setup():
        import jax, jax.numpy as jnp
        import numpy as np
        B, S, D = (2, 512, 256)
        H, DQ, DV = (16, 64, 64)
        key = jax.random.key(seed)
        k1, k2, k3, k4, k5 = jax.random.split(key, 5)
        scale = 0.02
        return {'x': jax.random.normal(k1, (B, S, D), dtype=jnp.float32), 'w_q': jax.random.normal(k2, (H, DQ, D), dtype=jnp.float32) * scale, 'w_k': jax.random.normal(k3, (H, DQ, D), dtype=jnp.float32) * scale, 'w_v': jax.random.normal(k4, (H, DV, D), dtype=jnp.float32) * scale, 'w_o': jax.random.normal(k5, (D, H * DV), dtype=jnp.float32) * scale}
    _L0_attn_in = _L0_attn_setup()

    def _L0_ffn_setup():
        import jax, jax.numpy as jnp
        import numpy as np
        HID = 256
        NH = 16
        NKV = 4
        HD = HID // NH
        E = 8
        TOPK = 2
        FFN = 512
        EPS = 1e-05
        THETA = 10000.0

        def _rmsnorm(x, w):
            var = jnp.mean(x * x, axis=-1, keepdims=True)
            return x * jax.lax.rsqrt(var + EPS) * w

        def _rope_tables(S):
            inv_freq = 1.0 / THETA ** (jnp.arange(0, HD, 2, dtype=jnp.float32) / HD)
            freqs = jnp.arange(S, dtype=jnp.float32)[:, None] * inv_freq[None, :]
            emb = jnp.concatenate([freqs, freqs], axis=-1)
            return (jnp.cos(emb), jnp.sin(emb))

        def _apply_rope(t, cos, sin):
            t1, t2 = jnp.split(t, 2, axis=-1)
            rot = jnp.concatenate([-t2, t1], axis=-1)
            return t * cos[None, :, None, :] + rot * sin[None, :, None, :]
        key = jax.random.key(seed)
        ks = jax.random.split(key, 6)
        B, S = (1, 512)
        x = jax.random.normal(ks[0], (B, S, HID), dtype=jnp.float32)
        wqkv = jax.random.normal(ks[1], ((NH + 2 * NKV) * HD, HID), dtype=jnp.float32) * 0.02
        wo = jax.random.normal(ks[2], (HID, NH * HD), dtype=jnp.float32) * 0.02
        gate_w = jax.random.normal(ks[3], (E, HID), dtype=jnp.float32) * 0.02
        w13 = jax.random.normal(ks[4], (E, 2 * FFN, HID), dtype=jnp.float32) * 0.02
        w2 = jax.random.normal(ks[5], (E, HID, FFN), dtype=jnp.float32) * 0.02
        return {'x': x, 'ln1_w': jnp.ones((HID,), jnp.float32), 'ln2_w': jnp.ones((HID,), jnp.float32), 'wqkv': wqkv, 'wo': wo, 'gate_w': gate_w, 'w13': w13, 'w2': w2}
    _L0_ffn_in = _L0_ffn_setup()
    _d = {'L0_attn_x': _L0_attn_in['x'], 'L0_attn_w_q': _L0_attn_in['w_q'], 'L0_attn_w_k': _L0_attn_in['w_k'], 'L0_attn_w_v': _L0_attn_in['w_v'], 'L0_attn_w_o': _L0_attn_in['w_o'], 'L0_ffn_ln1_w': _L0_ffn_in['ln1_w'], 'L0_ffn_ln2_w': _L0_ffn_in['ln2_w'], 'L0_ffn_wqkv': _L0_ffn_in['wqkv'], 'L0_ffn_wo': _L0_ffn_in['wo'], 'L0_ffn_gate_w': _L0_ffn_in['gate_w'], 'L0_ffn_w13': _L0_ffn_in['w13'], 'L0_ffn_w2': _L0_ffn_in['w2']}
    _x0 = _d['L0_attn_x']
    _d['L0_attn_x'] = jax.random.normal(jax.random.fold_in(jax.random.key(seed), 1), (4, 1024, 256), dtype=_x0.dtype)
    del _x0
    return _d

def reference(L0_attn_x, L0_attn_w_q, L0_attn_w_k, L0_attn_w_v, L0_attn_w_o, L0_ffn_ln1_w, L0_ffn_ln2_w, L0_ffn_wqkv, L0_ffn_wo, L0_ffn_gate_w, L0_ffn_w13, L0_ffn_w2):

    def _L0_attn_ref(x, w_q, w_k, w_v, w_o):
        import jax, jax.numpy as jnp
        import numpy as np
        B, S, D = (2, 512, 256)
        H, DQ, DV = (16, 64, 64)
        b, s, d = x.shape
        q = jnp.einsum('bsd,hqd->bhsq', x, w_q)
        k = jnp.einsum('bsd,hqd->bhsq', x, w_k)
        v = jnp.einsum('bsd,hvd->bhsv', x, w_v)
        scores = jnp.einsum('bhsq,bhtq->bhst', q, k)
        causal = jnp.triu(jnp.ones((s, s), dtype=bool), k=1)
        masked = jnp.where(causal, -jnp.inf, scores)
        dq = w_q.shape[1]
        weights = jax.nn.softmax(masked / jnp.sqrt(jnp.float32(dq)), axis=-1)
        out = jnp.einsum('bhst,bhtv->bhsv', weights, v)
        cat = out.transpose(0, 2, 1, 3).reshape(b, s, -1)
        return jnp.einsum('bsf,df->bsd', cat, w_o)

    def _L0_ffn_ref(x, ln1_w, ln2_w, wqkv, wo, gate_w, w13, w2):
        import jax, jax.numpy as jnp
        import numpy as np
        HID = 256
        NH = 16
        NKV = 4
        HD = HID // NH
        E = 8
        TOPK = 2
        FFN = 512
        EPS = 1e-05
        THETA = 10000.0

        def _rmsnorm(x, w):
            var = jnp.mean(x * x, axis=-1, keepdims=True)
            return x * jax.lax.rsqrt(var + EPS) * w

        def _rope_tables(S):
            inv_freq = 1.0 / THETA ** (jnp.arange(0, HD, 2, dtype=jnp.float32) / HD)
            freqs = jnp.arange(S, dtype=jnp.float32)[:, None] * inv_freq[None, :]
            emb = jnp.concatenate([freqs, freqs], axis=-1)
            return (jnp.cos(emb), jnp.sin(emb))

        def _apply_rope(t, cos, sin):
            t1, t2 = jnp.split(t, 2, axis=-1)
            rot = jnp.concatenate([-t2, t1], axis=-1)
            return t * cos[None, :, None, :] + rot * sin[None, :, None, :]
        B, S, _ = x.shape
        h = _rmsnorm(x, ln1_w)
        qkv = jnp.einsum('bsh,oh->bso', h, wqkv)
        q = qkv[..., :NH * HD].reshape(B, S, NH, HD)
        k = qkv[..., NH * HD:(NH + NKV) * HD].reshape(B, S, NKV, HD)
        v = qkv[..., (NH + NKV) * HD:].reshape(B, S, NKV, HD)
        cos, sin = _rope_tables(S)
        q = _apply_rope(q, cos, sin)
        k = _apply_rope(k, cos, sin)
        groups = NH // NKV
        k = jnp.repeat(k, groups, axis=2)
        v = jnp.repeat(v, groups, axis=2)
        scale = HD ** (-0.5)
        scores = jnp.einsum('bqhd,bkhd->bhqk', q, k) * scale
        causal = jnp.tril(jnp.ones((S, S), dtype=bool))
        scores = jnp.where(causal[None, None], scores, jnp.finfo(scores.dtype).min)
        probs = jax.nn.softmax(scores, axis=-1)
        attn = jnp.einsum('bhqk,bkhd->bqhd', probs, v).reshape(B, S, NH * HD)
        x = x + jnp.einsum('bso,ho->bsh', attn, wo)
        h = _rmsnorm(x, ln2_w).reshape(-1, HID)
        T = h.shape[0]
        logits = jnp.einsum('th,eh->te', h, gate_w)
        rprobs = jax.nn.softmax(logits.astype(jnp.float32), axis=-1)
        topw, topi = jax.lax.top_k(rprobs, TOPK)
        topw = topw / jnp.sum(topw, axis=-1, keepdims=True)
        wfull = jnp.zeros((T, E), jnp.float32).at[jnp.arange(T)[:, None], topi].set(topw)
        wfull = wfull.astype(h.dtype)
        out = jnp.zeros((T, HID), h.dtype)
        for e in range(E):
            w1 = w13[e, :FFN]
            w3 = w13[e, FFN:]
            g = jax.nn.silu(h @ w1.T) * (h @ w3.T)
            out = out + jnp.einsum('tf,hf->th', g, w2[e]) * wfull[:, e:e + 1]
        return x + out.reshape(B, S, HID)
    x = L0_attn_x
    x = x + _layernorm(_L0_attn_ref(_layernorm(x, axis=-1), L0_attn_w_q, L0_attn_w_k, L0_attn_w_v, L0_attn_w_o), axis=-1)
    x = x + _layernorm(_L0_ffn_ref(_layernorm(x, axis=-1), L0_ffn_ln1_w, L0_ffn_ln2_w, L0_ffn_wqkv, L0_ffn_wo, L0_ffn_gate_w, L0_ffn_w13, L0_ffn_w2), axis=-1)
    return x

_drawn_inputs = setup_inputs


def setup_inputs(seed=0):
    import zlib

    import numpy as np

    out = dict(_drawn_inputs(seed))
    spreads = {'L0_ffn_ln1_w': (1.0, 0.6), 'L0_ffn_ln2_w': (1.0, 0.6)}
    factors = {'L0_ffn_gate_w': 8.0, 'L0_ffn_w13': 7.027, 'L0_ffn_w2': 7.069}
    for name, (base, spread) in spreads.items():
        noise = np.random.default_rng([zlib.crc32(name.encode()), seed]).standard_normal(out[name].shape)
        drawn = base * np.exp(spread * noise) if base else spread * noise
        out[name] = jnp.asarray(drawn.astype(out[name].dtype))
    for name, factor in factors.items():
        out[name] = (out[name] * factor).astype(out[name].dtype)
    return out
```

```python
from contextlib import ExitStack

import numpy as np

import concourse.bass as bass
from concourse import mybir

F32 = mybir.dt.float32
F32R = mybir.dt.float32r
BF16 = mybir.dt.bfloat16
ALU = mybir.AluOpType
ACT = mybir.ActivationFunctionType
AX = mybir.AxisListType

P = 128
BANK = 512
B, S, D = 4, 1024, 256
TOK = B * S
NT = TOK // P
KD = D // P
ST_N = S // P
EPS = 1e-5
NEG = -1e30

H1, DH1 = 16, 64
PAIRS = H1 // 2

UNITS = [(c, j) for c in range(S // BANK) for j in range((c + 1) * BANK // P)]
NU = len(UNITS)
LAST = [n for n, (c, j) in enumerate(UNITS) if j == (c + 1) * BANK // P - 1]
MAXU = [(i, c) for i in range(ST_N) for c in range(i * P // BANK + 1)]


def first_col(c, j):
    return max(0, j * P - c * BANK)


def is_diag(c, j):
    return j * P >= c * BANK


def normalise(nc, x, hold):
    with ExitStack() as ctx:
        sb = lambda name, shape, dt=F32: ctx.enter_context(nc.sbuf_tensor(name, shape, dt))
        sem = lambda name: ctx.enter_context(nc.semaphore(name))
        X = sb("n_x", [P, NT, D])
        XN = sb("n_xn", [P, 4, D])
        stats = sb("n_stats", [P, NT, 6])
        scale = sb("n_scale", [P, NT])
        shift = sb("n_shift", [P, NT])
        mean2 = sb("n_mean2", [P, NT])
        diff = sb("n_diff", [P, NT])
        var = sb("n_var", [P, NT])
        std = sb("n_std", [P, NT])
        ident = sb("n_ident", [P, P])
        T = [ctx.enter_context(nc.psum_tensor(f"n_T{i}", [P, KD, 2, P], F32)) for i in range(2)]
        x_in = [sem(f"n_x_in{i}") for i in range(4)]
        id_set = sem("n_id_set")
        step = sem("n_step")
        var_ready = sem("n_var_ready")
        std_ready = sem("n_std_ready")
        xn_ready = sem("n_xn_ready")
        turned = sem("n_turned")
        stored = sem("n_stored")
        block = ctx.enter_context(nc.Block())

        @block.sync
        def _(sp):
            xt = x.rearrange("(t p) d -> p t d", p=P)
            for i in range(4):
                sp.dma_start(X[:, 8 * i:8 * i + 8, :], xt[:, 8 * i:8 * i + 8, :]).then_inc(x_in[i], 16)

        @block.gpsimd
        def _(pool):
            pool.memset(ident[:, :], 0.0).then_inc(id_set, 1)
            pool.wait_ge(id_set, 1)
            pool.affine_select(out=ident[:, :], in_=ident[:, :], compare_op=ALU.not_equal, fill=1.0, base=0,
                               pattern=[[-1, P]], channel_multiplier=1).then_inc(id_set, 1)

        @block.vector
        def _(dve):
            for i in range(4):
                dve.wait_ge(x_in[i], 16)
                with dve.Fori(8 * i, 8 * i + 8) as t:
                    dve.bn_stats(stats[:, bass.ds(t, 1), :].rearrange("p a s -> p (a s)"),
                                 X[:, bass.ds(t, 1), :].rearrange("p a d -> p (a d)")).then_inc(step, 1)
            n = [NT]

            def link(ins):
                n[0] += 1
                ins.then_inc(step, 1)
                dve.wait_ge(step, n[0])

            dve.wait_ge(step, NT)
            moments(dve, link, stats, mean2, diff, var)
            dve.sem_inc(var_ready, 1)
            dve.wait_ge(std_ready, 1)
            link(dve.reciprocal(scale[:, :], std[:, :]))
            link(dve.scalar_tensor_tensor(out=shift[:, :], in0=mean2[:, :], scalar=-0.5, in1=scale[:, :],
                                          op0=ALU.mult, op1=ALU.mult))
            with dve.Fori(0, NT // 4) as g:
                for k in range(4):
                    if k % 2 == 0:
                        dve.wait_ge(turned, g * 2 + k // 2 + 1)
                    dve.tensor_scalar(XN[:, k, :], X[:, bass.ds(g * 4 + k, 1), :].rearrange("p a d -> p (a d)"),
                                      scale[:, bass.ds(g * 4 + k, 1)], shift[:, bass.ds(g * 4 + k, 1)],
                                      ALU.mult, ALU.add).then_inc(xn_ready, 1)

        @block.scalar
        def _(act):
            act.wait_ge(var_ready, 1)
            act.activation(std[:, :], var[:, :], ACT.Sqrt).then_inc(std_ready, 1)
            act.sem_inc(stored, 2)
            with act.Fori(0, NT // 4) as g:
                for k in range(2):
                    act.wait_ge(turned, g * 2 + k + 3)
                    tile = g % (ST_N // 4) * 4 + 2 * k
                    act.activation(hold[:, bass.ds(g // (ST_N // 4), 1), :, bass.ds(tile * P, 2 * P)],
                                   T[k][:, :, :, :].rearrange("p a b q -> p a (b q)"),
                                   ACT.Copy).then_inc(stored, 1)

        @block.tensor
        def _(pe):
            pe.wait_ge(id_set, 2)
            pe.sem_inc(turned, 2)
            with pe.Fori(0, NT // 4) as g:
                for k in range(2):
                    pe.wait_ge(xn_ready, g * 4 + 2 * k + 2)
                    pe.wait_ge(stored, g * 2 + k + 1)
                    for u in range(2):
                        for kt in range(KD):
                            last = pe.transpose(T[k][:, kt, u, :], XN[:, 2 * k + u, kt * P:(kt + 1) * P], ident[:, :])
                    last.then_inc(turned, 1)


def moments(dve, link, stats, mean2, diff, var):
    link(dve.tensor_tensor(mean2[:, :], stats[:, :, 1], stats[:, :, 4], ALU.add))
    link(dve.tensor_tensor(diff[:, :], stats[:, :, 1], stats[:, :, 4], ALU.subtract))
    link(dve.tensor_tensor(var[:, :], stats[:, :, 2], stats[:, :, 5], ALU.add))
    link(dve.scalar_tensor_tensor(out=diff[:, :], in0=diff[:, :], scalar=0.25, in1=diff[:, :],
                                  op0=ALU.mult, op1=ALU.mult))
    link(dve.scalar_tensor_tensor(out=var[:, :], in0=var[:, :], scalar=1.0 / D, in1=diff[:, :],
                                  op0=ALU.mult, op1=ALU.add))
    link(dve.tensor_scalar(var[:, :], var[:, :], EPS, None, ALU.add))


FILL = {k: [] for k in range(2 * NU)}
for _k, _item in enumerate([("q", 0), ("q", 1), ("k", 0), ("k", 1), ("v", 0), ("v", 1)]):
    FILL[_k].append(_item)
for _n in range(2 * len(MAXU)):
    FILL[7 + _n // 2].append(("max", _n))
FILL[20].append(("turn", 0))


def attention_one(nc, hold, w_pair, w_out):
    rows = hold.rearrange("p b k s -> p b (k s)").rearrange("p b (t d) -> p (b t) d", d=D)
    with ExitStack() as ctx:
        sb = lambda name, shape, dt=F32: ctx.enter_context(nc.sbuf_tensor(name, shape, dt))
        ps = lambda name, shape, dt=F32: ctx.enter_context(nc.psum_tensor(name, shape, dt))
        sem = lambda name: ctx.enter_context(nc.semaphore(name))
        xT = sb("a_xT", [P, KD, S])
        W = [sb(f"a_W{i}", [P, KD, 3, P]) for i in range(2)]
        Wo = sb("a_Wo", [P, PAIRS, D])
        Q = [[sb(f"a_Q{i}{h}", [DH1 + 1, S]) for h in range(2)] for i in range(2)]
        K = [[sb(f"a_K{i}{h}", [DH1 + 1, S]) for h in range(2)] for i in range(2)]
        Qr = [[sb(f"a_Qr{i}{h}", [DH1, S], F32R) for h in range(2)] for i in range(2)]
        Kr = [[sb(f"a_Kr{i}{h}", [DH1, S], F32R) for h in range(2)] for i in range(2)]
        V = [[sb(f"a_V{i}{h}", [P, ST_N, 2 * DH1]) for h in range(2)] for i in range(2)]
        cat = sb("a_cat", [P, PAIRS, S])
        probs = [sb(f"a_P{i}", [P, BANK]) for i in range(4)]
        inv = [sb(f"a_inv{i}", [DH1, BANK]) for i in range(2)]
        peak = sb("a_peak", [P, 2, ST_N, 2])
        minus = sb("a_minus", [P, 2 * ST_N])
        minusT = sb("a_minusT", [2 * ST_N, P])
        ident = sb("a_ident", [P, P])
        identb = sb("a_identb", [P, P], BF16)
        maskb = sb("a_maskb", [P, P], BF16)
        SC = [ps(f"a_SC{i}", [P, BANK]) for i in range(2)]
        MX = [ps(f"a_MX{i}", [P, BANK]) for i in range(2)]
        O = [ps(f"a_O{i}", [P, BANK]) for i in range(2)]
        PR = [ps(f"a_PR{i}", [P, BANK]) for i in range(2)]

        consts = sem("a_consts")
        dve_consts = sem("a_dve_consts")
        x_in = sem("a_x_in")
        wo_in = sem("a_wo_in")
        w_in = [sem(f"a_w_in{i}") for i in range(2)]
        q_ready, q_copied = sem("a_q_ready"), sem("a_q_copied")
        k_ready, k_copied = sem("a_k_ready"), sem("a_k_copied")
        v_ready, v_copied = sem("a_v_ready"), sem("a_v_copied")
        max_ready, max_used = sem("a_max_ready"), sem("a_max_used")
        minus_ready = sem("a_minus_ready")
        turn_ready, turn_copied = sem("a_turn_ready"), sem("a_turn_copied")
        minus_in = sem("a_minus_in")
        scores_ready, exp_done = sem("a_scores_ready"), sem("a_exp_done")
        masked = sem("a_masked")
        mask_due = sem("a_mask_due")
        pv_done = sem("a_pv_done")
        inv_ready = sem("a_inv_ready")
        out_done = sem("a_out_done")
        proj_ready, proj_copied = sem("a_proj_ready"), sem("a_proj_copied")
        block = ctx.enter_context(nc.Block())

        def batches(eng, head, step, tail):
            with eng.Fori(0, B) as b:
                n = b * PAIRS
                head(b)
                step(n, None, 0, None)
                with eng.Fori(0, PAIRS // 2 - 1) as u:
                    m = n + u * 2
                    step(m + 1, m, 1, 0)
                    step(m + 2, m + 1, 0, 1)
                step(n + PAIRS - 1, n + PAIRS - 2, 1, 0)
                step(None, n + PAIRS - 1, None, 1)
                tail(b)

        @block.gpsimd
        def _(pool):
            for m, fill in ((ident, 0.0), (identb, 0.0), (maskb, 0.0)):
                pool.memset(m[:, :], fill).then_inc(consts, 1)
            pool.wait_ge(consts, 3)
            for m in (ident, identb):
                pool.affine_select(out=m[:, :], in_=m[:, :], compare_op=ALU.not_equal, fill=1.0, base=0,
                                   pattern=[[-1, P]], channel_multiplier=1).then_inc(consts, 1)
            pool.affine_select(out=maskb[:, :], in_=maskb[:, :], compare_op=ALU.is_ge, fill=NEG, base=0,
                               pattern=[[-1, P]], channel_multiplier=1).then_inc(consts, 1)

            def step(n1, n2, p1, p2):
                if n2 is None:
                    return
                for k in range(2 * NU):
                    c, j = UNITS[k % NU]
                    if is_diag(c, j):
                        a = first_col(c, j)
                        pool.wait_ge(exp_done, n2 * (2 * NU) + k + 3)
                        pool.sem_inc(mask_due, 1)
                        pool.affine_select(out=probs[k % 4][:, a:a + P], in_=probs[k % 4][:, a:a + P],
                                           compare_op=ALU.is_ge, fill=0.0, base=0, pattern=[[1, P]],
                                           channel_multiplier=-1).then_inc(masked, 1)

            batches(pool, lambda b: None, step, lambda b: None)

        @block.sync
        def _(sp):
            sp.dma_start(Wo[:, :, :], w_out).then_inc(wo_in, 16)
            for i in range(2):
                sp.dma_start(W[i][:, :, :, :], w_pair[i]).then_inc(w_in[i], 16)

            def head(b):
                sp.wait_ge(v_ready, b * (2 * PAIRS) + 1)
                sp.dma_start(xT[:, :, :], hold[:, bass.ds(b, 1), :, :].rearrange("p b k s -> p (b k) s")).then_inc(x_in, 16)

            def step(n1, n2, p1, p2):
                if n1 is not None:
                    sp.wait_ge(turn_copied, n1 + 2)
                    for h in range(2):
                        sp.dma_start(Q[p1][h][DH1:DH1 + 1, :],
                                     minusT[ST_N * h:ST_N * (h + 1), :]).then_inc(minus_in, 16)
                    sp.dma_start(W[p1][:, :, :, :], w_pair[bass.ds((n1 + 2) % PAIRS, 1)].rearrange(
                        "a p k w c -> p (a k) w c")).then_inc(w_in[p1], 16)

            batches(sp, head, step, lambda b: None)
            for i in range(2):
                sp.wait_ge(w_in[i], 16 * (B * PAIRS // 2 + 1))

        @block.scalar
        def _(act):
            act.sem_inc(exp_done, 2)
            act.sem_inc(v_copied, 1)

            def step(n1, n2, p1, p2):
                for k in range(2 * NU):
                    if n2 is not None:
                        a = first_col(*UNITS[k % NU])
                        act.wait_ge(scores_ready, n2 * (2 * NU) + k + 1)
                        act.wait_ge(pv_done, n2 * (2 * NU) + k + 1)
                        act.activation(probs[k % 4][:, a:], SC[k % 2][:, a:], ACT.Exp,
                                       scale=DH1 ** -0.5).then_inc(exp_done, 1)
                    if n1 is None:
                        continue
                    for what, c in FILL[k]:
                        if what == "q":
                            act.wait_ge(q_ready, n1 * 2 + c + 1)
                            for h in range(2):
                                for dst in (Q, Qr):
                                    act.activation(dst[p1][h][0:DH1, c * BANK:(c + 1) * BANK],
                                                   PR[c][DH1 * h:DH1 * (h + 1), :], ACT.Copy).then_inc(q_copied, 1)
                        elif what == "v":
                            act.wait_ge(v_ready, n1 * 2 + c + 2)
                            for h in range(2):
                                act.activation(V[p1][h][:, 4 * c:4 * c + 4, 0:DH1],
                                               PR[c][:, :].rearrange("p (t w) -> p t w", t=4)[:, :, DH1 * h:DH1 * (h + 1)],
                                               ACT.Copy).then_inc(v_copied, 1)

            def tail(b):
                for i in range(ST_N):
                    act.wait_ge(proj_ready, b * ST_N + i + 2)
                    act.activation(rows[:, bass.ds(b * ST_N + i, 1), :].rearrange("p a d -> p (a d)"),
                                   PR[i % 2][:, 0:D], ACT.Copy).then_inc(proj_copied, 1)

            act.sem_inc(proj_copied, 2)
            batches(act, lambda b: None, step, tail)

        @block.vector
        def _(dve):
            dve.memset(peak[:, :, :, :], 3 * NEG).then_inc(dve_consts, 1)
            for i in range(2):
                for h in range(2):
                    dve.memset(K[i][h][DH1:DH1 + 1, :], 1.0).then_inc(dve_consts, 1)
                    dve.memset(V[i][h][:, :, DH1:], 1.0).then_inc(dve_consts, 1)
            dve.wait_ge(dve_consts, 9)
            dve.sem_inc(max_used, 2)
            dve.sem_inc(minus_in, 1)
            dve.sem_inc(turn_copied, 1)
            dve.sem_inc(out_done, 2)

            def output(n2, pair, q):
                h, c = q // 2, q % 2
                dve.wait_ge(pv_done, n2 * (2 * NU) + h * NU + LAST[c] + 5)
                dve.reciprocal(inv[q % 2][:, :], O[q % 2][DH1:P, :]).then_inc(inv_ready, 1)
                dve.wait_ge(inv_ready, n2 * 4 + q + 1)
                dve.tensor_tensor(cat[DH1 * h:DH1 * (h + 1), pair, c * BANK:(c + 1) * BANK], O[q % 2][0:DH1, :],
                                  inv[q % 2][:, :], ALU.mult).then_inc(out_done, 1)

            def step(n1, n2, p1, p2):
                for k in range(2 * NU):
                    if n1 is not None:
                        for what, c in FILL[k]:
                            if what == "k":
                                dve.wait_ge(k_ready, n1 * 2 + c + 1)
                                for h in range(2):
                                    for dst in (K, Kr):
                                        dve.tensor_copy(dst[p1][h][0:DH1, c * BANK:(c + 1) * BANK],
                                                        PR[c][DH1 * h:DH1 * (h + 1), :]).then_inc(k_copied, 1)
                            elif what == "max":
                                h, (i, ch) = c // len(MAXU), MAXU[c % len(MAXU)]
                                n = min(BANK, (i + 1) * P - ch * BANK)
                                dve.wait_ge(max_ready, n1 * (2 * NU) + c + 1)
                                dve.tensor_reduce(peak[:, h, i, ch:ch + 1], MX[c % 2][:, 0:n], AX.X,
                                                  ALU.max).then_inc(max_used, 1)
                                if c == 2 * len(MAXU) - 1:
                                    dve.wait_ge(max_used, n1 * (2 * NU) + 2 * NU + 2)
                                    dve.tensor_reduce(minus[:, :].rearrange("p (h i) -> p h i", h=2), peak[:, :, :, :],
                                                      AX.X, ALU.max, negate=True).then_inc(minus_ready, 1)
                            elif what == "turn":
                                dve.wait_ge(turn_ready, n1 + 1)
                                dve.wait_ge(minus_in, n1 * 32 + 1)
                                dve.tensor_copy(minusT[:, :], PR[0][0:2 * ST_N, 0:P]).then_inc(turn_copied, 1)
                    if n2 is not None and k in (5, 13, 17):
                        q = (5, 13, 17).index(k)
                        output(n2, bass.ds(n2 % PAIRS, 1), q)
                if n2 is not None:
                    output(n2, bass.ds(n2 % PAIRS, 1), 3)

            batches(dve, lambda b: dve.wait_ge(proj_ready, b * ST_N + 1), step, lambda b: None)

        @block.tensor
        def _(pe):
            pe.wait_ge(consts, 6)
            pe.wait_ge(dve_consts, 9)
            pe.wait_ge(wo_in, 16)
            pe.sem_inc(pv_done, 4)
            pe.sem_inc(v_ready, 1)
            pe.sem_inc(proj_ready, 1)

            def scores(n2, p2, k):
                h, (c, j) = k // NU, UNITS[k % NU]
                a = first_col(c, j)
                if k == 0:
                    pe.wait_ge(minus_in, n2 * 32 + 33)
                pe.wait_ge(exp_done, n2 * (2 * NU) + k + 1)
                pe.matmul(SC[k % 2][:, a:], K[p2][h][:, j * P:(j + 1) * P], Q[p2][h][:, c * BANK + a:(c + 1) * BANK],
                          start=True, stop=True).then_inc(scores_ready, 1)

            def output(n2, p2, k):
                h, (c, j) = k // NU, UNITS[k % NU]
                q, a = 2 * h + c, first_col(c, j)
                if j == 0:
                    pe.wait_ge(out_done, n2 * 4 + q + 1)
                pe.wait_ge(exp_done, n2 * (2 * NU) + k + 3)
                if is_diag(c, j):
                    pe.wait_ge(masked, n2 * (2 * ST_N) + h * ST_N + j + 1)
                pe.matmul(O[q % 2][:, a:], V[p2][h][:, j, :], probs[k % 4][:, a:], start=(j == 0),
                          stop=(k % NU in LAST)).then_inc(pv_done, 1)

            def fill(n1, p1, what, c):
                if what in "qk":
                    if (what, c) == ("q", 0):
                        pe.wait_ge(w_in[p1], (n1 - p1) * 8 + 16)
                        pe.wait_ge(turn_copied, n1 + 1)
                    elif (what, c) == ("q", 1):
                        pe.wait_ge(v_copied, n1 * 4 + 1)
                    else:
                        pe.wait_ge(q_copied, n1 * 8 + 4 * c + 4)
                    for kt in range(KD):
                        last = pe.matmul(PR[c][:, :], W[p1][:, kt, "qk".index(what), :], xT[:, kt, c * BANK:(c + 1) * BANK],
                                         start=(kt == 0), stop=(kt == KD - 1))
                    last.then_inc(q_ready if what == "q" else k_ready, 1)
                elif what == "v":
                    pe.wait_ge(k_copied, n1 * 8 + 4 * c + 4)
                    for t in range(4):
                        for kt in range(KD):
                            last = pe.matmul(PR[c][:, t * P:(t + 1) * P], xT[:, kt, (4 * c + t) * P:(4 * c + t + 1) * P],
                                             W[p1][:, kt, 2, :], start=(kt == 0), stop=(kt == KD - 1))
                    last.then_inc(v_ready, 1)
                elif what == "max":
                    h, (i, ch) = c // len(MAXU), MAXU[c % len(MAXU)]
                    n = min(BANK, (i + 1) * P - ch * BANK)
                    diag = ch == i * P // BANK
                    if c == 0:
                        pe.wait_ge(q_copied, n1 * 8 + 8)
                        pe.wait_ge(k_copied, n1 * 8 + 8)
                    pe.wait_ge(max_used, n1 * (2 * NU) + c + 1)
                    last = pe.matmul(MX[c % 2][:, 0:n], Qr[p1][h][:, i * P:(i + 1) * P], Kr[p1][h][:, ch * BANK:ch * BANK + n],
                                     start=True, stop=not diag)
                    if diag:
                        last = pe.matmul(MX[c % 2][:, n - P:n], identb[:, :], maskb[:, :], start=False, stop=True)
                    last.then_inc(max_ready, 1)
                elif what == "turn":
                    pe.wait_ge(minus_ready, n1 + 1)
                    pe.wait_ge(v_copied, n1 * 4 + 3)
                    pe.transpose(PR[0][0:2 * ST_N, 0:P], minus[:, :], ident[:, :]).then_inc(turn_ready, 1)

            def step(n1, n2, p1, p2):
                for k in range(2 * NU):
                    if n2 is not None:
                        scores(n2, p2, k)
                    if n1 is not None:
                        for what, c in FILL[k]:
                            fill(n1, p1, what, c)
                    if n2 is not None and k >= 2:
                        output(n2, p2, k - 2)
                if n2 is not None:
                    output(n2, p2, 2 * NU - 2)
                    output(n2, p2, 2 * NU - 1)

            def tail(b):
                pe.wait_ge(out_done, b * (4 * PAIRS) + 4 * PAIRS + 2)
                pe.wait_ge(turn_copied, b * PAIRS + PAIRS + 1)
                pe.wait_ge(v_copied, b * (4 * PAIRS) + 4 * PAIRS + 1)
                for i in range(ST_N):
                    pe.wait_ge(proj_copied, b * ST_N + i + 1)
                    for p in range(PAIRS):
                        last = pe.matmul(PR[i % 2][:, 0:D], cat[:, p, i * P:(i + 1) * P], Wo[:, p, :],
                                         start=(p == 0), stop=(p == PAIRS - 1))
                    last.then_inc(proj_ready, 1)

            def head(b):
                pe.wait_ge(x_in, b * 16 + 16)
                pe.wait_ge(proj_copied, b * ST_N + 2)

            batches(pe, head, step, tail)


H2, KV2, DH2 = 16, 4, 16
GROUP = H2 // KV2
QK2 = (H2 + KV2) * DH2
QKV2 = QK2 + KV2 * DH2
Q_PARTS = (0, 0, 0, 1, 1, 2)
K_PARTS = (0, 1, 2, 0, 1, 0)
PARTS = len(Q_PARTS)
STACK = PARTS * DH2
HEADS2 = H2 + KV2


def counted(eng, sem, base):
    n = [0]

    def link(ins):
        n[0] += 1
        ins.then_inc(sem, 1)
        eng.wait_ge(sem, base + n[0])

    return link


def project_two(nc, x, hold, w_qkv, ln1, cos2, sin2, norm_z, shift_z, V2, stack_dram):
    rows = hold.rearrange("p b k s -> p (b k s)").rearrange("p (t d) -> p t d", d=D)
    with ExitStack() as ctx:
        sb = lambda name, shape, dt=F32: ctx.enter_context(nc.sbuf_tensor(name, shape, dt))
        ps = lambda name, shape, dt=F32: ctx.enter_context(nc.psum_tensor(name, shape, dt))
        sem = lambda name: ctx.enter_context(nc.semaphore(name))
        X = sb("p_x", [P, NT, D])
        Y = sb("p_y", [P, 4, D])
        Wq = sb("p_w", [P, KD, QKV2])
        ln = sb("p_ln", [P, KD])
        cos = sb("p_cos", [P, ST_N, DH2])
        sin = sb("p_sin", [P, ST_N, DH2])
        stats = sb("p_stats", [P, NT, 6])
        small = {k: sb(f"p_{k}", [P, NT]) for k in ("mean2", "diff", "var", "std", "scale", "shift", "ratio", "hscale", "hshift")}
        ident = sb("p_ident", [P, P])
        HN = [sb(f"p_hn{i}", [P, D]) for i in range(2)]
        hT = [sb(f"p_hT{i}", [P, KD, P]) for i in range(2)]
        rot = [sb(f"p_rot{i}", [P, QK2]) for i in range(2)]
        crs = [sb(f"p_crs{i}", [P, QK2]) for i in range(2)]
        stk = [sb(f"p_stk{i}", [P, HEADS2, PARTS, DH2], BF16) for i in range(2)]
        T = [ps(f"p_T{i}", [P, BANK]) for i in range(2)]
        QKV = [ps(f"p_QKV{i}", [P, BANK]) for i in range(2)]
        names = ("x_in", "w_in", "id_set", "step", "ones_set", "var_ready", "std_ready", "y_ready", "y_used", "hn_ready",
                 "turned", "hT_ready", "qkv_ready", "v_copied", "rotated", "first_set", "rest", "second_set",
                 "third_set")
        s = {k: sem(f"p_{k}") for k in names}
        x_in = [sem(f"p_x_in{i}") for i in range(4)]
        stored = [sem(f"p_stored{i}") for i in range(2)]
        block = ctx.enter_context(nc.Block())

        @block.sync
        def _(sp):
            xt = x.rearrange("(t p) d -> p t d", p=P)
            for i in range(4):
                sp.dma_start(X[:, 8 * i:8 * i + 8, :], xt[:, 8 * i:8 * i + 8, :]).then_inc(x_in[i], 16)
            for dst, src in ((Wq, w_qkv), (cos, cos2), (sin, sin2)):
                sp.dma_start(dst[:, :, :], src).then_inc(s["w_in"], 16)
            sp.dma_start(ln[:, :], ln1).then_inc(s["w_in"], 16)
            with sp.Fori(0, NT // 2) as g:
                for i in range(2):
                    sp.wait_ge(s["third_set"], g * 4 + 2 * i + 5)
                    sp.dma_start(stack_dram[bass.ds(g * 2 + i, 1), :, :].rearrange("t p w -> (t p) w"),
                                 stk[i][:, :, :, :].rearrange("p h a d -> p (h a d)")).then_inc(stored[i], 16)
            for i in range(2):
                sp.wait_ge(stored[i], 16 * (NT // 2) + 1)

        @block.gpsimd
        def _(pool):
            pool.memset(ident[:, :], 0.0).then_inc(s["id_set"], 1)
            pool.wait_ge(s["id_set"], 1)
            pool.affine_select(out=ident[:, :], in_=ident[:, :], compare_op=ALU.not_equal, fill=1.0, base=0,
                               pattern=[[-1, P]], channel_multiplier=1).then_inc(s["id_set"], 1)
            pool.memset(V2, 1.0).then_inc(s["ones_set"], 1)

        def tile_of(t, n, k):
            return t[:, bass.ds(n, 1), :].rearrange("p a d -> p (a d)")

        @block.vector
        def _(dve):
            sm = {k: v[:, :] for k, v in small.items()}
            with dve.Fori(0, NT) as t:
                dve.bn_stats(tile_of(stats, t, 0), tile_of(rows, t, 0)).then_inc(s["step"], 1)
            dve.wait_ge(s["step"], NT)
            link = counted(dve, s["step"], NT)
            moments(dve, link, stats, small["mean2"], small["diff"], small["var"])
            dve.sem_inc(s["var_ready"], 1)
            dve.wait_ge(s["std_ready"], 1)
            link(dve.reciprocal(sm["scale"], sm["std"]))
            link(dve.scalar_tensor_tensor(out=sm["shift"], in0=sm["mean2"], scalar=-0.5, in1=sm["scale"],
                                          op0=ALU.mult, op1=ALU.mult))
            dve.sem_inc(s["var_ready"], 1)
            dve.sem_inc(s["y_used"], 4)
            base = NT + 8
            for i in range(4):
                dve.wait_ge(x_in[i], 16)
                with dve.Fori(2 * i, 2 * i + 2) as f:
                    t = f * 4
                    for k in range(4):
                        dve.wait_ge(s["y_ready"], t + k + 1)
                        dve.tensor_tensor(tile_of(rows, t + k, 0), Y[:, k, :], tile_of(X, t + k, 0),
                                          ALU.add).then_inc(s["y_used"], 1)
                    for k in range(4):
                        dve.wait_ge(s["y_used"], t + k + 5)
                        dve.bn_stats(tile_of(stats, t + k, 0), tile_of(rows, t + k, 0)).then_inc(s["step"], 1)
            dve.wait_ge(s["step"], base + NT)
            link = counted(dve, s["step"], base + NT)
            moments(dve, link, stats, small["mean2"], small["diff"], small["var"])
            dve.sem_inc(s["var_ready"], 1)
            dve.wait_ge(s["std_ready"], 2)
            link(dve.reciprocal(norm_z, sm["std"]))
            link(dve.scalar_tensor_tensor(out=shift_z, in0=sm["mean2"], scalar=-0.5, in1=norm_z,
                                          op0=ALU.mult, op1=ALU.mult))
            link(dve.tensor_scalar(sm["diff"], sm["var"], -EPS, None, ALU.add))
            link(dve.tensor_tensor(sm["diff"], sm["diff"], norm_z, ALU.mult))
            link(dve.tensor_tensor(sm["diff"], sm["diff"], norm_z, ALU.mult))
            link(dve.tensor_scalar(sm["var"], sm["diff"], EPS, None, ALU.add))
            dve.sem_inc(s["var_ready"], 1)
            dve.wait_ge(s["std_ready"], 3)
            link(dve.reciprocal(sm["ratio"], sm["std"]))
            link(dve.tensor_tensor(sm["hscale"], norm_z, sm["ratio"], ALU.mult))
            link(dve.tensor_tensor(sm["hshift"], shift_z, sm["ratio"], ALU.mult))
            dve.wait_ge(s["w_in"], 64)
            dve.wait_ge(s["ones_set"], 1)
            dve.sem_inc(stored[0], 1)
            dve.sem_inc(stored[1], 1)
            dve.sem_inc(s["rotated"], 2)

            def narrow(t, i):
                dve.tensor_scalar(HN[i][:, :], tile_of(rows, t, 0),
                                  small["hscale"][:, bass.ds(t, 1)], small["hshift"][:, bass.ds(t, 1)],
                                  ALU.mult, ALU.add).then_inc(s["hn_ready"], 1)

            def body(g, more):
                if more:
                    for i in range(2):
                        dve.wait_ge(s["turned"], g * 2 + i + 3)
                        narrow(g * 2 + (2 + i), i)
                for i in range(2):
                    t = g * 2 + i
                    dve.wait_ge(s["v_copied"], t + 3)
                    C = cos[:, bass.ds(t % ST_N, 1), :].to_broadcast([P, HEADS2, DH2])
                    qk = QKV[i][:, 0:QK2].rearrange("p (h d) -> p h d", d=DH2)
                    X4 = crs[i][:, :].rearrange("p (h d) -> p h d", d=DH2)
                    half = DH2 // 2
                    dve.wait_ge(s["third_set"], t * 2 + 1)
                    dve.tensor_tensor(rot[i][:, :].rearrange("p (h d) -> p h d", d=DH2), qk, C, ALU.mult).then_inc(s["rest"], 1)
                    for a in range(2):
                        dve.tensor_tensor(X4[:, :, a * half:(a + 1) * half], qk[:, :, (1 - a) * half:(2 - a) * half],
                                          sin[:, bass.ds(t % ST_N, 1), a * half:(a + 1) * half].to_broadcast([P, HEADS2, half]),
                                          ALU.mult).then_inc(s["rest"], 1)
                for i in range(2):
                    t = g * 2 + i
                    dve.wait_ge(s["rest"], g * 10 + 3 * i + 3)
                    dve.tensor_tensor(rot[i][:, :], rot[i][:, :], crs[i][:, :], ALU.add).then_inc(s["rotated"], 1)
                for i in range(2):
                    t = g * 2 + i
                    dve.wait_ge(s["first_set"], t * 3 + 3)
                    r = rot[i][:, :].rearrange("p (h d) -> p h d", d=DH2)
                    dve.tensor_tensor(r[:, 0:H2, :], r[:, 0:H2, :], stk[i][:, 0:H2, Q_PARTS.index(0), :], ALU.subtract).then_inc(s["rest"], 1)
                    dve.tensor_tensor(r[:, H2:, :], r[:, H2:, :], stk[i][:, H2:, K_PARTS.index(0), :], ALU.subtract).then_inc(s["rest"], 1)
                for i in range(2):
                    t = g * 2 + i
                    dve.wait_ge(s["second_set"], t * 2 + 2)
                    r = rot[i][:, :].rearrange("p (h d) -> p h d", d=DH2)
                    for lo, hi, parts in ((0, H2, Q_PARTS), (H2, HEADS2, K_PARTS)):
                        dve.tensor_tensor(stk[i][:, lo:hi, parts.index(2), :], r[:, lo:hi, :],
                                          stk[i][:, lo:hi, parts.index(1), :], ALU.subtract).then_inc(s["third_set"], 1)

            for i in range(2):
                narrow(i, i)
            with dve.Fori(0, NT // 2 - 1) as g:
                body(g, True)
            body(NT // 2 - 1, False)

        @block.scalar
        def _(act):
            act.wait_ge(s["var_ready"], 1)
            act.activation(small["std"][:, :], small["var"][:, :], ACT.Sqrt).then_inc(s["std_ready"], 1)
            act.wait_ge(s["var_ready"], 2)
            with act.Fori(0, NT // 4) as f:
                t = f * 4
                for k in range(4):
                    act.wait_ge(s["y_used"], t + k + 1)
                    act.activation(Y[:, k, :], tile_of(rows, t + k, 0), ACT.Identity,
                                   scale=small["scale"][:, bass.ds(t + k, 1)],
                                   bias=small["shift"][:, bass.ds(t + k, 1)]).then_inc(s["y_ready"], 1)
            for n in range(2):
                act.wait_ge(s["var_ready"], 3 + n)
                act.activation(small["std"][:, :], small["var"][:, :], ACT.Sqrt).then_inc(s["std_ready"], 1)
            act.wait_ge(s["w_in"], 64)
            act.wait_ge(s["ones_set"], 1)
            act.sem_inc(s["v_copied"], 2)
            with act.Fori(0, NT // 2) as g:
                for i in range(2):
                    t = g * 2 + i
                    act.wait_ge(s["turned"], t + 3)
                    for kt in range(KD):
                        act.activation(hT[i][:, kt, :], T[i][:, kt * P:(kt + 1) * P], ACT.Copy,
                                       scale=ln[:, kt:kt + 1]).then_inc(s["hT_ready"], 1)
                for i in range(2):
                    t = g * 2 + i
                    act.wait_ge(s["qkv_ready"], t + 1)
                    act.activation(V2[:, bass.ds(t // ST_N, 1), :, bass.ds(t % ST_N, 1), 0:DH2].rearrange("p a g b d -> p (a g) (b d)"),
                                   QKV[i][:, QK2:].rearrange("p (g d) -> p g d", d=DH2)[:, 0:KV2, :], ACT.Copy).then_inc(s["v_copied"], 1)
                for i in range(2):
                    t = g * 2 + i
                    act.wait_ge(s["rotated"], t + 3)
                    act.wait_ge(stored[i], g * 16 + 1)
                    r = rot[i][:, :].rearrange("p (h a d) -> p h a d", a=1, d=DH2)
                    act.activation(stk[i][:, 0:H2, 0:3, :], r[:, 0:H2].to_broadcast([P, H2, 3, DH2]), ACT.Copy).then_inc(s["first_set"], 1)
                    act.activation(stk[i][:, H2:, 0:4:3, :], r[:, H2:].to_broadcast([P, KV2, 2, DH2]), ACT.Copy).then_inc(s["first_set"], 1)
                    act.activation(stk[i][:, H2:, 5:6, :], r[:, H2:], ACT.Copy).then_inc(s["first_set"], 1)
                for i in range(2):
                    t = g * 2 + i
                    act.wait_ge(s["rest"], g * 10 + 6 + 2 * i + 2)
                    r = rot[i][:, :].rearrange("p (h a d) -> p h a d", a=1, d=DH2)
                    act.activation(stk[i][:, 0:H2, 3:5, :], r[:, 0:H2].to_broadcast([P, H2, 2, DH2]), ACT.Copy).then_inc(s["second_set"], 1)
                    act.activation(stk[i][:, H2:, 1:5:3, :], r[:, H2:].to_broadcast([P, KV2, 2, DH2]), ACT.Copy).then_inc(s["second_set"], 1)

        @block.tensor
        def _(pe):
            pe.wait_ge(s["id_set"], 2)
            pe.wait_ge(s["w_in"], 64)
            pe.sem_inc(s["turned"], 2)
            pe.sem_inc(s["third_set"], 3)
            pe.sem_inc(s["hT_ready"], 4)
            with pe.Fori(0, NT // 2) as g:
                for i in range(2):
                    t = g * 2 + i
                    pe.wait_ge(s["hn_ready"], t + 1)
                    pe.wait_ge(s["hT_ready"], t * 2 + 2)
                    for kt in range(KD):
                        last = pe.transpose(T[i][:, kt * P:(kt + 1) * P], HN[i][:, kt * P:(kt + 1) * P], ident[:, :])
                    last.then_inc(s["turned"], 1)
                for i in range(2):
                    t = g * 2 + i
                    pe.wait_ge(s["hT_ready"], t * 2 + 6)
                    pe.wait_ge(s["rotated"], t + 1)
                    pe.wait_ge(s["v_copied"], t + 1)
                    for kt in range(KD):
                        last = pe.matmul(QKV[i][:, 0:QKV2], hT[i][:, kt, :], Wq[:, kt, :], start=(kt == 0), stop=(kt == KD - 1))
                    last.then_inc(s["qkv_ready"], 1)


STEPS2 = B * KV2
UNITS2 = [(c, j, h) for c, j in UNITS for h in range(GROUP)]
NU2 = len(UNITS2)
MAX2 = [(h, i, c) for h in range(GROUP) for i, c in MAXU]
LAG2 = 5
RING2 = 8
FILL2 = {k: [] for k in range(NU2)}
for _n in range(GROUP + 1):
    FILL2[_n].append(("stack", _n))
for _n in range(NU2):
    FILL2[5 + _n * (NU2 - 6) // NU2].append(("max", _n))


def attention_two(nc, stack_dram, V2, A2):
    with ExitStack() as ctx:
        sb = lambda name, shape, dt=F32: ctx.enter_context(nc.sbuf_tensor(name, shape, dt))
        ps = lambda name, shape, dt=F32: ctx.enter_context(nc.psum_tensor(name, shape, dt))
        sem = lambda name: ctx.enter_context(nc.semaphore(name))
        stk = [sb(f"b_stk{i}", [P, ST_N, GROUP + 1, STACK], BF16) for i in range(2)]
        V = [sb(f"b_V{i}", [P, ST_N, 2 * DH2]) for i in range(2)]
        Q = [sb(f"b_Q{i}", [STACK + 2, GROUP, S], BF16) for i in range(2)]
        K = [sb(f"b_K{i}", [STACK + 2, S], BF16) for i in range(2)]
        probs = [sb(f"b_P{i}", [P, BANK]) for i in range(RING2)]
        OT = [sb(f"b_OT{i}", [P, BANK]) for i in range(2)]
        inv = sb("b_inv", [P, 2, GROUP, GROUP])
        peak = sb("b_peak", [P, GROUP, ST_N, 2])
        minus = sb("b_minus", [P, GROUP * ST_N])
        hi = sb("b_hi", [GROUP * ST_N, P], BF16)
        lo = sb("b_lo", [GROUP * ST_N, P], BF16)
        ident = sb("b_ident", [P, P])
        identb = sb("b_identb", [P, P], BF16)
        maskb = sb("b_maskb", [P, P], BF16)
        SC = [ps(f"b_SC{i}", [P, BANK]) for i in range(2)]
        MX = [ps(f"b_MX{i}", [P, BANK]) for i in range(2)]
        O = [ps(f"b_O{i}", [P, BANK]) for i in range(2)]
        TR = ps("b_TR", [STACK, S], BF16)
        SM = ps("b_SM", [P, BANK])
        names = ("consts", "dve_consts", "stack_ready", "stack_copied", "max_ready", "max_used", "minus_ready",
                 "turn_ready", "turn_copied", "minus_in", "scores_ready", "exp_done", "masked", "pv_done",
                 "OT_copied", "OT_ready", "inv_ready", "A2_done", "v_in", "mask_due")
        s = {k: sem(f"b_{k}") for k in names}
        loaded = [sem(f"b_loaded{i}") for i in range(2)]
        block = ctx.enter_context(nc.Block())

        def run(eng, step):
            step(0, None, 0, None)
            with eng.Fori(0, STEPS2 // 2 - 1) as u:
                step(u * 2 + 1, u * 2, 1, 0)
                step(u * 2 + 2, u * 2 + 1, 0, 1)
            step(STEPS2 - 1, STEPS2 - 2, 1, 0)
            step(None, STEPS2 - 1, None, 1)

        @block.gpsimd
        def _(pool):
            for m in (ident, identb, maskb):
                pool.memset(m[:, :], 0.0).then_inc(s["consts"], 1)
            pool.wait_ge(s["consts"], 3)
            for m in (ident, identb):
                pool.affine_select(out=m[:, :], in_=m[:, :], compare_op=ALU.not_equal, fill=1.0, base=0,
                                   pattern=[[-1, P]], channel_multiplier=1).then_inc(s["consts"], 1)
            pool.affine_select(out=maskb[:, :], in_=maskb[:, :], compare_op=ALU.is_ge, fill=NEG, base=0,
                               pattern=[[-1, P]], channel_multiplier=1).then_inc(s["consts"], 1)

            def step(n1, n2, p1, p2):
                if n2 is None:
                    return
                for k, (c, j, h) in enumerate(UNITS2):
                    if is_diag(c, j):
                        a = first_col(c, j)
                        pool.wait_ge(s["exp_done"], n2 * NU2 + k + 3)
                        pool.sem_inc(s["mask_due"], 1)
                        pool.affine_select(out=probs[k % RING2][:, a:a + P], in_=probs[k % RING2][:, a:a + P],
                                           compare_op=ALU.is_ge, fill=0.0, base=0, pattern=[[1, P]],
                                           channel_multiplier=-1).then_inc(s["masked"], 1)

            run(pool, step)

        @block.sync
        def _(sp):
            def load(n, p):
                b, g = n // KV2, n % KV2
                src = stack_dram.rearrange("(b t) p (h w) -> b p t h w", b=B, w=STACK)[bass.ds(b, 1)].rearrange("b p t h w -> (b p) t h w")
                for t in range(ST_N):
                    sp.dma_start(stk[p][:, t, 0:GROUP, :], src[:, t, bass.ds(g * GROUP, GROUP), :]).then_inc(loaded[p], 16)
                sp.dma_start(stk[p][:, :, GROUP:, :].rearrange("p t h w -> p t (h w)"), src[:, :, bass.ds(g + H2, 1), :].rearrange("p t h w -> p t (h w)")).then_inc(loaded[p], 16)

            load(0, 0)

            def step(n1, n2, p1, p2):
                if n1 is not None:
                    sp.wait_ge(s["stack_ready"], n1 * (GROUP + 1) + 1)
                    b, g = n1 // KV2, n1 % KV2
                    sp.dma_start(V[p1][:, :, :], V2[:, bass.ds(b, 1), bass.ds(g, 1), :, :].rearrange(
                        "p b g t w -> p (b g t) w")).then_inc(s["v_in"], 16)
                    if not (isinstance(n1, int) and n1 == STEPS2 - 1):
                        load(n1 + 1, 1 - p1)
                if n1 is not None:
                    sp.wait_ge(s["turn_copied"], n1 * 2 + 3)
                    for n, part in enumerate((hi, lo)):
                        sp.dma_start(Q[p1][STACK + n:STACK + n + 1, :, :].rearrange("p h s -> p (h s)"), part[:, :]).then_inc(s["minus_in"], 16)

            run(sp, step)

        @block.scalar
        def _(act):
            act.sem_inc(s["exp_done"], 2)
            act.sem_inc(s["stack_copied"], 1)
            act.sem_inc(s["OT_copied"], 2)

            def turn_out(n2, c):
                act.wait_ge(s["pv_done"], n2 * NU2 + (16 if c == 0 else NU2) + RING2)
                act.wait_ge(s["OT_ready"], n2 * 2 + c + 1)
                act.activation(OT[c][:, :], O[c][:, :], ACT.Copy).then_inc(s["OT_copied"], 1)

            def step(n1, n2, p1, p2):
                for k, (c, j, h) in enumerate(UNITS2):
                    if n2 is not None:
                        a = first_col(c, j)
                        act.wait_ge(s["scores_ready"], n2 * NU2 + k + 1)
                        act.wait_ge(s["pv_done"], n2 * NU2 + k + 1)
                        act.activation(probs[k % RING2][:, a:], SC[k % 2][:, a:], ACT.Exp,
                                       scale=DH2 ** -0.5).then_inc(s["exp_done"], 1)
                        if k == 16 + LAG2:
                            turn_out(n2, 0)
                    if n1 is not None:
                        for what, n in FILL2[k]:
                            if what == "stack":
                                act.wait_ge(s["stack_ready"], n1 * (GROUP + 1) + n + 1)
                                dst = K[p1][0:STACK, :] if n == 0 else Q[p1][0:STACK, n - 1, :]
                                act.activation(dst, TR[:, :], ACT.Copy).then_inc(s["stack_copied"], 1)
                if n2 is not None:
                    turn_out(n2, 1)

            run(act, step)

        @block.vector
        def _(dve):
            dve.memset(peak[:, :, :, :], 3 * NEG).then_inc(s["dve_consts"], 1)
            for i in range(2):
                dve.memset(K[i][STACK:, :], 1.0).then_inc(s["dve_consts"], 1)
            dve.wait_ge(s["dve_consts"], 3)
            dve.sem_inc(s["max_used"], 2)
            dve.sem_inc(s["turn_copied"], 1)
            dve.sem_inc(s["minus_in"], 1)
            dve.sem_inc(s["A2_done"], 1)

            def rows_out(n2, c):
                b, g = n2 // KV2, n2 % KV2
                dve.wait_ge(s["OT_ready"], n2 * 2 + c + 3)
                O4 = SM[:, :].rearrange("p (t h w) -> p t h w", t=4, h=GROUP)
                dve.reciprocal(inv[:, c, :, :], O4[:, :, :, DH2]).then_inc(s["inv_ready"], 1)
                dve.wait_ge(s["inv_ready"], n2 * 2 + c + 1)
                dve.tensor_tensor(A2[:, bass.ds(b * ST_N + 4 * c, 4), bass.ds(g * (GROUP * DH2), GROUP * DH2)].rearrange(
                    "p t (h d) -> p t h d", h=GROUP), O4[:, :, :, 0:DH2],
                    inv[:, c, :, :].rearrange("p t (h a) -> p t h a", a=1).to_broadcast([P, 4, GROUP, DH2]), ALU.mult).then_inc(s["A2_done"], 1)

            def step(n1, n2, p1, p2):
                for k in range(NU2):
                    if n1 is not None:
                        for what, n in FILL2[k]:
                            if what == "max":
                                h, i, ch = MAX2[n]
                                w = min(BANK, (i + 1) * P - ch * BANK)
                                dve.wait_ge(s["max_ready"], n1 * NU2 + n + 1)
                                dve.tensor_reduce(peak[:, h, i, ch:ch + 1], MX[n % 2][:, 0:w], AX.X, ALU.max).then_inc(s["max_used"], 1)
                    if n2 is not None and k == 16 + LAG2 + 3:
                        rows_out(n2, 0)
                if n1 is not None:
                    dve.wait_ge(s["max_used"], n1 * NU2 + NU2 + 2)
                    dve.tensor_reduce(minus[:, :].rearrange("p (h i) -> p h i", h=GROUP), peak[:, :, :, :],
                                      AX.X, ALU.max, negate=True).then_inc(s["minus_ready"], 1)
                    dve.wait_ge(s["turn_ready"], n1 + 1)
                    dve.wait_ge(s["minus_in"], n1 * 32 + 1)
                    T = SM[0:GROUP * ST_N, 0:P]
                    dve.tensor_copy(hi[:, :], T).then_inc(s["turn_copied"], 1)
                    dve.wait_ge(s["turn_copied"], n1 * 2 + 2)
                    dve.tensor_tensor(lo[:, :], T, hi[:, :], ALU.subtract).then_inc(s["turn_copied"], 1)
                if n2 is not None:
                    rows_out(n2, 1)

            run(dve, step)

        @block.tensor
        def _(pe):
            pe.wait_ge(s["consts"], 6)
            pe.wait_ge(s["dve_consts"], 3)
            pe.sem_inc(s["pv_done"], RING2)
            pe.sem_inc(s["OT_ready"], 2)

            def scores(n2, p2, k):
                c, j, h = UNITS2[k]
                a = first_col(c, j)
                if k == 0:
                    pe.wait_ge(s["minus_in"], n2 * 32 + 33)
                    pe.wait_ge(s["v_in"], n2 * 16 + 16)
                pe.wait_ge(s["exp_done"], n2 * NU2 + k + 1)
                pe.matmul(SC[k % 2][:, a:], K[p2][:, j * P:(j + 1) * P], Q[p2][:, h, c * BANK + a:(c + 1) * BANK],
                          start=True, stop=True).then_inc(s["scores_ready"], 1)

            def output(n2, p2, k):
                c, j, h = UNITS2[k]
                a = first_col(c, j)
                if (j, h) == (0, 0):
                    pe.wait_ge(s["OT_copied"], n2 * 2 + c + 1)
                pe.wait_ge(s["exp_done"], n2 * NU2 + k + 3)
                if is_diag(c, j):
                    pe.wait_ge(s["masked"], n2 * (GROUP * ST_N) + j * GROUP + h + 1)
                pe.matmul(O[c][32 * h:32 * h + 32, a:], V[p2][:, j, :], probs[k % RING2][:, a:], start=(j == 0),
                          stop=(j == (c + 1) * 4 - 1)).then_inc(s["pv_done"], 1)

            def turn_out(n2, c):
                pe.wait_ge(s["OT_copied"], n2 * 2 + c + 3)
                pe.wait_ge(s["A2_done"], n2 * 2 + c + 1)
                for t in range(4):
                    last = pe.transpose(SM[:, t * P:(t + 1) * P], OT[c][:, t * P:(t + 1) * P], ident[:, :])
                last.then_inc(s["OT_ready"], 1)

            def step(n1, n2, p1, p2):
                for k in range(NU2):
                    if n2 is not None:
                        scores(n2, p2, k)
                    if n1 is not None:
                        for what, n in FILL2[k]:
                            if what == "stack":
                                if n == 0:
                                    pe.wait_ge(loaded[p1], (n1 - p1) * 72 + 144)
                                pe.wait_ge(s["stack_copied"], n1 * (GROUP + 1) + n + 1)
                                for t in range(ST_N):
                                    last = pe.transpose(TR[:, t * P:(t + 1) * P], stk[p1][:, t, (n - 1) % (GROUP + 1), :], identb[:, :])
                                last.then_inc(s["stack_ready"], 1)
                            else:
                                h, i, ch = MAX2[n]
                                w = min(BANK, (i + 1) * P - ch * BANK)
                                diag = ch == i * P // BANK
                                if n == 0:
                                    pe.wait_ge(s["stack_copied"], n1 * (GROUP + 1) + GROUP + 2)
                                pe.wait_ge(s["max_used"], n1 * NU2 + n + 1)
                                last = pe.matmul(MX[n % 2][:, 0:w], Q[p1][0:STACK, h, i * P:(i + 1) * P],
                                                 K[p1][0:STACK, ch * BANK:ch * BANK + w], start=True, stop=not diag)
                                if diag:
                                    last = pe.matmul(MX[n % 2][:, w - P:w], identb[:, :], maskb[:, :], start=False, stop=True)
                                last.then_inc(s["max_ready"], 1)
                    if n2 is not None:
                        if k >= LAG2:
                            output(n2, p2, k - LAG2)
                        if k == 16 + LAG2 + 2:
                            if n1 is not None:
                                pe.wait_ge(s["turn_copied"], n1 * 2 + 1)
                            turn_out(n2, 0)
                if n2 is not None:
                    for k in range(NU2 - LAG2, NU2):
                        output(n2, p2, k)
                if n1 is not None:
                    pe.wait_ge(s["minus_ready"], n1 + 1)
                    if n2 is not None:
                        pe.wait_ge(s["A2_done"], n2 * 2 + 2)
                    pe.transpose(SM[0:GROUP * ST_N, 0:P], minus[:, :], ident[:, :]).then_inc(s["turn_ready"], 1)
                    if n2 is not None:
                        pe.wait_ge(s["turn_copied"], n1 * 2 + 3)
                if n2 is not None:
                    turn_out(n2, 1)

            run(pe, step)


EXPERTS, FFN = 8, 512
KF = FFN // P
SLOTS = (2 * TOK + EXPERTS * (P - 1)) // P
SLOTS += SLOTS % 2


def route(nc, hold, norm_z, shift_z, A2, w_out, ln2, w_gate, sorted_rows, weight, place, expert_of):
    rows = hold.rearrange("p b k s -> p (b k s)").rearrange("p (t d) -> p t d", d=D)
    with ExitStack() as ctx:
        sb = lambda name, shape, dt=F32: ctx.enter_context(nc.sbuf_tensor(name, shape, dt))
        ps = lambda name, shape, dt=F32: ctx.enter_context(nc.psum_tensor(name, shape, dt))
        sem = lambda name: ctx.enter_context(nc.semaphore(name))
        Wo = sb("r_Wo", [P, KD, D])
        Wg = sb("r_Wg", [P, KD, EXPERTS])
        ln = sb("r_ln", [P, KD])
        ident = sb("r_ident", [P, P])
        before = sb("r_before", [P, P], BF16)
        ones = sb("r_ones", [P, P], BF16)
        H = sb("r_H", [P, NT, D])
        zeros = sb("r_zeros", [P, 8, D])
        stage = [sb(f"r_stage{i}", [P, D]) for i in range(2)]
        HN = [sb(f"r_HN{i}", [P, D]) for i in range(2)]
        hT = [sb(f"r_hT{i}", [P, KD, P]) for i in range(2)]
        Z = [sb(f"r_Z{i}", [P, D]) for i in range(2)]
        square = sb("r_square", [P, D])
        total = sb("r_total", [P, NT])
        std = sb("r_std", [P, NT])
        logits = sb("r_logits", [P, NT, EXPERTS])
        rank = sb("r_rank", [P, NT, EXPERTS])
        slots = sb("r_slots", [P, SLOTS])
        small = {k: sb(f"r_{k}", [P, NT, EXPERTS]) for k in ("a", "b", "first", "second", "sa", "sb", "pos")}
        count = sb("r_count", [P, NT, EXPERTS], BF16)
        col = {k: sb(f"r_c_{k}", [P, NT]) for k in ("m1", "m2", "top", "e")}
        ex = {k: sb(f"r_e_{k}", [P, EXPERTS]) for k in ("tiles", "end", "end2", "start")}
        exi = sb("r_exi", [P, EXPERTS], mybir.dt.int32)
        cmp = sb("r_cmp", [1, SLOTS, EXPERTS - 1])
        eidx = sb("r_eidx", [1, SLOTS])
        T = [ps(f"r_T{i}", [P, BANK]) for i in range(2)]
        Y = [ps(f"r_Y{i}", [P, BANK]) for i in range(2)]
        CT = [ps(f"r_CT{i}", [P, BANK]) for i in range(2)]
        names = ("w_in", "consts", "zeros_set", "zeroed", "turned", "hT_ready", "y_ready", "x2_ready", "z_ready", "summed", "var_ready", "std_ready",
                 "h_ready", "lg_ready", "lg_copied", "step", "counted", "prefix_ready", "gap_ready", "share_ready", "placed", "scattered")
        s = {k: sem(f"r_{k}") for k in names}
        staged = [sem(f"r_staged{i}") for i in range(2)]
        kept = [sem(f"r_kept{i}") for i in range(2)]
        block = ctx.enter_context(nc.Block())

        def tile_of(t, n):
            return t[:, bass.ds(n, 1), :].rearrange("p a d -> p (a d)")

        @block.sync
        def _(sp):
            for i in range(2):
                sp.dma_start(stage[i][:, :], A2[:, i, :]).then_inc(staged[i], 16)
            for dst, src in ((Wo, w_out), (Wg, w_gate)):
                sp.dma_start(dst[:, :, :], src).then_inc(s["w_in"], 16)
            sp.dma_start(ln[:, :], ln2).then_inc(s["w_in"], 16)
            sp.wait_ge(s["zeros_set"], 1)
            for i in range(SLOTS // 8):
                sp.dma_start(sorted_rows.rearrange("(n p) d -> p n d", p=P)[:, 8 * i:8 * i + 8, :], zeros[:, :, :]).then_inc(s["zeroed"], 16)
            with sp.Fori(0, NT // 2 - 1) as g:
                for i in range(2):
                    sp.wait_ge(s["turned"], g * 2 + i + 1)
                    sp.dma_start(stage[i][:, :], tile_of(A2, g * 2 + (2 + i))).then_inc(staged[i], 16)
            with sp.Fori(0, NT // 2) as g:
                for i in range(2):
                    sp.wait_ge(s["h_ready"], g * 2 + i + 1)
                    sp.dma_start(tile_of(H, g * 2 + i), HN[i][:, :]).then_inc(kept[i], 16)

        @block.gpsimd
        def _(pool):
            pool.memset(zeros[:, :, :], 0.0).then_inc(s["zeros_set"], 1)
            pool.memset(ident[:, :], 0.0).then_inc(s["consts"], 1)
            pool.memset(before[:, :], 1.0).then_inc(s["consts"], 1)
            pool.memset(ones[:, :], 1.0).then_inc(s["consts"], 1)
            pool.iota(slots[:, :], pattern=[[1, SLOTS]], base=0, channel_multiplier=0,
                      allow_small_or_imprecise_dtypes=True).then_inc(s["consts"], 1)
            for e in range(EXPERTS):
                pool.memset(rank[:, :, e:e + 1], float(EXPERTS - e)).then_inc(s["consts"], 1)
            pool.wait_ge(s["consts"], 4 + EXPERTS)
            pool.affine_select(out=ident[:, :], in_=ident[:, :], compare_op=ALU.not_equal, fill=1.0, base=0,
                               pattern=[[-1, P]], channel_multiplier=1).then_inc(s["consts"], 1)
            pool.affine_select(out=before[:, :], in_=before[:, :], compare_op=ALU.is_gt, fill=0.0, base=0,
                               pattern=[[1, P]], channel_multiplier=-1).then_inc(s["consts"], 1)
            pool.wait_ge(s["placed"], 1)
            pool.wait_ge(s["zeroed"], 16 * (SLOTS // 8))
            for i in range(2):
                pool.wait_ge(kept[i], 16 * (NT // 2) + 1)
            for t in range(NT):
                for k in range(2):
                    pool.indirect_dma_start(out=sorted_rows, out_offset=bass.IndirectOffsetOnAxis(ap=place[:, k, t:t + 1], axis=0),
                                            in_=H[:, t, :], in_offset=None).then_inc(s["scattered"], 16)
            pool.wait_ge(s["scattered"], 16 * 2 * NT)

        @block.tensor
        def _(pe):
            pe.wait_ge(s["consts"], 6 + EXPERTS)
            pe.wait_ge(s["w_in"], 48)
            pe.sem_inc(s["hT_ready"], 4)
            pe.sem_inc(s["x2_ready"], 2)
            with pe.Fori(0, NT // 2) as g:
                for i in range(2):
                    t = g * 2 + i
                    pe.wait_ge(staged[i], g * 16 + 16)
                    pe.wait_ge(s["hT_ready"], t * 2 + 2)
                    for kt in range(KD):
                        last = pe.transpose(T[i][:, kt * P:(kt + 1) * P], stage[i][:, kt * P:(kt + 1) * P], ident[:, :])
                    last.then_inc(s["turned"], 1)
                for i in range(2):
                    t = g * 2 + i
                    pe.wait_ge(s["hT_ready"], t * 2 + 6)
                    pe.wait_ge(s["x2_ready"], t + 1)
                    for kt in range(KD):
                        last = pe.matmul(Y[i][:, 0:D], hT[i][:, kt, :], Wo[:, kt, :], start=(kt == 0), stop=(kt == KD - 1))
                    last.then_inc(s["y_ready"], 1)
            with pe.Fori(0, NT // 2) as g:
                for i in range(2):
                    t = g * 2 + i
                    pe.wait_ge(s["h_ready"], t + 1)
                    pe.wait_ge(s["hT_ready"], t * 2 + (2 * NT + 2))
                    for kt in range(KD):
                        last = pe.transpose(T[i][:, kt * P:(kt + 1) * P], HN[i][:, kt * P:(kt + 1) * P], ident[:, :])
                    last.then_inc(s["turned"], 1)
                for i in range(2):
                    t = g * 2 + i
                    pe.wait_ge(s["hT_ready"], t * 2 + (2 * NT + 6))
                    pe.wait_ge(s["x2_ready"], NT + 2)
                    pe.wait_ge(s["lg_copied"], t + 1)
                    for kt in range(KD):
                        last = pe.matmul(Y[i][:, 0:EXPERTS], hT[i][:, kt, :], Wg[:, kt, :], start=(kt == 0), stop=(kt == KD - 1))
                    last.then_inc(s["lg_ready"], 1)
            pe.wait_ge(s["counted"], 1)
            flat = count[:, :, :].rearrange("p t e -> p (t e)")
            pe.matmul(CT[0][:, 0:NT * EXPERTS], before[:, :], flat, start=True, stop=True).then_inc(s["prefix_ready"], 1)
            pe.matmul(CT[1][:, 0:NT * EXPERTS], ones[:, :], flat, start=True, stop=True).then_inc(s["prefix_ready"], 1)

        @block.scalar
        def _(act):
            act.wait_ge(s["w_in"], 48)
            with act.Fori(0, NT // 2) as g:
                for i in range(2):
                    t = g * 2 + i
                    act.wait_ge(s["turned"], t + 1)
                    for kt in range(KD):
                        act.activation(hT[i][:, kt, :], T[i][:, kt * P:(kt + 1) * P], ACT.Copy).then_inc(s["hT_ready"], 1)
                for i in range(2):
                    t = g * 2 + i
                    act.wait_ge(s["x2_ready"], t + 3)
                    act.wait_ge(s["summed"], t + 1)
                    act.activation(square[:, :], tile_of(A2, t), ACT.Square, accum_out=total[:, bass.ds(t, 1)]).then_inc(s["summed"], 1)
            act.wait_ge(s["var_ready"], 1)
            act.activation(std[:, :], total[:, :], ACT.Sqrt).then_inc(s["std_ready"], 1)
            with act.Fori(0, NT // 2) as g:
                for i in range(2):
                    t = g * 2 + i
                    act.wait_ge(s["turned"], t + (NT + 1))
                    for kt in range(KD):
                        act.activation(hT[i][:, kt, :], T[i][:, kt * P:(kt + 1) * P], ACT.Copy,
                                       scale=ln[:, kt:kt + 1]).then_inc(s["hT_ready"], 1)
                for i in range(2):
                    t = g * 2 + i
                    act.wait_ge(s["lg_ready"], t + 1)
                    act.activation(tile_of(logits, t), Y[i][:, 0:EXPERTS], ACT.Copy).then_inc(s["lg_copied"], 1)
            act.wait_ge(s["gap_ready"], 1)
            act.activation(col["e"][:, :], col["e"][:, :], ACT.Exp).then_inc(s["share_ready"], 1)

        @block.vector
        def _(dve):
            dve.sem_inc(s["summed"], 1)
            dve.sem_inc(s["lg_copied"], 2)
            for i in range(2):
                dve.sem_inc(kept[i], 1)
            with dve.Fori(0, NT // 2) as g:
                for i in range(2):
                    t = g * 2 + i
                    dve.wait_ge(s["x2_ready"], t + 1)
                    dve.tensor_scalar(Z[i][:, :], tile_of(rows, t), norm_z[:, bass.ds(t, 1)], shift_z[:, bass.ds(t, 1)],
                                      ALU.mult, ALU.add).then_inc(s["z_ready"], 1)
                for i in range(2):
                    t = g * 2 + i
                    dve.wait_ge(s["z_ready"], t + 1)
                    dve.wait_ge(s["y_ready"], t + 1)
                    dve.tensor_tensor(tile_of(A2, t), Z[i][:, :], Y[i][:, 0:D], ALU.add).then_inc(s["x2_ready"], 1)
            link = counted(dve, s["step"], 0)
            dve.wait_ge(s["summed"], NT + 1)
            link(dve.tensor_scalar(total[:, :], total[:, :], 1.0 / D, EPS, ALU.mult, ALU.add))
            dve.sem_inc(s["var_ready"], 1)
            dve.wait_ge(s["std_ready"], 1)
            link(dve.reciprocal(std[:, :], std[:, :]))
            with dve.Fori(0, NT // 2) as g:
                for i in range(2):
                    t = g * 2 + i
                    dve.wait_ge(s["turned"], t + (NT - 1))
                    dve.wait_ge(kept[i], g * 16 + 1)
                    dve.tensor_scalar(HN[i][:, :], tile_of(A2, t), std[:, bass.ds(t, 1)], None, ALU.mult).then_inc(s["h_ready"], 1)
            dve.wait_ge(s["lg_copied"], NT + 2)
            dve.wait_ge(s["consts"], 6 + EXPERTS)
            v = {k: x[:, :, :] for k, x in small.items()}
            c = {k: x[:, :] for k, x in col.items()}
            L = logits[:, :, :]

            def wide(x):
                return x.rearrange("p (t a) -> p t a", a=1).to_broadcast([P, NT, EXPERTS])

            def best(scores, out, peak):
                link(dve.tensor_reduce(peak, scores, AX.X, ALU.max))
                link(dve.tensor_tensor(v["a"], scores, wide(peak), ALU.is_equal))
                link(dve.tensor_tensor(v["a"], v["a"], rank[:, :, :], ALU.mult))
                link(dve.tensor_reduce(c["top"], v["a"], AX.X, ALU.max))
                link(dve.tensor_tensor(out, v["a"], wide(c["top"]), ALU.is_equal))

            best(L, v["first"], c["m1"])
            link(dve.scalar_tensor_tensor(out=v["b"], in0=v["first"], scalar=3 * NEG, in1=L, op0=ALU.mult, op1=ALU.add))
            best(v["b"], v["second"], c["m2"])
            link(dve.tensor_tensor(c["e"], c["m2"], c["m1"], ALU.subtract))
            dve.sem_inc(s["gap_ready"], 1)
            link(dve.tensor_tensor(count[:, :, :], v["first"], v["second"], ALU.add))
            dve.sem_inc(s["counted"], 1)
            dve.wait_ge(s["share_ready"], 1)
            link(dve.tensor_scalar(c["top"], c["e"], 1.0, None, ALU.add))
            link(dve.reciprocal(weight[:, 0, :], c["top"]))
            link(dve.tensor_tensor(weight[:, 1, :], weight[:, 0, :], c["e"], ALU.mult))
            dve.wait_ge(s["prefix_ready"], 2)
            tot = CT[1][:, 0:NT * EXPERTS].rearrange("p (t e) -> p t e", e=EXPERTS)
            link(dve.tensor_copy(v["sa"], tot))
            a, b = "sa", "sb"
            gap = 1
            while gap < NT:
                link(dve.tensor_copy(v[b][:, 0:gap], v[a][:, 0:gap]))
                link(dve.tensor_tensor(v[b][:, gap:], v[a][:, gap:], v[a][:, 0:NT - gap], ALU.add))
                a, b = b, a
                gap *= 2
            n = v[a][:, NT - 1]
            link(dve.tensor_scalar(exi[:, :], n, (P - 1) / 1.0 - P / 2 + 0.5, 1.0 / P, ALU.add, ALU.mult))
            link(dve.tensor_copy(ex["tiles"][:, :], exi[:, :]))
            link(dve.tensor_copy(ex["end"][:, :], ex["tiles"][:, :]))
            p, q = "end", "end2"
            gap = 1
            while gap < EXPERTS:
                link(dve.tensor_copy(ex[q][:, 0:gap], ex[p][:, 0:gap]))
                link(dve.tensor_tensor(ex[q][:, gap:], ex[p][:, gap:], ex[p][:, 0:EXPERTS - gap], ALU.add))
                p, q = q, p
                gap *= 2
            link(dve.tensor_tensor(ex["start"][:, :], ex[p][:, :], ex["tiles"][:, :], ALU.subtract))
            link(dve.tensor_scalar(ex["start"][:, :], ex["start"][:, :], float(P), None, ALU.mult))
            link(dve.tensor_tensor(v["pos"], v[a], tot, ALU.subtract))
            pre = CT[0][:, 0:NT * EXPERTS].rearrange("p (t e) -> p t e", e=EXPERTS)
            link(dve.tensor_tensor(v["pos"], v["pos"], pre, ALU.add))
            link(dve.tensor_tensor(v["pos"], v["pos"], ex["start"][:, :].rearrange("p (a e) -> p a e", a=1).to_broadcast([P, NT, EXPERTS]),
                                   ALU.add))
            for k, pick in enumerate(("first", "second")):
                link(dve.tensor_tensor(v["a"], v["pos"], v[pick], ALU.mult))
                link(dve.tensor_reduce(c["top"], v["a"], AX.X, ALU.add))
                link(dve.tensor_copy(place[:, k, :], c["top"]))
            dve.sem_inc(s["placed"], 1)
            link(dve.tensor_tensor(cmp[:, :, :], slots[0:1, :].rearrange("p (t a) -> p t a", a=1).to_broadcast([1, SLOTS, EXPERTS - 1]),
                                   ex[p][0:1, 0:EXPERTS - 1].rearrange("p (a e) -> p a e", a=1).to_broadcast([1, SLOTS, EXPERTS - 1]),
                                   ALU.is_ge))
            link(dve.tensor_reduce(eidx[:, :], cmp[:, :, :], AX.X, ALU.add))
            link(dve.tensor_copy(expert_of, eidx[:, :]))


def experts(nc, sorted_rows, done_rows, w13, w2, ln2, expert_of):
    with ExitStack() as ctx:
        sb = lambda name, shape, dt=F32: ctx.enter_context(nc.sbuf_tensor(name, shape, dt))
        ps = lambda name, shape, dt=F32: ctx.enter_context(nc.psum_tensor(name, shape, dt))
        sem = lambda name: ctx.enter_context(nc.semaphore(name))
        W13 = sb("e_W13", [P, EXPERTS, KD, 2 * FFN])
        W2 = sb("e_W2", [P, EXPERTS, KF, D])
        ln = sb("e_ln", [P, KD])
        ident = sb("e_ident", [P, P])
        G = [sb(f"e_G{i}", [P, D]) for i in range(2)]
        hT = [sb(f"e_hT{i}", [P, KD, P]) for i in range(2)]
        gate = [sb(f"e_gate{i}", [P, FFN]) for i in range(2)]
        act_T = [sb(f"e_actT{i}", [P, KF, P]) for i in range(2)]
        out = [sb(f"e_out{i}", [P, D]) for i in range(2)]
        T = ps("e_T", [P, BANK])
        GU = [[ps(f"e_GU{i}{k}", [P, BANK]) for k in range(2)] for i in range(2)]
        AT = ps("e_AT", [P, BANK])
        Y = [ps(f"e_Y{i}", [P, BANK]) for i in range(2)]
        names = ("w13_in", "w2_in", "ln_in", "consts", "turned", "hT_ready", "gu_ready", "gated", "act_ready", "at_ready", "actT_ready",
                 "y_ready", "y_copied")
        s = {k: sem(f"e_{k}") for k in names}
        rows_in = [sem(f"e_rows_in{i}") for i in range(2)]
        stored = [sem(f"e_stored{i}") for i in range(2)]
        block = ctx.enter_context(nc.Block())

        def slot(t, n):
            return t.rearrange("(n p) d -> n p d", p=P)[bass.ds(n, 1)].rearrange("n p d -> (n p) d")

        @block.sync
        def _(sp):
            sp.dma_start(ln[:, :], ln2).then_inc(s["ln_in"], 16)
            for i in range(2):
                sp.dma_start(G[i][:, :], sorted_rows[i * P:(i + 1) * P, :]).then_inc(rows_in[i], 16)
            for e in range(EXPERTS):
                sp.dma_start(W13[:, e, :, :], w13[:, e, :, :]).then_inc(s["w13_in"], 16)
                sp.dma_start(W2[:, e, :, :], w2[:, e, :, :]).then_inc(s["w2_in"], 16)
            with sp.Fori(0, SLOTS // 2) as g:
                for i in range(2):
                    if i == 0:
                        sp.wait_ge(s["turned"], g * 2 + 1)
                    else:
                        sp.wait_ge(s["turned"], g * 2 + 2)
                    sp.dma_start(G[i][:, :], slot(sorted_rows, (g * 2 + (2 + i)) % SLOTS)).then_inc(rows_in[i], 16)
                    sp.wait_ge(s["y_copied"], g * 2 + i + 3)
                    sp.dma_start(slot(done_rows, g * 2 + i), out[i][:, :]).then_inc(stored[i], 16)
            for i in range(2):
                sp.wait_ge(stored[i], 16 * (SLOTS // 2) + 1)
                sp.wait_ge(rows_in[i], 16 * (SLOTS // 2 + 1))

        @block.gpsimd
        def _(pool):
            pool.memset(ident[:, :], 0.0).then_inc(s["consts"], 1)
            pool.wait_ge(s["consts"], 1)
            pool.affine_select(out=ident[:, :], in_=ident[:, :], compare_op=ALU.not_equal, fill=1.0, base=0,
                               pattern=[[-1, P]], channel_multiplier=1).then_inc(s["consts"], 1)

        @block.tensor
        def _(pe):
            pe.wait_ge(s["consts"], 2)
            pe.sem_inc(s["hT_ready"], 1)
            pe.sem_inc(s["gated"], 2)
            pe.sem_inc(s["actT_ready"], 1)
            pe.sem_inc(s["y_copied"], 2)

            def turn(n, i):
                pe.wait_ge(rows_in[i], (n - i) * 8 + 16)
                pe.wait_ge(s["hT_ready"], n * 2 + 1)
                for kt in range(KD):
                    last = pe.transpose(T[:, kt * P:(kt + 1) * P], G[i][:, kt * P:(kt + 1) * P], ident[:, :])
                last.then_inc(s["turned"], 1)

            def up(n, i):
                e = pe.value_load(expert_of[0:1, bass.ds(n, 1)], min_val=0, max_val=EXPERTS - 1)
                pe.wait_ge(s["hT_ready"], n * 2 + 3)
                pe.wait_ge(s["gated"], n + 1)
                for half in range(2):
                    for kt in range(KD):
                        last = pe.matmul(GU[i][half][:, :], hT[i][:, kt, :],
                                         W13[:, bass.ds(e, 1), kt, half * FFN:(half + 1) * FFN].rearrange("p a f -> p (a f)"),
                                         start=(kt == 0), stop=(kt == KD - 1))
                    last.then_inc(s["gu_ready"], 1)

            def turn_act(n, i):
                pe.wait_ge(s["gated"], n + 3)
                pe.wait_ge(s["actT_ready"], n + 1)
                for kt in range(KF):
                    last = pe.transpose(AT[:, kt * P:(kt + 1) * P], gate[i][:, kt * P:(kt + 1) * P], ident[:, :])
                last.then_inc(s["at_ready"], 1)

            def down(n, i):
                e = pe.value_load(expert_of[0:1, bass.ds(n, 1)], min_val=0, max_val=EXPERTS - 1)
                pe.wait_ge(s["actT_ready"], n + 2)
                pe.wait_ge(s["y_copied"], n + 1)
                for kt in range(KF):
                    last = pe.matmul(Y[i][:, 0:D], act_T[i][:, kt, :], W2[:, bass.ds(e, 1), kt, :].rearrange("p a d -> p (a d)"),
                                     start=(kt == 0), stop=(kt == KF - 1))
                last.then_inc(s["y_ready"], 1)

            turn(0, 0)
            pe.wait_ge(s["w13_in"], 16 * EXPERTS)
            up(0, 0)
            turn(1, 1)
            turn_act(0, 0)
            pe.wait_ge(s["w2_in"], 16 * EXPERTS)
            with pe.Fori(0, SLOTS // 2 - 1) as g:
                m = g * 2 + 1
                up(m, 1)
                turn(m + 1, 0)
                down(m - 1, 0)
                turn_act(m, 1)
                up(m + 1, 0)
                turn(m + 2, 1)
                down(m, 1)
                turn_act(m + 1, 0)
            up(SLOTS - 1, 1)
            down(SLOTS - 2, 0)
            turn_act(SLOTS - 1, 1)
            down(SLOTS - 1, 1)

        @block.scalar
        def _(act):
            act.wait_ge(s["ln_in"], 16)

            def feed(n, i):
                act.wait_ge(s["turned"], n + 1)
                for kt in range(KD):
                    act.activation(hT[i][:, kt, :], T[:, kt * P:(kt + 1) * P], ACT.Copy, scale=ln[:, kt:kt + 1]).then_inc(s["hT_ready"], 1)

            def silu(n, i):
                act.wait_ge(s["gu_ready"], n * 2 + 1)
                act.wait_ge(s["at_ready"], n + 1)
                act.activation(gate[i][:, :], GU[i][0][:, :], ACT.Silu).then_inc(s["act_ready"], 1)

            def rows(n, i):
                act.wait_ge(s["y_ready"], n + 1)
                act.wait_ge(stored[i], (n - i) * 8 + 1)
                act.activation(out[i][:, :], Y[i][:, 0:D], ACT.Copy).then_inc(s["y_copied"], 1)

            act.sem_inc(s["at_ready"], 2)
            act.sem_inc(stored[0], 1)
            act.sem_inc(stored[1], 1)
            feed(0, 0)
            silu(0, 0)
            feed(1, 1)
            with act.Fori(0, SLOTS // 2 - 1) as g:
                m = g * 2 + 1
                silu(m, 1)
                feed(m + 1, 0)
                rows(m - 1, 0)
                silu(m + 1, 0)
                feed(m + 2, 1)
                rows(m, 1)
            silu(SLOTS - 1, 1)
            rows(SLOTS - 2, 0)
            rows(SLOTS - 1, 1)

        @block.vector
        def _(dve):
            with dve.Fori(0, SLOTS // 2) as g:
                for i in range(2):
                    n = g * 2 + i
                    dve.wait_ge(s["act_ready"], n + 1)
                    dve.wait_ge(s["gu_ready"], n * 2 + 2)
                    dve.tensor_tensor(gate[i][:, :], gate[i][:, :], GU[i][1][:, :], ALU.mult).then_inc(s["gated"], 1)
                    dve.wait_ge(s["at_ready"], n + 3)
                    dve.tensor_copy(act_T[i][:, :, :].rearrange("p k q -> p (k q)"), AT[:, :]).then_inc(s["actT_ready"], 1)


def combine(nc, hold, A2, weight, place, done_rows, out):
    rows = hold.rearrange("p b k s -> p (b k s)").rearrange("p (t d) -> p t d", d=D)
    with ExitStack() as ctx:
        sb = lambda name, shape, dt=F32: ctx.enter_context(nc.sbuf_tensor(name, shape, dt))
        sem = lambda name: ctx.enter_context(nc.semaphore(name))
        E = [sb(f"c_E{k}", [P, NT, D]) for k in range(2)]
        stats = sb("c_stats", [P, NT, 6])
        small = {k: sb(f"c_{k}", [P, NT]) for k in ("mean2", "diff", "var", "std", "scale", "shift")}
        Y = [sb(f"c_Y{i}", [P, D]) for i in range(4)]
        s = {k: sem(f"c_{k}") for k in ("halfway", "mixed", "step", "var_ready", "std_ready", "y_ready", "row_ready", "stored")}
        fetched = [sem(f"c_fetched{i}") for i in range(4)]
        block = ctx.enter_context(nc.Block())

        def tile_of(t, n):
            return t[:, bass.ds(n, 1), :].rearrange("p a d -> p (a d)")

        @block.gpsimd
        def _(pool):
            for t in range(NT):
                for k in range(2):
                    pool.indirect_dma_start(out=E[k][:, t, :], out_offset=None, in_=done_rows,
                                            in_offset=bass.IndirectOffsetOnAxis(ap=place[:, k, t:t + 1], axis=0)).then_inc(fetched[t // 8], 16)

        @block.vector
        def _(dve):
            dve.sem_inc(s["row_ready"], 1)
            for i in range(4):
                dve.wait_ge(fetched[i], 16 * 2 * 8)
                with dve.Fori(4 * i, 4 * i + 4) as g:
                    for k in range(2):
                        for u in range(2):
                            t = g * 2 + u
                            if k:
                                dve.wait_ge(s["halfway"], t + 1)
                            dve.scalar_tensor_tensor(out=tile_of(A2, t), in0=tile_of(E[k], t), scalar=weight[:, k, bass.ds(t, 1)],
                                                     in1=tile_of(A2, t), op0=ALU.mult, op1=ALU.add).then_inc(s["mixed"] if k else s["halfway"], 1)
                    for u in range(2):
                        dve.wait_ge(s["mixed"], g * 2 + u + 1)
                        dve.bn_stats(tile_of(stats, g * 2 + u), tile_of(A2, g * 2 + u)).then_inc(s["step"], 1)
            dve.wait_ge(s["step"], NT)
            link = counted(dve, s["step"], NT)
            moments(dve, link, stats, small["mean2"], small["diff"], small["var"])
            dve.sem_inc(s["var_ready"], 1)
            dve.wait_ge(s["std_ready"], 1)
            link(dve.reciprocal(small["scale"][:, :], small["std"][:, :]))
            link(dve.scalar_tensor_tensor(out=small["shift"][:, :], in0=small["mean2"][:, :], scalar=-0.5, in1=small["scale"][:, :],
                                          op0=ALU.mult, op1=ALU.mult))
            dve.sem_inc(s["var_ready"], 1)
            with dve.Fori(0, NT // 4) as g:
                for k in range(4):
                    dve.wait_ge(s["y_ready"], g * 4 + k + 1)
                    dve.tensor_tensor(tile_of(rows, g * 4 + k), Y[k][:, :], tile_of(rows, g * 4 + k), ALU.add).then_inc(s["row_ready"], 1)

        @block.scalar
        def _(act):
            act.wait_ge(s["var_ready"], 1)
            act.activation(small["std"][:, :], small["var"][:, :], ACT.Sqrt).then_inc(s["std_ready"], 1)
            act.wait_ge(s["var_ready"], 2)
            act.sem_inc(s["row_ready"], 3)
            with act.Fori(0, NT // 4) as g:
                for k in range(4):
                    t = g * 4 + k
                    act.wait_ge(s["row_ready"], t + 1)
                    act.activation(Y[k][:, :], tile_of(A2, t), ACT.Identity, scale=small["scale"][:, bass.ds(t, 1)],
                                   bias=small["shift"][:, bass.ds(t, 1)]).then_inc(s["y_ready"], 1)

        @block.sync
        def _(sp):
            o = out.rearrange("(t p) d -> p t d", p=P)
            for i in range(8):
                sp.wait_ge(s["row_ready"], 4 * i + 8)
                sp.dma_start(o[:, 4 * i:4 * i + 4, :], rows[:, 4 * i:4 * i + 4, :]).then_inc(s["stored"], 16)
            sp.wait_ge(s["stored"], 16 * 8)


def layer(nc, x, w_pair, w_out1, w_qkv2, w_out2, ln1, ln2, w_gate, w13, w2, cos2, sin2, out):
    nc.disable_value_cache = True
    stack_dram = nc.dram_tensor("stack_rows", [NT, P, HEADS2 * STACK], BF16, kind="Internal").ap()
    sorted_rows = nc.dram_tensor("sorted_rows", [SLOTS * P, D], F32, kind="Internal").ap()
    done_rows = nc.dram_tensor("done_rows", [SLOTS * P, D], F32, kind="Internal").ap()
    with ExitStack() as ctx:
        sb = lambda name, shape, dt=F32: ctx.enter_context(nc.sbuf_tensor(name, shape, dt))
        hold = sb("hold", [P, B, KD, S])[:, :, :, :]
        norm_z, shift_z = sb("norm_z", [P, NT])[:, :], sb("shift_z", [P, NT])[:, :]
        normalise(nc, x, hold)
        attention_one(nc, hold, w_pair, w_out1)
        weight = sb("weight", [P, 2, NT])[:, :, :]
        place = sb("place", [P, 2, NT], mybir.dt.uint32)[:, :, :]
        expert_of = sb("expert_of", [1, SLOTS], mybir.dt.int32)[:, :]
        A2 = sb("A2", [P, NT, D])[:, :, :]
        with ExitStack() as inner:
            V2 = inner.enter_context(nc.sbuf_tensor("V2", [P, B, KV2, ST_N, 2 * DH2], F32))[:, :, :, :, :]
            project_two(nc, x, hold, w_qkv2, ln1, cos2, sin2, norm_z, shift_z, V2, stack_dram)
            attention_two(nc, stack_dram, V2, A2)
        route(nc, hold, norm_z, shift_z, A2, w_out2, ln2, w_gate, sorted_rows, weight, place, expert_of)
        experts(nc, sorted_rows, done_rows, w13, w2, ln2, expert_of)
        combine(nc, hold, A2, weight, place, done_rows, out)


def kernel(**inputs):
    import concourse.bacc as bacc
    from concourse.bass_utils import run_bass_kernel_spmd as run

    a = {k: np.asarray(v) for k, v in inputs.items()}

    def turned(w, cols=None):
        return np.ascontiguousarray(w.T.reshape(w.shape[1] // P, P, w.shape[0]).transpose(1, 0, 2))

    f = np.float32
    inv_freq = (f(1) / np.power(f(10000.0), np.arange(0, DH2, 2, dtype=f) / f(DH2))).astype(f)
    angle = np.arange(S, dtype=f)[:, None] * inv_freq[None, :]
    table = lambda left, right: np.ascontiguousarray(
        np.concatenate([left, right], 1).astype(f).reshape(ST_N, P, DH2).transpose(1, 0, 2))
    qkv = np.stack([a["L0_attn_w_q"].reshape(H1 * DH1, D), a["L0_attn_w_k"].reshape(H1 * DH1, D),
                    a["L0_attn_w_v"].reshape(H1 * DH1, D)])
    arrays = {
        "x": np.ascontiguousarray(a["L0_attn_x"].reshape(TOK, D)),
        "w_pair": np.ascontiguousarray(qkv.reshape(3, PAIRS, P, KD, P).transpose(1, 4, 3, 0, 2)),
        "w_out1": turned(a["L0_attn_w_o"]),
        "w_qkv2": turned(a["L0_ffn_wqkv"]),
        "w_out2": turned(a["L0_ffn_wo"]),
        "ln1": np.ascontiguousarray(a["L0_ffn_ln1_w"].reshape(KD, P).T),
        "ln2": np.ascontiguousarray(a["L0_ffn_ln2_w"].reshape(KD, P).T),
        "w_gate": turned(a["L0_ffn_gate_w"]),
        "w13": np.ascontiguousarray(a["L0_ffn_w13"].reshape(EXPERTS, 2 * FFN, KD, P).transpose(3, 0, 2, 1)),
        "w2": np.ascontiguousarray(a["L0_ffn_w2"].reshape(EXPERTS, D, KF, P).transpose(3, 0, 2, 1)),
        "cos2": table(np.cos(angle), np.cos(angle)),
        "sin2": table(-np.sin(angle), np.sin(angle)),
    }
    nc = bacc.Bacc("TRN2", target_bir_lowering=False, num_devices=1)
    args = {k: nc.dram_tensor(f"in_{k}", v.shape, mybir.dt.from_np(v.dtype), kind="ExternalInput").ap()
            for k, v in arrays.items()}
    out = nc.dram_tensor("out_rows", (TOK, D), F32, kind="ExternalOutput").ap()
    layer(nc, out=out, **args)
    r = run(nc, [{f"in_{k}": v for k, v in arrays.items()}], core_ids=[0])
    return r.results[0]["out_rows"].reshape(B, S, D)
```

```python
from contextlib import ExitStack

import numpy as np

import concourse.bass as bass
from concourse import mybir

F32 = mybir.dt.float32
F32R = mybir.dt.float32r
BF16 = mybir.dt.bfloat16
ALU = mybir.AluOpType
ACT = mybir.ActivationFunctionType
AX = mybir.AxisListType

P = 128
BANK = 512
B, S, D = 4, 1024, 256
TOK = B * S
NT = TOK // P
KD = D // P
ST_N = S // P
EPS = 1e-5
NEG = -1e30

H1, DH1 = 16, 64
PAIRS = H1 // 2

UNITS = [(c, j) for c in range(S // BANK) for j in range((c + 1) * BANK // P)]
NU = len(UNITS)
LAST = [n for n, (c, j) in enumerate(UNITS) if j == (c + 1) * BANK // P - 1]
MAXU = [(i, c) for i in range(ST_N) for c in range(i * P // BANK + 1)]


def first_col(c, j):
    return max(0, j * P - c * BANK)


def is_diag(c, j):
    return j * P >= c * BANK


def normalise(nc, x, hold):
    with ExitStack() as ctx:
        sb = lambda name, shape, dt=F32: ctx.enter_context(nc.sbuf_tensor(name, shape, dt))
        sem = lambda name: ctx.enter_context(nc.semaphore(name))
        X = sb("n_x", [P, NT, D])
        XN = sb("n_xn", [P, 4, D])
        stats = sb("n_stats", [P, NT, 6])
        scale = sb("n_scale", [P, NT])
        shift = sb("n_shift", [P, NT])
        mean2 = sb("n_mean2", [P, NT])
        diff = sb("n_diff", [P, NT])
        var = sb("n_var", [P, NT])
        std = sb("n_std", [P, NT])
        ident = sb("n_ident", [P, P])
        T = [ctx.enter_context(nc.psum_tensor(f"n_T{i}", [P, KD, 2, P], F32)) for i in range(2)]
        x_in = [sem(f"n_x_in{i}") for i in range(4)]
        id_set = sem("n_id_set")
        step = sem("n_step")
        var_ready = sem("n_var_ready")
        std_ready = sem("n_std_ready")
        xn_ready = sem("n_xn_ready")
        turned = sem("n_turned")
        stored = sem("n_stored")
        block = ctx.enter_context(nc.Block())

        @block.sync
        def _(sp):
            xt = x.rearrange("(t p) d -> p t d", p=P)
            for i in range(4):
                sp.dma_start(X[:, 8 * i:8 * i + 8, :], xt[:, 8 * i:8 * i + 8, :]).then_inc(x_in[i], 16)

        @block.gpsimd
        def _(pool):
            pool.memset(ident[:, :], 0.0).then_inc(id_set, 1)
            pool.wait_ge(id_set, 1)
            pool.affine_select(out=ident[:, :], in_=ident[:, :], compare_op=ALU.not_equal, fill=1.0, base=0,
                               pattern=[[-1, P]], channel_multiplier=1).then_inc(id_set, 1)

        @block.vector
        def _(dve):
            for i in range(4):
                dve.wait_ge(x_in[i], 16)
                with dve.Fori(8 * i, 8 * i + 8) as t:
                    dve.bn_stats(stats[:, bass.ds(t, 1), :].rearrange("p a s -> p (a s)"),
                                 X[:, bass.ds(t, 1), :].rearrange("p a d -> p (a d)")).then_inc(step, 1)
            n = [NT]

            def link(ins):
                n[0] += 1
                ins.then_inc(step, 1)
                dve.wait_ge(step, n[0])

            dve.wait_ge(step, NT)
            moments(dve, link, stats, mean2, diff, var)
            dve.sem_inc(var_ready, 1)
            dve.wait_ge(std_ready, 1)
            link(dve.reciprocal(scale[:, :], std[:, :]))
            link(dve.scalar_tensor_tensor(out=shift[:, :], in0=mean2[:, :], scalar=-0.5, in1=scale[:, :],
                                          op0=ALU.mult, op1=ALU.mult))
            with dve.Fori(0, NT // 4) as g:
                for k in range(4):
                    if k % 2 == 0:
                        dve.wait_ge(turned, g * 2 + k // 2 + 1)
                    dve.tensor_scalar(XN[:, k, :], X[:, bass.ds(g * 4 + k, 1), :].rearrange("p a d -> p (a d)"),
                                      scale[:, bass.ds(g * 4 + k, 1)], shift[:, bass.ds(g * 4 + k, 1)],
                                      ALU.mult, ALU.add).then_inc(xn_ready, 1)

        @block.scalar
        def _(act):
            act.wait_ge(var_ready, 1)
            act.activation(std[:, :], var[:, :], ACT.Sqrt).then_inc(std_ready, 1)
            act.sem_inc(stored, 2)
            with act.Fori(0, NT // 4) as g:
                for k in range(2):
                    act.wait_ge(turned, g * 2 + k + 3)
                    tile = g % (ST_N // 4) * 4 + 2 * k
                    act.activation(hold[:, bass.ds(g // (ST_N // 4), 1), :, bass.ds(tile * P, 2 * P)],
                                   T[k][:, :, :, :].rearrange("p a b q -> p a (b q)"),
                                   ACT.Copy).then_inc(stored, 1)

        @block.tensor
        def _(pe):
            pe.wait_ge(id_set, 2)
            pe.sem_inc(turned, 2)
            with pe.Fori(0, NT // 4) as g:
                for k in range(2):
                    pe.wait_ge(xn_ready, g * 4 + 2 * k + 2)
                    pe.wait_ge(stored, g * 2 + k + 1)
                    for u in range(2):
                        for kt in range(KD):
                            last = pe.transpose(T[k][:, kt, u, :], XN[:, 2 * k + u, kt * P:(kt + 1) * P], ident[:, :])
                    last.then_inc(turned, 1)


def moments(dve, link, stats, mean2, diff, var):
    link(dve.tensor_tensor(mean2[:, :], stats[:, :, 1], stats[:, :, 4], ALU.add))
    link(dve.tensor_tensor(diff[:, :], stats[:, :, 1], stats[:, :, 4], ALU.subtract))
    link(dve.tensor_tensor(var[:, :], stats[:, :, 2], stats[:, :, 5], ALU.add))
    link(dve.scalar_tensor_tensor(out=diff[:, :], in0=diff[:, :], scalar=0.25, in1=diff[:, :],
                                  op0=ALU.mult, op1=ALU.mult))
    link(dve.scalar_tensor_tensor(out=var[:, :], in0=var[:, :], scalar=1.0 / D, in1=diff[:, :],
                                  op0=ALU.mult, op1=ALU.add))
    link(dve.tensor_scalar(var[:, :], var[:, :], EPS, None, ALU.add))


MAXN = [(h, i, c) for early in (True, False) for h in range(2) for i, c in MAXU if (i < BANK // P) == early]
NMAX = len(MAXN)
FILL = {n: [] for n in range(NU)}
for _n, _item in ((0, ("q", 0)), (2, ("k", 0)), (3, ("q", 1)), (4, ("v", 0)), (5, ("k", 1)), (8, ("v", 1))):
    FILL[_n].append(_item)
for _n in range(NMAX):
    FILL[(4, 4, 4, 4, 5, 5, 6, 6, 7, 7, 7, 7, 8, 8, 8, 8, 9, 9, 9, 9, 10, 10, 10, 10)[_n]].append(("max", _n))
FILL[11].append(("turn", 0))
LAG = 2
RING = 5
ADDS = [n for n, (c, j) in enumerate(UNITS) if j > 0]
SUM_SLOT = (6, 0)
COPY_SLOT = (7, 1)
PIECES = 4


def attention_one(nc, hold, w_pair, w_out):
    rows = hold.rearrange("p b k s -> p b (k s)").rearrange("p b (t d) -> p (b t) d", d=D)
    with ExitStack() as ctx:
        sb = lambda name, shape, dt=F32: ctx.enter_context(nc.sbuf_tensor(name, shape, dt))
        ps = lambda name, shape, dt=F32: ctx.enter_context(nc.psum_tensor(name, shape, dt))
        sem = lambda name: ctx.enter_context(nc.semaphore(name))
        xT = sb("a_xT", [P, KD, S])
        W = [sb(f"a_W{i}", [P, KD, 3, P]) for i in range(2)]
        Wo = sb("a_Wo", [P, PAIRS, D])
        QR = [[sb(f"a_QR{i}{h}", [P, S], F32R) for h in range(2)] for i in range(2)]
        KR = [[sb(f"a_KR{i}{h}", [P, S], F32R) for h in range(2)] for i in range(2)]
        QS = [[sb(f"a_QS{i}{h}", [DH1 + 1, S], F32R) for h in range(2)] for i in range(2)]
        KS = [[sb(f"a_KS{i}{h}", [DH1 + 1, S], F32R) for h in range(2)] for i in range(2)]
        V = [[sb(f"a_V{i}{h}", [P, ST_N, DH1]) for h in range(2)] for i in range(2)]
        cat = sb("a_cat", [P, PAIRS, S])
        ring = [[sb(f"a_P{h}{i}", [P, BANK]) for i in range(RING)] for h in range(2)]
        acc = [[sb(f"a_A{h}{c}", [P, BANK]) for c in range(2)] for h in range(2)]
        total = [sb(f"a_total{c}", [P, BANK]) for c in range(2)]
        inv = [sb(f"a_inv{c}", [P, BANK]) for c in range(2)]
        peak = sb("a_peak", [P, 2, ST_N, 2])
        minus = sb("a_minus", [P, 2 * ST_N])
        minusT = sb("a_minusT", [2 * ST_N, P], F32R)
        ident = sb("a_ident", [P, P])
        ones = sb("a_ones", [P, DH1])
        identb = sb("a_identb", [P, P], BF16)
        maskb = sb("a_maskb", [P, P], BF16)
        SC = [ps(f"a_SC{h}", [P, BANK]) for h in range(2)]
        MX = [ps(f"a_MX{i}", [P, BANK]) for i in range(2)]
        O = [ps(f"a_O{c}", [P, BANK]) for c in range(2)]
        PR = [ps(f"a_PR{i}", [P, BANK]) for i in range(2)]

        names = ("consts", "dve_consts", "x_in", "wo_in", "q_ready", "q_copied", "q_split", "k_ready", "k_copied", "k_split",
                 "v_ready", "v_copied", "max_ready", "max_used", "minus_ready", "turn_ready", "turn_copied", "minus_in",
                 "scores_ready", "exp_done", "mask_due", "masked", "pv_done", "sums_ready", "sums_copied", "inv_ready", "out_done",
                 "proj_ready", "proj_copied")
        s = {k: sem(f"a_{k}") for k in names}
        w_in = [sem(f"a_w_in{i}") for i in range(2)]
        added = [sem(f"a_added{h}") for h in range(2)]
        block = ctx.enter_context(nc.Block())

        N2 = 2 * NU
        NA = len(ADDS)

        def buffer(n, h):
            c, j = UNITS[n]
            return acc[h][c] if j == 0 else ring[h][ADDS.index(n) % RING]

        def batches(eng, head, step, tail):
            with eng.Fori(0, B) as b:
                n = b * PAIRS
                head(b)
                step(n, None, None, 0)
                step(n + 1, n, None, 1)
                with eng.Fori(0, PAIRS // 2 - 1) as u:
                    m = n + u * 2
                    step(m + 2, m + 1, m, 0)
                    step(m + 3, m + 2, m + 1, 1)
                step(None, n + PAIRS - 1, n + PAIRS - 2, 0)
                step(None, None, n + PAIRS - 1, 1)
                tail(b)

        def add(eng, n2, n, h):
            c, j = UNITS[n]
            a = first_col(c, j)
            if is_diag(c, j):
                eng.wait_ge(s["masked"], n2 * (2 * ST_N) + 2 * j + h + 1)
            else:
                eng.wait_ge(s["exp_done"], n2 * N2 + 2 * n + h + 3)
            if j == 1:
                eng.wait_ge(s["pv_done"], n2 * N2 + N2 + 2 * (n - 1) + h + 1)
            else:
                eng.wait_ge(added[h], n2 * NA + NA + ADDS.index(n))
            eng.tensor_tensor(acc[h][c][:, a:], acc[h][c][:, a:], buffer(n, h)[:, a:], ALU.add).then_inc(added[h], 1)

        @block.gpsimd
        def _(pool):
            for m, fill in ((ident, 0.0), (identb, 0.0), (maskb, 0.0)):
                pool.memset(m[:, :], fill).then_inc(s["consts"], 1)
            pool.wait_ge(s["consts"], 3)
            for m in (ident, identb):
                pool.affine_select(out=m[:, :], in_=m[:, :], compare_op=ALU.not_equal, fill=1.0, base=0,
                                   pattern=[[-1, P]], channel_multiplier=1).then_inc(s["consts"], 1)
            pool.affine_select(out=maskb[:, :], in_=maskb[:, :], compare_op=ALU.is_ge, fill=NEG, base=0,
                               pattern=[[-1, P]], channel_multiplier=1).then_inc(s["consts"], 1)

            def step(n1, n2, n3, p):
                if n2 is None:
                    return
                for n, (c, j) in enumerate(UNITS):
                    for h in range(2):
                        if is_diag(c, j):
                            a = first_col(c, j)
                            t = buffer(n, h)[:, a:a + P]
                            pool.wait_ge(s["exp_done"], n2 * N2 + 2 * n + h + 3)
                            pool.sem_inc(s["mask_due"], 1)
                            pool.affine_select(out=t, in_=t, compare_op=ALU.is_ge, fill=0.0, base=0, pattern=[[1, P]],
                                               channel_multiplier=-1).then_inc(s["masked"], 1)
                    if n - 1 in ADDS:
                        add(pool, n2, n - 1, 1)
                add(pool, n2, NU - 1, 1)

            pool.sem_inc(added[1], NA)
            batches(pool, lambda b: None, step, lambda b: None)

        @block.sync
        def _(sp):
            sp.dma_start(Wo[:, :, :], w_out).then_inc(s["wo_in"], 16)
            for i in range(2):
                sp.dma_start(W[i][:, :, :, :], w_pair[i]).then_inc(w_in[i], 16)

            def head(b):
                sp.wait_ge(s["v_ready"], b * (2 * PAIRS) + 1)
                sp.dma_start(xT[:, :, :], hold[:, bass.ds(b, 1), :, :].rearrange("p b k s -> p (b k) s")).then_inc(s["x_in"], 16)

            def step(n1, n2, n3, p):
                if n1 is not None:
                    sp.wait_ge(s["turn_copied"], n1 + 2)
                    for h in range(2):
                        sp.dma_start(QS[p][h][DH1:DH1 + 1, :].bitcast(F32),
                                     minusT[ST_N * h:ST_N * (h + 1), :].bitcast(F32)).then_inc(s["minus_in"], 16)
                    sp.dma_start(W[p][:, :, :, :], w_pair[bass.ds((n1 + 2) % PAIRS, 1)].rearrange(
                        "a p k w c -> p (a k) w c")).then_inc(w_in[p], 16)

            batches(sp, head, step, lambda b: None)
            for i in range(2):
                sp.wait_ge(w_in[i], 16 * (B * PAIRS // 2 + 1))

        @block.scalar
        def _(act):
            act.sem_inc(s["exp_done"], 2)
            act.sem_inc(s["v_copied"], 1)

            def feed(n1, p, what, c):
                cols = slice(c * BANK, (c + 1) * BANK)
                if what == "q":
                    act.wait_ge(s["q_ready"], n1 * 2 + c + 1)
                    for h in range(2):
                        for half in (h, 1 - h):
                            act.activation(QR[p][h][DH1 * half:DH1 * (half + 1), cols],
                                           PR[c][DH1 * h:DH1 * (h + 1), :], ACT.Copy).then_inc(s["q_copied"], 1)
                elif what == "k":
                    act.wait_ge(s["k_ready"], n1 * 2 + c + 1)
                    for h in range(2):
                        for dst in (KR[p][h][DH1 * h:DH1 * (h + 1), cols], KS[p][h][0:DH1, cols]):
                            act.activation(dst, PR[c][DH1 * h:DH1 * (h + 1), :], ACT.Copy).then_inc(s["k_copied"], 1)
                elif what == "v":
                    act.wait_ge(s["v_ready"], n1 * 2 + c + 2)
                    for h in range(2):
                        act.activation(V[p][h][:, 4 * c:4 * c + 4, :],
                                       PR[c][:, :].rearrange("p (t w) -> p t w", t=4)[:, :, DH1 * h:DH1 * (h + 1)],
                                       ACT.Copy).then_inc(s["v_copied"], 1)

            def step(n1, n2, n3, p):
                for n, (ch, j) in enumerate(UNITS):
                    if n == 0 and n1 is not None:
                        feed(n1, p, *FILL[0][0])
                    if n2 is not None:
                        a = first_col(ch, j)
                        for h in range(2):
                            act.wait_ge(s["scores_ready"], n2 * N2 + 2 * n + h + 1)
                            if j == 0:
                                act.wait_ge(s["sums_ready"], n2 * 2 + ch + 1)
                            else:
                                m = ADDS.index(n) - RING
                                k = 2 * ADDS[m] + h + (N2 if m >= 0 else 0)
                                act.wait_ge(s["pv_done"], n2 * N2 + k + 1)
                                act.wait_ge(added[h], n2 * NA + NA + m + 1)
                            act.activation(buffer(n, h)[:, a:], SC[h][:, a:], ACT.Exp, scale=DH1 ** -0.5).then_inc(s["exp_done"], 1)
                    if n1 is not None and n > 0:
                        for what, c in FILL[n]:
                            feed(n1, p, what, c)
                    for c, m in ((0, n2), (1, n3)):
                        if m is not None and n == COPY_SLOT[c]:
                            act.wait_ge(s["sums_ready"], m * 2 + c + 3)
                            act.wait_ge(s["inv_ready"], (m * 2 + c + 1) * PIECES)
                            act.activation(total[c][:, :], PR[1][:, :], ACT.Copy).then_inc(s["sums_copied"], 1)

            def tail(b):
                for i in range(ST_N):
                    act.wait_ge(s["proj_ready"], b * ST_N + i + 2)
                    act.activation(rows[:, bass.ds(b * ST_N + i, 1), :].rearrange("p a d -> p (a d)"),
                                   PR[i % 2][:, 0:D], ACT.Copy).then_inc(s["proj_copied"], 1)

            act.sem_inc(s["proj_copied"], 2)
            batches(act, lambda b: None, step, tail)

        @block.vector
        def _(dve):
            dve.memset(peak[:, :, :, :], 3 * NEG).then_inc(s["dve_consts"], 1)
            dve.memset(ones[:, :], 1.0).then_inc(s["dve_consts"], 1)
            dve.memset(inv[0][DH1:DH1 + 1, :], 1.0).then_inc(s["dve_consts"], 1)
            dve.wait_ge(s["dve_consts"], 3)
            for i in range(2):
                for h in range(2):
                    for c in range(2):
                        dve.tensor_copy(KS[i][h][DH1:DH1 + 1, c * BANK:(c + 1) * BANK], inv[0][DH1:DH1 + 1, :]).then_inc(s["dve_consts"], 1)
            dve.wait_ge(s["dve_consts"], 11)
            dve.sem_inc(s["max_used"], 2)
            dve.sem_inc(s["minus_in"], 1)
            dve.sem_inc(s["turn_copied"], 1)
            dve.sem_inc(s["out_done"], 4)
            dve.sem_inc(added[0], NA)
            dve.sem_inc(s["sums_copied"], 4)
            dve.sem_inc(s["inv_ready"], 2 * PIECES)

            def inverse(n, c, i):
                if i == 0:
                    dve.wait_ge(s["sums_copied"], n * 2 + c + 5)
                    dve.wait_ge(s["out_done"], n * 2 + c + 3)
                cols = slice(i * BANK // PIECES, (i + 1) * BANK // PIECES)
                dve.reciprocal(inv[c][:, cols], total[c][:, cols]).then_inc(s["inv_ready"], 1)

            def output(n, c):
                dve.wait_ge(s["inv_ready"], (n * 2 + c + 3) * PIECES)
                dve.tensor_tensor(cat[:, bass.ds(n % PAIRS, 1), c * BANK:(c + 1) * BANK].rearrange("p a s -> p (a s)"), O[c][:, :],
                                  inv[c][:, :], ALU.mult).then_inc(s["out_done"], 1)

            def reduce_max(n1, c):
                h, i, ch = MAXN[c]
                w = min(BANK, (i + 1) * P - ch * BANK)
                dve.wait_ge(s["max_ready"], n1 * NMAX + c + 1)
                dve.tensor_reduce(peak[:, h, i, ch:ch + 1], MX[c % 2][:, 0:w], AX.X, ALU.max).then_inc(s["max_used"], 1)
                if c == NMAX - 1:
                    dve.wait_ge(s["max_used"], n1 * NMAX + NMAX + 2)
                    dve.tensor_reduce(minus[:, :].rearrange("p (h i) -> p h i", h=2), peak[:, :, :, :],
                                      AX.X, ALU.max, negate=True).then_inc(s["minus_ready"], 1)

            def split(n1, p, what, c, h):
                own, cols = slice(DH1 * h, DH1 * (h + 1)), slice(c * BANK, (c + 1) * BANK)
                if what == "q":
                    dve.wait_ge(s["q_copied"], n1 * 8 + 4 * c + 4)
                    dve.tensor_tensor(QS[p][h][0:DH1, cols], PR[c][own, :], QR[p][h][own, cols],
                                      ALU.subtract).then_inc(s["q_split"], 1)
                else:
                    dve.wait_ge(s["k_copied"], n1 * 8 + 4 * c + 4)
                    dve.tensor_tensor(KR[p][h][DH1 * (1 - h):DH1 * (2 - h), cols], PR[c][own, :],
                                      KR[p][h][own, cols], ALU.subtract).then_inc(s["k_split"], 1)

            def turn(n1):
                dve.wait_ge(s["turn_ready"], n1 + 1)
                dve.wait_ge(s["minus_in"], n1 * 32 + 1)
                dve.tensor_copy(minusT[:, :], PR[0][0:2 * ST_N, 0:P]).then_inc(s["turn_copied"], 1)

            def step(n1, n2, n3, p):
                if n3 is not None:
                    add(dve, n3, NU - 1, 0)
                for n in range(NU):
                    maxima = [c for what, c in FILL[n] if n1 is not None and what == "max"]

                    def one_max():
                        if maxima:
                            reduce_max(n1, maxima.pop(0))

                    one_max()
                    if n1 is not None:
                        for what, c in (FILL[0] if n == 0 else []) + (FILL[n - 1] if n > 1 else []):
                            if what in "qk":
                                for h in range(2):
                                    split(n1, p, what, c, h)
                                    one_max()
                    if n2 is not None and n - 1 in ADDS:
                        one_max()
                        add(dve, n2, n - 1, 0)
                    one_max()
                    for c, m in ((0, n2), (1, n3)):
                        i = n - COPY_SLOT[c]
                        if m is not None and 0 <= i < PIECES:
                            inverse(m, c, i)
                            one_max()
                            if i == PIECES - 1:
                                output(m, c)
                    while maxima:
                        one_max()
                    if n1 is not None and ("turn", 0) in FILL[n]:
                        turn(n1)

            batches(dve, lambda b: dve.wait_ge(s["proj_ready"], b * ST_N + 1), step, lambda b: None)

        @block.tensor
        def _(pe):
            pe.wait_ge(s["consts"], 6)
            pe.wait_ge(s["dve_consts"], 11)
            pe.wait_ge(s["wo_in"], 16)
            pe.sem_inc(s["pv_done"], N2)
            pe.sem_inc(s["sums_ready"], 2)
            pe.sem_inc(s["v_ready"], 1)
            pe.sem_inc(s["proj_ready"], 1)

            def scores(n2, p, n, h):
                c, j = UNITS[n]
                a = first_col(c, j)
                keys, queries = slice(j * P, (j + 1) * P), slice(c * BANK + a, (c + 1) * BANK)
                if n == 0:
                    pe.wait_ge(s["minus_in"], n2 * 32 + 33)
                pe.wait_ge(s["exp_done"], n2 * N2 + 2 * n + h + 1)
                pe.matmul(SC[h][:, a:], KR[p][h][:, keys], QR[p][h][:, queries], start=True, stop=False)
                pe.matmul(SC[h][:, a:], KS[p][h][:, keys], QS[p][h][:, queries], start=False,
                          stop=True).then_inc(s["scores_ready"], 1)

            def output(n2, p, n):
                c, j = UNITS[n]
                a = first_col(c, j)
                if j == 0:
                    pe.wait_ge(s["out_done"], n2 * 2 + c + 3)
                pe.wait_ge(s["exp_done"], n2 * N2 + 2 * n + 4)
                if is_diag(c, j):
                    pe.wait_ge(s["masked"], n2 * (2 * ST_N) + 2 * j + 2)
                for h in range(2):
                    pe.matmul(O[c][DH1 * h:DH1 * (h + 1), a:], V[p][h][:, j, :], buffer(n, h)[:, a:], start=(j == 0),
                              stop=(n in LAST)).then_inc(s["pv_done"], 1)

            def sums(n2, c):
                for h in range(2):
                    pe.wait_ge(added[h], n2 * NA + NA + ADDS.index(LAST[c]) + 1)
                pe.wait_ge(s["sums_copied"], n2 * 2 + c + 4)
                for h in range(2):
                    last = pe.matmul(PR[1][DH1 * h:DH1 * (h + 1), :], ones[:, :], acc[h][c][:, :], start=True, stop=True)
                last.then_inc(s["sums_ready"], 1)

            def fill(n1, p, what, c):
                if what in "qk":
                    if (what, c) == ("q", 0):
                        pe.wait_ge(w_in[p], (n1 - p) * 8 + 16)
                        pe.wait_ge(s["turn_copied"], n1 + 1)
                    elif (what, c) == ("q", 1):
                        pe.wait_ge(s["v_copied"], n1 * 4 + 1)
                        pe.wait_ge(s["sums_copied"], n1 * 2 + 2)
                    else:
                        pe.wait_ge(s["q_split"], n1 * 4 + 2 * c + 2)
                        pe.wait_ge(s["q_copied"], n1 * 8 + 4 * c + 4)
                    for kt in range(KD):
                        last = pe.matmul(PR[c][:, :], W[p][:, kt, "qk".index(what), :], xT[:, kt, c * BANK:(c + 1) * BANK],
                                         start=(kt == 0), stop=(kt == KD - 1))
                    last.then_inc(s["q_ready"] if what == "q" else s["k_ready"], 1)
                elif what == "v":
                    pe.wait_ge(s["k_split"], n1 * 4 + 2 * c + 2)
                    pe.wait_ge(s["k_copied"], n1 * 8 + 4 * c + 4)
                    if c == 1:
                        pe.wait_ge(s["sums_copied"], n1 * 2 + 3)
                    for t in range(4):
                        for kt in range(KD):
                            last = pe.matmul(PR[c][:, t * P:(t + 1) * P], xT[:, kt, (4 * c + t) * P:(4 * c + t + 1) * P],
                                             W[p][:, kt, 2, :], start=(kt == 0), stop=(kt == KD - 1))
                    last.then_inc(s["v_ready"], 1)
                elif what == "max":
                    h, i, ch = MAXN[c]
                    w = min(BANK, (i + 1) * P - ch * BANK)
                    diag = ch == i * P // BANK
                    own = slice(DH1 * h, DH1 * (h + 1))
                    if i * P // BANK == 1 or c == 0:
                        pe.wait_ge(s["q_copied"], n1 * 8 + 4 * (i * P // BANK) + 4)
                        pe.wait_ge(s["k_copied"], n1 * 8 + 4 * (i * P // BANK) + 4)
                    pe.wait_ge(s["max_used"], n1 * NMAX + c + 1)
                    last = pe.matmul(MX[c % 2][:, 0:w], QR[p][h][own, i * P:(i + 1) * P], KR[p][h][own, ch * BANK:ch * BANK + w],
                                     start=True, stop=not diag)
                    if diag:
                        last = pe.matmul(MX[c % 2][:, w - P:w], identb[:, :], maskb[:, :], start=False, stop=True)
                    last.then_inc(s["max_ready"], 1)
                elif what == "turn":
                    pe.wait_ge(s["minus_ready"], n1 + 1)
                    pe.wait_ge(s["v_copied"], n1 * 4 + 3)
                    pe.transpose(PR[0][0:2 * ST_N, 0:P], minus[:, :], ident[:, :]).then_inc(s["turn_ready"], 1)

            def step(n1, n2, n3, p):
                for n in range(NU):
                    if n3 is not None and n == 0:
                        output(n3, p, NU - 2)
                    if n1 is not None and n == 0:
                        fill(n1, p, *FILL[0][0])
                    if n3 is not None and n == 0:
                        output(n3, p, NU - 1)
                    maxima = [f for f in FILL[n] if n1 is not None and f[0] == "max"]
                    others = [f for f in FILL[n] if n1 is not None and n > 0 and f[0] != "max"]

                    def one_max():
                        if maxima:
                            fill(n1, p, *maxima.pop(0))

                    for h in range(2):
                        if n2 is not None:
                            scores(n2, 1 - p, n, h)
                        one_max()
                    for f in others:
                        fill(n1, p, *f)
                    one_max()
                    if n2 is not None and n >= LAG:
                        output(n2, 1 - p, n - LAG)
                    one_max()
                    while maxima:
                        one_max()
                    if n3 is not None and n == SUM_SLOT[1]:
                        if n2 is not None:
                            pe.wait_ge(s["v_copied"], n3 * 4 + 9)
                        sums(n3, 1)
                    if n2 is not None and n == SUM_SLOT[0]:
                        if n1 is not None:
                            pe.wait_ge(s["k_copied"], n1 * 8 + 8)
                            pe.wait_ge(s["k_split"], n1 * 4 + 4)
                        sums(n2, 0)

            def tail(b):
                pe.wait_ge(s["out_done"], b * (2 * PAIRS) + 2 * PAIRS + 4)
                pe.wait_ge(s["turn_copied"], b * PAIRS + PAIRS + 1)
                pe.wait_ge(s["v_copied"], b * (4 * PAIRS) + 4 * PAIRS + 1)
                for i in range(ST_N):
                    pe.wait_ge(s["proj_copied"], b * ST_N + i + 1)
                    for p in range(PAIRS):
                        last = pe.matmul(PR[i % 2][:, 0:D], cat[:, p, i * P:(i + 1) * P], Wo[:, p, :],
                                         start=(p == 0), stop=(p == PAIRS - 1))
                    last.then_inc(s["proj_ready"], 1)

            def head(b):
                pe.wait_ge(s["x_in"], b * 16 + 16)
                pe.wait_ge(s["proj_copied"], b * ST_N + 2)

            batches(pe, head, step, tail)


H2, KV2, DH2 = 16, 4, 16
GROUP = H2 // KV2
QK2 = (H2 + KV2) * DH2
QKV2 = QK2 + KV2 * DH2
Q_PARTS = (0, 0, 0, 1, 1, 2)
K_PARTS = (0, 1, 2, 0, 1, 0)
PARTS = len(Q_PARTS)
STACK = PARTS * DH2
HEADS2 = H2 + KV2


def counted(eng, sem, base):
    n = [0]

    def link(ins):
        n[0] += 1
        ins.then_inc(sem, 1)
        eng.wait_ge(sem, base + n[0])

    return link


def project_two(nc, x, hold, w_qkv, ln1, cos2, sin2, norm_z, shift_z, V2, stack_dram):
    rows = hold.rearrange("p b k s -> p (b k s)").rearrange("p (t d) -> p t d", d=D)
    with ExitStack() as ctx:
        sb = lambda name, shape, dt=F32: ctx.enter_context(nc.sbuf_tensor(name, shape, dt))
        ps = lambda name, shape, dt=F32: ctx.enter_context(nc.psum_tensor(name, shape, dt))
        sem = lambda name: ctx.enter_context(nc.semaphore(name))
        X = sb("p_x", [P, NT, D])
        Y = sb("p_y", [P, 4, D])
        Wq = sb("p_w", [P, KD, QKV2])
        ln = sb("p_ln", [P, KD])
        cos = sb("p_cos", [P, ST_N, DH2])
        sin = sb("p_sin", [P, ST_N, DH2])
        stats = sb("p_stats", [P, NT, 6])
        small = {k: sb(f"p_{k}", [P, NT]) for k in ("mean2", "diff", "var", "std", "scale", "shift", "ratio", "hscale", "hshift")}
        ident = sb("p_ident", [P, P])
        HN = [sb(f"p_hn{i}", [P, D]) for i in range(2)]
        hT = [sb(f"p_hT{i}", [P, KD, P]) for i in range(2)]
        rot = [sb(f"p_rot{i}", [P, QK2]) for i in range(2)]
        crs = [sb(f"p_crs{i}", [P, QK2]) for i in range(2)]
        stk = [sb(f"p_stk{i}", [P, HEADS2, PARTS, DH2], BF16) for i in range(2)]
        T = [ps(f"p_T{i}", [P, BANK]) for i in range(2)]
        QKV = [ps(f"p_QKV{i}", [P, BANK]) for i in range(2)]
        names = ("x_in", "w_in", "id_set", "step", "ones_set", "var_ready", "std_ready", "y_ready", "y_used", "hn_ready",
                 "turned", "hT_ready", "qkv_ready", "v_copied", "rotated", "first_set", "rest", "second_set",
                 "third_set")
        s = {k: sem(f"p_{k}") for k in names}
        x_in = [sem(f"p_x_in{i}") for i in range(4)]
        stored = [sem(f"p_stored{i}") for i in range(2)]
        block = ctx.enter_context(nc.Block())

        @block.sync
        def _(sp):
            xt = x.rearrange("(t p) d -> p t d", p=P)
            for i in range(4):
                sp.dma_start(X[:, 8 * i:8 * i + 8, :], xt[:, 8 * i:8 * i + 8, :]).then_inc(x_in[i], 16)
            for dst, src in ((Wq, w_qkv), (cos, cos2), (sin, sin2)):
                sp.dma_start(dst[:, :, :], src).then_inc(s["w_in"], 16)
            sp.dma_start(ln[:, :], ln1).then_inc(s["w_in"], 16)
            with sp.Fori(0, NT // 2) as g:
                for i in range(2):
                    sp.wait_ge(s["third_set"], g * 4 + 2 * i + 5)
                    sp.dma_start(stack_dram[bass.ds(g * 2 + i, 1), :, :].rearrange("t p w -> (t p) w"),
                                 stk[i][:, :, :, :].rearrange("p h a d -> p (h a d)")).then_inc(stored[i], 16)
            for i in range(2):
                sp.wait_ge(stored[i], 16 * (NT // 2) + 1)

        @block.gpsimd
        def _(pool):
            pool.memset(ident[:, :], 0.0).then_inc(s["id_set"], 1)
            pool.wait_ge(s["id_set"], 1)
            pool.affine_select(out=ident[:, :], in_=ident[:, :], compare_op=ALU.not_equal, fill=1.0, base=0,
                               pattern=[[-1, P]], channel_multiplier=1).then_inc(s["id_set"], 1)
            pool.memset(V2, 1.0).then_inc(s["ones_set"], 1)

        def tile_of(t, n, k):
            return t[:, bass.ds(n, 1), :].rearrange("p a d -> p (a d)")

        @block.vector
        def _(dve):
            sm = {k: v[:, :] for k, v in small.items()}
            with dve.Fori(0, NT) as t:
                dve.bn_stats(tile_of(stats, t, 0), tile_of(rows, t, 0)).then_inc(s["step"], 1)
            dve.wait_ge(s["step"], NT)
            link = counted(dve, s["step"], NT)
            moments(dve, link, stats, small["mean2"], small["diff"], small["var"])
            dve.sem_inc(s["var_ready"], 1)
            dve.wait_ge(s["std_ready"], 1)
            link(dve.reciprocal(sm["scale"], sm["std"]))
            link(dve.scalar_tensor_tensor(out=sm["shift"], in0=sm["mean2"], scalar=-0.5, in1=sm["scale"],
                                          op0=ALU.mult, op1=ALU.mult))
            dve.sem_inc(s["var_ready"], 1)
            dve.sem_inc(s["y_used"], 4)
            base = NT + 8
            for i in range(4):
                dve.wait_ge(x_in[i], 16)
                with dve.Fori(2 * i, 2 * i + 2) as f:
                    t = f * 4
                    for k in range(4):
                        dve.wait_ge(s["y_ready"], t + k + 1)
                        dve.tensor_tensor(tile_of(rows, t + k, 0), Y[:, k, :], tile_of(X, t + k, 0),
                                          ALU.add).then_inc(s["y_used"], 1)
                    for k in range(4):
                        dve.wait_ge(s["y_used"], t + k + 5)
                        dve.bn_stats(tile_of(stats, t + k, 0), tile_of(rows, t + k, 0)).then_inc(s["step"], 1)
            dve.wait_ge(s["step"], base + NT)
            link = counted(dve, s["step"], base + NT)
            moments(dve, link, stats, small["mean2"], small["diff"], small["var"])
            dve.sem_inc(s["var_ready"], 1)
            dve.wait_ge(s["std_ready"], 2)
            link(dve.reciprocal(norm_z, sm["std"]))
            link(dve.scalar_tensor_tensor(out=shift_z, in0=sm["mean2"], scalar=-0.5, in1=norm_z,
                                          op0=ALU.mult, op1=ALU.mult))
            link(dve.tensor_scalar(sm["diff"], sm["var"], -EPS, None, ALU.add))
            link(dve.tensor_tensor(sm["diff"], sm["diff"], norm_z, ALU.mult))
            link(dve.tensor_tensor(sm["diff"], sm["diff"], norm_z, ALU.mult))
            link(dve.tensor_scalar(sm["var"], sm["diff"], EPS, None, ALU.add))
            dve.sem_inc(s["var_ready"], 1)
            dve.wait_ge(s["std_ready"], 3)
            link(dve.reciprocal(sm["ratio"], sm["std"]))
            link(dve.tensor_tensor(sm["hscale"], norm_z, sm["ratio"], ALU.mult))
            link(dve.tensor_tensor(sm["hshift"], shift_z, sm["ratio"], ALU.mult))
            dve.wait_ge(s["w_in"], 64)
            dve.wait_ge(s["ones_set"], 1)
            dve.sem_inc(stored[0], 1)
            dve.sem_inc(stored[1], 1)
            dve.sem_inc(s["rotated"], 2)

            def narrow(t, i):
                dve.tensor_scalar(HN[i][:, :], tile_of(rows, t, 0),
                                  small["hscale"][:, bass.ds(t, 1)], small["hshift"][:, bass.ds(t, 1)],
                                  ALU.mult, ALU.add).then_inc(s["hn_ready"], 1)

            def body(g, more):
                if more:
                    for i in range(2):
                        dve.wait_ge(s["turned"], g * 2 + i + 3)
                        narrow(g * 2 + (2 + i), i)
                for i in range(2):
                    t = g * 2 + i
                    dve.wait_ge(s["v_copied"], t + 3)
                    C = cos[:, bass.ds(t % ST_N, 1), :].to_broadcast([P, HEADS2, DH2])
                    qk = QKV[i][:, 0:QK2].rearrange("p (h d) -> p h d", d=DH2)
                    X4 = crs[i][:, :].rearrange("p (h d) -> p h d", d=DH2)
                    half = DH2 // 2
                    dve.wait_ge(s["third_set"], t * 2 + 1)
                    dve.tensor_tensor(rot[i][:, :].rearrange("p (h d) -> p h d", d=DH2), qk, C, ALU.mult).then_inc(s["rest"], 1)
                    for a in range(2):
                        dve.tensor_tensor(X4[:, :, a * half:(a + 1) * half], qk[:, :, (1 - a) * half:(2 - a) * half],
                                          sin[:, bass.ds(t % ST_N, 1), a * half:(a + 1) * half].to_broadcast([P, HEADS2, half]),
                                          ALU.mult).then_inc(s["rest"], 1)
                for i in range(2):
                    t = g * 2 + i
                    dve.wait_ge(s["rest"], g * 10 + 3 * i + 3)
                    dve.tensor_tensor(rot[i][:, :], rot[i][:, :], crs[i][:, :], ALU.add).then_inc(s["rotated"], 1)
                for i in range(2):
                    t = g * 2 + i
                    dve.wait_ge(s["first_set"], t * 3 + 3)
                    r = rot[i][:, :].rearrange("p (h d) -> p h d", d=DH2)
                    dve.tensor_tensor(r[:, 0:H2, :], r[:, 0:H2, :], stk[i][:, 0:H2, Q_PARTS.index(0), :], ALU.subtract).then_inc(s["rest"], 1)
                    dve.tensor_tensor(r[:, H2:, :], r[:, H2:, :], stk[i][:, H2:, K_PARTS.index(0), :], ALU.subtract).then_inc(s["rest"], 1)
                for i in range(2):
                    t = g * 2 + i
                    dve.wait_ge(s["second_set"], t * 2 + 2)
                    r = rot[i][:, :].rearrange("p (h d) -> p h d", d=DH2)
                    for lo, hi, parts in ((0, H2, Q_PARTS), (H2, HEADS2, K_PARTS)):
                        dve.tensor_tensor(stk[i][:, lo:hi, parts.index(2), :], r[:, lo:hi, :],
                                          stk[i][:, lo:hi, parts.index(1), :], ALU.subtract).then_inc(s["third_set"], 1)

            for i in range(2):
                narrow(i, i)
            with dve.Fori(0, NT // 2 - 1) as g:
                body(g, True)
            body(NT // 2 - 1, False)

        @block.scalar
        def _(act):
            act.wait_ge(s["var_ready"], 1)
            act.activation(small["std"][:, :], small["var"][:, :], ACT.Sqrt).then_inc(s["std_ready"], 1)
            act.wait_ge(s["var_ready"], 2)
            with act.Fori(0, NT // 4) as f:
                t = f * 4
                for k in range(4):
                    act.wait_ge(s["y_used"], t + k + 1)
                    act.activation(Y[:, k, :], tile_of(rows, t + k, 0), ACT.Identity,
                                   scale=small["scale"][:, bass.ds(t + k, 1)],
                                   bias=small["shift"][:, bass.ds(t + k, 1)]).then_inc(s["y_ready"], 1)
            for n in range(2):
                act.wait_ge(s["var_ready"], 3 + n)
                act.activation(small["std"][:, :], small["var"][:, :], ACT.Sqrt).then_inc(s["std_ready"], 1)
            act.wait_ge(s["w_in"], 64)
            act.wait_ge(s["ones_set"], 1)
            act.sem_inc(s["v_copied"], 2)
            with act.Fori(0, NT // 2) as g:
                for i in range(2):
                    t = g * 2 + i
                    act.wait_ge(s["turned"], t + 3)
                    for kt in range(KD):
                        act.activation(hT[i][:, kt, :], T[i][:, kt * P:(kt + 1) * P], ACT.Copy,
                                       scale=ln[:, kt:kt + 1]).then_inc(s["hT_ready"], 1)
                for i in range(2):
                    t = g * 2 + i
                    act.wait_ge(s["qkv_ready"], t + 1)
                    act.activation(V2[:, bass.ds(t // ST_N, 1), :, bass.ds(t % ST_N, 1), 0:DH2].rearrange("p a g b d -> p (a g) (b d)"),
                                   QKV[i][:, QK2:].rearrange("p (g d) -> p g d", d=DH2)[:, 0:KV2, :], ACT.Copy).then_inc(s["v_copied"], 1)
                for i in range(2):
                    t = g * 2 + i
                    act.wait_ge(s["rotated"], t + 3)
                    act.wait_ge(stored[i], g * 16 + 1)
                    r = rot[i][:, :].rearrange("p (h a d) -> p h a d", a=1, d=DH2)
                    act.activation(stk[i][:, 0:H2, 0:3, :], r[:, 0:H2].to_broadcast([P, H2, 3, DH2]), ACT.Copy).then_inc(s["first_set"], 1)
                    act.activation(stk[i][:, H2:, 0:4:3, :], r[:, H2:].to_broadcast([P, KV2, 2, DH2]), ACT.Copy).then_inc(s["first_set"], 1)
                    act.activation(stk[i][:, H2:, 5:6, :], r[:, H2:], ACT.Copy).then_inc(s["first_set"], 1)
                for i in range(2):
                    t = g * 2 + i
                    act.wait_ge(s["rest"], g * 10 + 6 + 2 * i + 2)
                    r = rot[i][:, :].rearrange("p (h a d) -> p h a d", a=1, d=DH2)
                    act.activation(stk[i][:, 0:H2, 3:5, :], r[:, 0:H2].to_broadcast([P, H2, 2, DH2]), ACT.Copy).then_inc(s["second_set"], 1)
                    act.activation(stk[i][:, H2:, 1:5:3, :], r[:, H2:].to_broadcast([P, KV2, 2, DH2]), ACT.Copy).then_inc(s["second_set"], 1)

        @block.tensor
        def _(pe):
            pe.wait_ge(s["id_set"], 2)
            pe.wait_ge(s["w_in"], 64)
            pe.sem_inc(s["turned"], 2)
            pe.sem_inc(s["third_set"], 3)
            pe.sem_inc(s["hT_ready"], 4)
            with pe.Fori(0, NT // 2) as g:
                for i in range(2):
                    t = g * 2 + i
                    pe.wait_ge(s["hn_ready"], t + 1)
                    pe.wait_ge(s["hT_ready"], t * 2 + 2)
                    for kt in range(KD):
                        last = pe.transpose(T[i][:, kt * P:(kt + 1) * P], HN[i][:, kt * P:(kt + 1) * P], ident[:, :])
                    last.then_inc(s["turned"], 1)
                for i in range(2):
                    t = g * 2 + i
                    pe.wait_ge(s["hT_ready"], t * 2 + 6)
                    pe.wait_ge(s["rotated"], t + 1)
                    pe.wait_ge(s["v_copied"], t + 1)
                    for kt in range(KD):
                        last = pe.matmul(QKV[i][:, 0:QKV2], hT[i][:, kt, :], Wq[:, kt, :], start=(kt == 0), stop=(kt == KD - 1))
                    last.then_inc(s["qkv_ready"], 1)


STEPS2 = B * KV2
UNITS2 = [(c, j, h) for c, j in UNITS for h in range(GROUP)]
NU2 = len(UNITS2)
MAX2 = [(h, i, c) for h in range(GROUP) for i, c in MAXU]
LAG2 = 10
RING2 = 16
STACK_SLOTS = (0, 2, 8, 17, 26)
TURN_SLOT, OUT_SLOTS = NU2 - 5, (16 + LAG2 + 2, LAG2 + 4)
FILL2 = {k: [] for k in range(NU2)}
for _n, _k in enumerate(STACK_SLOTS):
    FILL2[_k].append(("stack", _n))
for _n in range(NU2):
    FILL2[3 + _n * (TURN_SLOT - 5) // NU2].append(("max", _n))


def attention_two(nc, stack_dram, V2, A2):
    with ExitStack() as ctx:
        sb = lambda name, shape, dt=F32: ctx.enter_context(nc.sbuf_tensor(name, shape, dt))
        ps = lambda name, shape, dt=F32: ctx.enter_context(nc.psum_tensor(name, shape, dt))
        sem = lambda name: ctx.enter_context(nc.semaphore(name))
        stk = [sb(f"b_stk{i}", [P, ST_N, GROUP + 1, STACK], BF16) for i in range(2)]
        V = [sb(f"b_V{i}", [P, ST_N, 2 * DH2]) for i in range(2)]
        Q = [sb(f"b_Q{i}", [STACK + 2, GROUP, S], BF16) for i in range(2)]
        K = [sb(f"b_K{i}", [STACK + 2, S], BF16) for i in range(2)]
        probs = [sb(f"b_P{i}", [P, BANK]) for i in range(RING2)]
        OT = [sb(f"b_OT{i}", [P, BANK]) for i in range(2)]
        inv = sb("b_inv", [P, 2, GROUP, GROUP])
        peak = sb("b_peak", [P, GROUP, ST_N, 2])
        minus = sb("b_minus", [P, GROUP * ST_N])
        hi = sb("b_hi", [GROUP * ST_N, P], BF16)
        lo = sb("b_lo", [GROUP * ST_N, P], BF16)
        ident = sb("b_ident", [P, P])
        identb = sb("b_identb", [P, P], BF16)
        maskb = sb("b_maskb", [P, P], BF16)
        SC = [ps(f"b_SC{i}", [P, BANK]) for i in range(2)]
        MX = [ps(f"b_MX{i}", [P, BANK]) for i in range(2)]
        O = [ps(f"b_O{i}", [P, BANK]) for i in range(2)]
        TR = ps("b_TR", [STACK, S], BF16)
        SM = ps("b_SM", [P, BANK])
        names = ("consts", "dve_consts", "stack_ready", "stack_copied", "max_ready", "max_used", "minus_ready",
                 "turn_ready", "turn_copied", "minus_in", "scores_ready", "exp_done", "masked", "pv_done",
                 "OT_copied", "OT_ready", "inv_ready", "A2_done", "v_in", "mask_due")
        s = {k: sem(f"b_{k}") for k in names}
        loaded = [sem(f"b_loaded{i}") for i in range(2)]
        block = ctx.enter_context(nc.Block())

        def run(eng, step):
            step(0, None, None, 0)
            step(1, 0, None, 1)
            with eng.Fori(0, STEPS2 // 2 - 1) as u:
                step(u * 2 + 2, u * 2 + 1, u * 2, 0)
                step(u * 2 + 3, u * 2 + 2, u * 2 + 1, 1)
            step(None, STEPS2 - 1, STEPS2 - 2, 0)
            step(None, None, STEPS2 - 1, 1)

        @block.gpsimd
        def _(pool):
            for m in (ident, identb, maskb):
                pool.memset(m[:, :], 0.0).then_inc(s["consts"], 1)
            pool.wait_ge(s["consts"], 3)
            for m in (ident, identb):
                pool.affine_select(out=m[:, :], in_=m[:, :], compare_op=ALU.not_equal, fill=1.0, base=0,
                                   pattern=[[-1, P]], channel_multiplier=1).then_inc(s["consts"], 1)
            pool.affine_select(out=maskb[:, :], in_=maskb[:, :], compare_op=ALU.is_ge, fill=NEG, base=0,
                               pattern=[[-1, P]], channel_multiplier=1).then_inc(s["consts"], 1)

            def step(n1, n2, n3, p):
                if n2 is None:
                    return
                for k, (c, j, h) in enumerate(UNITS2):
                    if is_diag(c, j):
                        a = first_col(c, j)
                        pool.wait_ge(s["exp_done"], n2 * NU2 + k + 3)
                        pool.sem_inc(s["mask_due"], 1)
                        pool.affine_select(out=probs[k % RING2][:, a:a + P], in_=probs[k % RING2][:, a:a + P],
                                           compare_op=ALU.is_ge, fill=0.0, base=0, pattern=[[1, P]],
                                           channel_multiplier=-1).then_inc(s["masked"], 1)

            run(pool, step)

        @block.sync
        def _(sp):
            def load(n, p):
                b, g = n // KV2, n % KV2
                src = stack_dram.rearrange("(b t) p (h w) -> b p t h w", b=B, w=STACK)[bass.ds(b, 1)].rearrange("b p t h w -> (b p) t h w")
                for t in range(ST_N):
                    sp.dma_start(stk[p][:, t, 0:GROUP, :], src[:, t, bass.ds(g * GROUP, GROUP), :]).then_inc(loaded[p], 16)
                sp.dma_start(stk[p][:, :, GROUP:, :].rearrange("p t h w -> p t (h w)"), src[:, :, bass.ds(g + H2, 1), :].rearrange("p t h w -> p t (h w)")).then_inc(loaded[p], 16)

            load(0, 0)

            def step(n1, n2, n3, p):
                if n1 is not None:
                    sp.wait_ge(s["stack_ready"], n1 * (GROUP + 1) + 1)
                    b, g = n1 // KV2, n1 % KV2
                    if n3 is not None:
                        sp.wait_ge(s["pv_done"], n3 * NU2 + NU2 + RING2)
                    sp.dma_start(V[p][:, :, :], V2[:, bass.ds(b, 1), bass.ds(g, 1), :, :].rearrange(
                        "p b g t w -> p (b g t) w")).then_inc(s["v_in"], 16)
                    load((n1 + 1) % STEPS2, 1 - p)
                    sp.wait_ge(s["turn_copied"], n1 * 2 + 3)
                    for n, part in enumerate((hi, lo)):
                        sp.dma_start(Q[p][STACK + n:STACK + n + 1, :, :].rearrange("p h s -> p (h s)"), part[:, :]).then_inc(s["minus_in"], 16)

            run(sp, step)
            sp.wait_ge(loaded[0], 144 * (STEPS2 // 2 + 1))

        @block.scalar
        def _(act):
            act.sem_inc(s["exp_done"], 2)
            act.sem_inc(s["stack_copied"], 1)
            act.sem_inc(s["OT_copied"], 2)

            def turn_out(n2, c):
                act.wait_ge(s["pv_done"], n2 * NU2 + (16 if c == 0 else NU2) + RING2)
                act.wait_ge(s["OT_ready"], n2 * 2 + c + 1)
                act.activation(OT[c][:, :], O[c][:, :], ACT.Copy).then_inc(s["OT_copied"], 1)

            def step(n1, n2, n3, p):
                for k, (c, j, h) in enumerate(UNITS2):
                    if n2 is not None:
                        a = first_col(c, j)
                        act.wait_ge(s["scores_ready"], n2 * NU2 + k + 1)
                        act.wait_ge(s["pv_done"], n2 * NU2 + k + 1)
                        act.activation(probs[k % RING2][:, a:], SC[k % 2][:, a:], ACT.Exp,
                                       scale=DH2 ** -0.5).then_inc(s["exp_done"], 1)
                        if k == 16 + LAG2:
                            turn_out(n2, 0)
                    if n1 is not None:
                        for what, n in FILL2[k]:
                            if what == "stack":
                                act.wait_ge(s["stack_ready"], n1 * (GROUP + 1) + n + 1)
                                dst = K[p][0:STACK, :] if n == 0 else Q[p][0:STACK, n - 1, :]
                                act.activation(dst, TR[:, :], ACT.Copy).then_inc(s["stack_copied"], 1)
                    if n3 is not None and k == LAG2 + 1:
                        turn_out(n3, 1)

            run(act, step)

        @block.vector
        def _(dve):
            dve.memset(peak[:, :, :, :], 3 * NEG).then_inc(s["dve_consts"], 1)
            for i in range(2):
                dve.memset(K[i][STACK:, :], 1.0).then_inc(s["dve_consts"], 1)
            dve.wait_ge(s["dve_consts"], 3)
            dve.sem_inc(s["max_used"], 2)
            dve.sem_inc(s["turn_copied"], 1)
            dve.sem_inc(s["minus_in"], 1)
            dve.sem_inc(s["A2_done"], 1)

            def rows_out(n2, c):
                b, g = n2 // KV2, n2 % KV2
                dve.wait_ge(s["OT_ready"], n2 * 2 + c + 3)
                O4 = SM[:, :].rearrange("p (t h w) -> p t h w", t=4, h=GROUP)
                dve.reciprocal(inv[:, c, :, :], O4[:, :, :, DH2]).then_inc(s["inv_ready"], 1)
                dve.wait_ge(s["inv_ready"], n2 * 2 + c + 1)
                dve.tensor_tensor(A2[:, bass.ds(b * ST_N + 4 * c, 4), bass.ds(g * (GROUP * DH2), GROUP * DH2)].rearrange(
                    "p t (h d) -> p t h d", h=GROUP), O4[:, :, :, 0:DH2],
                    inv[:, c, :, :].rearrange("p t (h a) -> p t h a", a=1).to_broadcast([P, 4, GROUP, DH2]), ALU.mult).then_inc(s["A2_done"], 1)

            def step(n1, n2, n3, p):
                for k in range(NU2):
                    if n1 is not None:
                        for what, n in FILL2[k]:
                            if what == "max":
                                h, i, ch = MAX2[n]
                                w = min(BANK, (i + 1) * P - ch * BANK)
                                dve.wait_ge(s["max_ready"], n1 * NU2 + n + 1)
                                dve.tensor_reduce(peak[:, h, i, ch:ch + 1], MX[n % 2][:, 0:w], AX.X, ALU.max).then_inc(s["max_used"], 1)
                    for c, m in ((0, n2), (1, n3)):
                        if m is not None and k == OUT_SLOTS[c] + 2:
                            rows_out(m, c)
                    if n1 is not None and k == TURN_SLOT - 1:
                        dve.wait_ge(s["max_used"], n1 * NU2 + NU2 + 2)
                        dve.tensor_reduce(minus[:, :].rearrange("p (h i) -> p h i", h=GROUP), peak[:, :, :, :],
                                          AX.X, ALU.max, negate=True).then_inc(s["minus_ready"], 1)
                    if n1 is not None and k == TURN_SLOT:
                        dve.wait_ge(s["turn_ready"], n1 + 1)
                        dve.wait_ge(s["minus_in"], n1 * 32 + 1)
                        T = SM[0:GROUP * ST_N, 0:P]
                        dve.tensor_copy(hi[:, :], T).then_inc(s["turn_copied"], 1)
                        dve.wait_ge(s["turn_copied"], n1 * 2 + 2)
                        dve.tensor_tensor(lo[:, :], T, hi[:, :], ALU.subtract).then_inc(s["turn_copied"], 1)

            run(dve, step)

        @block.tensor
        def _(pe):
            pe.wait_ge(s["consts"], 6)
            pe.wait_ge(s["dve_consts"], 3)
            pe.sem_inc(s["pv_done"], RING2)
            pe.sem_inc(s["OT_ready"], 2)

            def scores(n2, p2, k):
                c, j, h = UNITS2[k]
                a = first_col(c, j)
                if k == 0:
                    pe.wait_ge(s["minus_in"], n2 * 32 + 33)
                    pe.wait_ge(s["v_in"], n2 * 16 + 16)
                pe.wait_ge(s["exp_done"], n2 * NU2 + k + 1)
                pe.matmul(SC[k % 2][:, a:], K[p2][:, j * P:(j + 1) * P], Q[p2][:, h, c * BANK + a:(c + 1) * BANK],
                          start=True, stop=True).then_inc(s["scores_ready"], 1)

            def output(n2, p2, k):
                c, j, h = UNITS2[k]
                a = first_col(c, j)
                if (j, h) == (0, 0):
                    pe.wait_ge(s["OT_copied"], n2 * 2 + c + 1)
                pe.wait_ge(s["exp_done"], n2 * NU2 + k + 3)
                if is_diag(c, j):
                    pe.wait_ge(s["masked"], n2 * (GROUP * ST_N) + j * GROUP + h + 1)
                pe.matmul(O[c][32 * h:32 * h + 32, a:], V[p2][:, j, :], probs[k % RING2][:, a:], start=(j == 0),
                          stop=(j == (c + 1) * 4 - 1)).then_inc(s["pv_done"], 1)

            def turn_out(n, c, turned):
                pe.wait_ge(s["OT_copied"], n * 2 + c + 3)
                pe.wait_ge(s["turn_copied"], turned * 2 + 1)
                pe.wait_ge(s["A2_done"], n * 2 + c + 1)
                for t in range(4):
                    last = pe.transpose(SM[:, t * P:(t + 1) * P], OT[c][:, t * P:(t + 1) * P], ident[:, :])
                last.then_inc(s["OT_ready"], 1)

            def fill(n1, p, what, n):
                if what == "stack":
                    if n == 0:
                        pe.wait_ge(loaded[p], (n1 - p) * 72 + 144)
                    pe.wait_ge(s["stack_copied"], n1 * (GROUP + 1) + n + 1)
                    for t in range(ST_N):
                        last = pe.transpose(TR[:, t * P:(t + 1) * P], stk[p][:, t, (n - 1) % (GROUP + 1), :], identb[:, :])
                    last.then_inc(s["stack_ready"], 1)
                else:
                    h, i, ch = MAX2[n]
                    w = min(BANK, (i + 1) * P - ch * BANK)
                    diag = ch == i * P // BANK
                    if (i, ch) == MAXU[0]:
                        pe.wait_ge(s["stack_copied"], n1 * (GROUP + 1) + h + 3)
                    pe.wait_ge(s["max_used"], n1 * NU2 + n + 1)
                    last = pe.matmul(MX[n % 2][:, 0:w], Q[p][0:STACK, h, i * P:(i + 1) * P],
                                     K[p][0:STACK, ch * BANK:ch * BANK + w], start=True, stop=not diag)
                    if diag:
                        last = pe.matmul(MX[n % 2][:, w - P:w], identb[:, :], maskb[:, :], start=False, stop=True)
                    last.then_inc(s["max_ready"], 1)

            def step(n1, n2, n3, p):
                for k in range(NU2):
                    if n3 is not None and k < LAG2:
                        output(n3, p, NU2 - LAG2 + k)
                    if n2 is not None and k > 0:
                        scores(n2, 1 - p, k)
                    if n1 is not None:
                        for f in FILL2[k]:
                            fill(n1, p, *f)
                    if n2 is not None:
                        if k == 0:
                            scores(n2, 1 - p, 0)
                        if k >= LAG2:
                            output(n2, 1 - p, k - LAG2)
                        if k == OUT_SLOTS[0]:
                            turn_out(n2, 0, n2 + 1)
                    if n3 is not None and k == OUT_SLOTS[1]:
                        turn_out(n3, 1, n3 + 2 if n2 is not None else n3 + 1)
                    if n1 is not None and k == TURN_SLOT:
                        pe.wait_ge(s["minus_ready"], n1 + 1)
                        if n2 is not None:
                            pe.wait_ge(s["A2_done"], n2 * 2 + 2)
                        pe.transpose(SM[0:GROUP * ST_N, 0:P], minus[:, :], ident[:, :]).then_inc(s["turn_ready"], 1)

            run(pe, step)


EXPERTS, FFN = 8, 512
KF = FFN // P
SLOTS = (2 * TOK + EXPERTS * (P - 1)) // P
SLOTS += SLOTS % 2
ZEROS = 12


def route(nc, hold, norm_z, shift_z, A2, w_out, ln2, w_gate, sorted_rows, weight, place, expert_of, W13, w13,
          w13_in):
    rows = hold.rearrange("p b k s -> p (b k s)").rearrange("p (t d) -> p t d", d=D)
    with ExitStack() as ctx:
        sb = lambda name, shape, dt=F32: ctx.enter_context(nc.sbuf_tensor(name, shape, dt))
        ps = lambda name, shape, dt=F32: ctx.enter_context(nc.psum_tensor(name, shape, dt))
        sem = lambda name: ctx.enter_context(nc.semaphore(name))
        Wo = sb("r_Wo", [P, KD, D])
        Wg = sb("r_Wg", [P, KD, EXPERTS])
        ln = sb("r_ln", [P, KD])
        ident = sb("r_ident", [P, P])
        before = sb("r_before", [P, P], BF16)
        ones = sb("r_ones", [P, P], BF16)
        H = sb("r_H", [P, NT, D])
        zeros = sb("r_zeros", [P, ZEROS, D])
        stage = [sb(f"r_stage{i}", [P, 2, D]) for i in range(2)]
        HN = [sb(f"r_HN{i}", [P, 2, D]) for i in range(2)]
        hT = [sb(f"r_hT{i}", [P, KD, 2, P]) for i in range(2)]
        Z = [sb(f"r_Z{i}", [P, 2, D]) for i in range(2)]
        square = sb("r_square", [P, D])
        total = sb("r_total", [P, NT])
        std = sb("r_std", [P, NT])
        logits = sb("r_logits", [P, NT, EXPERTS])
        rank = sb("r_rank", [P, NT, EXPERTS])
        slots = sb("r_slots", [P, SLOTS])
        small = {k: sb(f"r_{k}", [P, NT, EXPERTS]) for k in ("a", "b", "first", "second", "sa", "sb", "pos")}
        count = sb("r_count", [P, NT, EXPERTS], BF16)
        col = {k: sb(f"r_c_{k}", [P, NT]) for k in ("m1", "m2", "top", "e")}
        ex = {k: sb(f"r_e_{k}", [P, EXPERTS]) for k in ("tiles", "end", "end2", "start")}
        exi = sb("r_exi", [P, EXPERTS], mybir.dt.int32)
        cmp = sb("r_cmp", [1, SLOTS, EXPERTS - 1])
        eidx = sb("r_eidx", [1, SLOTS])
        T = [ps(f"r_T{i}", [P, KD, 2, P]) for i in range(2)]
        Y = [ps(f"r_Y{i}", [P, 2, D]) for i in range(2)]
        CT = [ps(f"r_CT{i}", [P, BANK]) for i in range(2)]
        names = ("w_in", "consts", "zeros_set", "zeroed", "turned", "hT_ready", "y_ready", "x2_ready", "z_ready", "summed", "var_ready", "std_ready",
                 "h_ready", "lg_ready", "lg_copied", "step", "counted", "prefix_ready", "gap_ready", "share_ready", "placed", "scattered")
        s = {k: sem(f"r_{k}") for k in names}
        staged = [sem(f"r_staged{i}") for i in range(2)]
        kept = [sem(f"r_kept{i}") for i in range(2)]
        block = ctx.enter_context(nc.Block())

        def tile_of(t, n):
            return t[:, bass.ds(n, 1), :].rearrange("p a d -> p (a d)")

        def pair_of(t, n):
            return t[:, bass.ds(n * 2, 2), :]

        NR = NT // 2

        @block.sync
        def _(sp):
            for i in range(2):
                sp.dma_start(stage[i][:, :, :], A2[:, 2 * i:2 * i + 2, :]).then_inc(staged[i], 16)
            for dst, src in ((Wo, w_out), (Wg, w_gate)):
                sp.dma_start(dst[:, :, :], src).then_inc(s["w_in"], 16)
            sp.dma_start(ln[:, :], ln2).then_inc(s["w_in"], 16)
            sp.wait_ge(s["zeros_set"], 1)

            def stage_in(g):
                for i in range(2):
                    sp.wait_ge(s["turned"], g * 2 + i + 1)
                    sp.dma_start(stage[i][:, :, :], pair_of(A2, g * 2 + (2 + i))).then_inc(staged[i], 16)

            with sp.Fori(0, SLOTS // ZEROS) as g:
                stage_in(g)
                sp.dma_start(sorted_rows.rearrange("(n p) d -> p n d", p=P)[:, bass.ds(g * ZEROS, ZEROS), :],
                             zeros[:, :, :]).then_inc(s["zeroed"], 16)
            with sp.Fori(SLOTS // ZEROS, NR // 2 - 1) as g:
                stage_in(g)
            with sp.Fori(0, NR // 2) as g:
                for i in range(2):
                    sp.wait_ge(s["h_ready"], (g * 2 + i) * 2 + 2)
                    sp.dma_start(pair_of(H, g * 2 + i), HN[i][:, :, :]).then_inc(kept[i], 16)
            for e in range(EXPERTS):
                sp.dma_start(W13[:, e, :, :], w13[:, e, :, :]).then_inc(w13_in, 16)

        @block.gpsimd
        def _(pool):
            pool.memset(zeros[:, :, :], 0.0).then_inc(s["zeros_set"], 1)
            pool.memset(ident[:, :], 0.0).then_inc(s["consts"], 1)
            pool.memset(before[:, :], 1.0).then_inc(s["consts"], 1)
            pool.memset(ones[:, :], 1.0).then_inc(s["consts"], 1)
            pool.iota(slots[:, :], pattern=[[1, SLOTS]], base=0, channel_multiplier=0,
                      allow_small_or_imprecise_dtypes=True).then_inc(s["consts"], 1)
            for e in range(EXPERTS):
                pool.memset(rank[:, :, e:e + 1], float(EXPERTS - e)).then_inc(s["consts"], 1)
            pool.wait_ge(s["consts"], 4 + EXPERTS)
            pool.affine_select(out=ident[:, :], in_=ident[:, :], compare_op=ALU.not_equal, fill=1.0, base=0,
                               pattern=[[-1, P]], channel_multiplier=1).then_inc(s["consts"], 1)
            pool.affine_select(out=before[:, :], in_=before[:, :], compare_op=ALU.is_gt, fill=0.0, base=0,
                               pattern=[[1, P]], channel_multiplier=-1).then_inc(s["consts"], 1)
            pool.wait_ge(s["placed"], 1)
            pool.wait_ge(s["zeroed"], 16 * (SLOTS // ZEROS))
            for i in range(2):
                pool.wait_ge(kept[i], 16 * (NR // 2) + 1)
            for t in range(NT):
                for k in range(2):
                    pool.indirect_dma_start(out=sorted_rows, out_offset=bass.IndirectOffsetOnAxis(ap=place[:, k, t:t + 1], axis=0),
                                            in_=H[:, t, :], in_offset=None).then_inc(s["scattered"], 16)
            pool.wait_ge(s["scattered"], 16 * 2 * NT)

        @block.tensor
        def _(pe):
            pe.wait_ge(s["consts"], 6 + EXPERTS)
            pe.wait_ge(s["w_in"], 48)
            pe.sem_inc(s["hT_ready"], 4)
            pe.sem_inc(s["x2_ready"], 2)
            def turn(src, i):
                for u in range(2):
                    for kt in range(KD):
                        last = pe.transpose(T[i][:, kt, u, :], src[i][:, u, kt * P:(kt + 1) * P], ident[:, :])
                last.then_inc(s["turned"], 1)

            with pe.Fori(0, NR // 2) as g:
                for i in range(2):
                    r = g * 2 + i
                    pe.wait_ge(staged[i], g * 16 + 16)
                    pe.wait_ge(s["hT_ready"], r * 2 + 2)
                    turn(stage, i)
                for i in range(2):
                    r = g * 2 + i
                    pe.wait_ge(s["hT_ready"], r * 2 + 6)
                    pe.wait_ge(s["x2_ready"], r + 1)
                    for u in range(2):
                        for kt in range(KD):
                            last = pe.matmul(Y[i][:, u, :], hT[i][:, kt, u, :], Wo[:, kt, :], start=(kt == 0), stop=(kt == KD - 1))
                    last.then_inc(s["y_ready"], 1)
            with pe.Fori(0, NR // 2) as g:
                for i in range(2):
                    r = g * 2 + i
                    pe.wait_ge(s["h_ready"], r * 2 + 2)
                    pe.wait_ge(s["hT_ready"], r * 2 + (2 * NR + 2))
                    turn(HN, i)
                for i in range(2):
                    r = g * 2 + i
                    pe.wait_ge(s["hT_ready"], r * 2 + (2 * NR + 6))
                    pe.wait_ge(s["x2_ready"], NR + 2)
                    pe.wait_ge(s["lg_copied"], r + 1)
                    for u in range(2):
                        for kt in range(KD):
                            last = pe.matmul(Y[i][:, u, 0:EXPERTS], hT[i][:, kt, u, :], Wg[:, kt, :], start=(kt == 0),
                                             stop=(kt == KD - 1))
                    last.then_inc(s["lg_ready"], 1)
            pe.wait_ge(s["counted"], 1)
            flat = count[:, :, :].rearrange("p t e -> p (t e)")
            pe.matmul(CT[0][:, 0:NT * EXPERTS], before[:, :], flat, start=True, stop=True).then_inc(s["prefix_ready"], 1)
            pe.matmul(CT[1][:, 0:NT * EXPERTS], ones[:, :], flat, start=True, stop=True).then_inc(s["prefix_ready"], 1)

        @block.scalar
        def _(act):
            act.wait_ge(s["w_in"], 48)
            act.activation(square[:, 0:KD], ln[:, :], ACT.Square).then_inc(s["summed"], 1)
            with act.Fori(0, NR // 2) as g:
                for i in range(2):
                    act.wait_ge(s["turned"], g * 2 + i + 1)
                    act.activation(hT[i][:, :, :, :], T[i][:, :, :, :], ACT.Copy).then_inc(s["hT_ready"], 2)
                for i in range(2):
                    r = g * 2 + i
                    act.wait_ge(s["x2_ready"], r + 3)
                    for u in range(2):
                        act.wait_ge(s["summed"], r * 2 + u + 1)
                        act.activation(square[:, :], tile_of(A2, r * 2 + u), ACT.Square,
                                       accum_out=total[:, bass.ds(r * 2 + u, 1)]).then_inc(s["summed"], 1)
            act.wait_ge(s["var_ready"], 1)
            act.activation(std[:, :], total[:, :], ACT.Sqrt).then_inc(s["std_ready"], 1)
            with act.Fori(0, NR // 2) as g:
                for i in range(2):
                    act.wait_ge(s["turned"], g * 2 + i + (NR + 1))
                    for kt in range(KD):
                        act.activation(hT[i][:, kt, :, :], T[i][:, kt, :, :], ACT.Copy,
                                       scale=ln[:, kt:kt + 1]).then_inc(s["hT_ready"], 1)
                for i in range(2):
                    act.wait_ge(s["lg_ready"], g * 2 + i + 1)
                    act.activation(pair_of(logits, g * 2 + i), Y[i][:, :, 0:EXPERTS], ACT.Copy).then_inc(s["lg_copied"], 1)
            act.wait_ge(s["gap_ready"], 1)
            act.activation(col["e"][:, :], col["e"][:, :], ACT.Exp).then_inc(s["share_ready"], 1)

        @block.vector
        def _(dve):
            dve.sem_inc(s["lg_copied"], 2)
            for i in range(2):
                dve.sem_inc(kept[i], 1)
            with dve.Fori(0, NR // 2) as g:
                for i in range(2):
                    r = g * 2 + i
                    dve.wait_ge(s["x2_ready"], r + 1)
                    for u in range(2):
                        t = r * 2 + u
                        dve.tensor_scalar(Z[i][:, u, :], tile_of(rows, t), norm_z[:, bass.ds(t, 1)], shift_z[:, bass.ds(t, 1)],
                                          ALU.mult, ALU.add).then_inc(s["z_ready"], 1)
                for i in range(2):
                    r = g * 2 + i
                    dve.wait_ge(s["z_ready"], r * 2 + 2)
                    dve.wait_ge(s["y_ready"], r + 1)
                    dve.tensor_tensor(pair_of(A2, r), Z[i][:, :, :], Y[i][:, :, :], ALU.add).then_inc(s["x2_ready"], 1)
            link = counted(dve, s["step"], 0)
            dve.wait_ge(s["summed"], NT + 1)
            link(dve.tensor_scalar(total[:, :], total[:, :], 1.0 / D, EPS, ALU.mult, ALU.add))
            dve.sem_inc(s["var_ready"], 1)
            dve.wait_ge(s["std_ready"], 1)
            link(dve.reciprocal(std[:, :], std[:, :]))
            with dve.Fori(0, NR // 2) as g:
                for i in range(2):
                    r = g * 2 + i
                    dve.wait_ge(s["turned"], r + (NR - 1))
                    dve.wait_ge(kept[i], g * 16 + 1)
                    for u in range(2):
                        dve.tensor_scalar(HN[i][:, u, :], tile_of(A2, r * 2 + u), std[:, bass.ds(r * 2 + u, 1)], None,
                                          ALU.mult).then_inc(s["h_ready"], 1)
            dve.wait_ge(s["lg_copied"], NR + 2)
            dve.wait_ge(s["consts"], 6 + EXPERTS)
            v = {k: x[:, :, :] for k, x in small.items()}
            c = {k: x[:, :] for k, x in col.items()}
            L = logits[:, :, :]

            def wide(x):
                return x.rearrange("p (t a) -> p t a", a=1).to_broadcast([P, NT, EXPERTS])

            def best(scores, out, peak):
                link(dve.tensor_reduce(peak, scores, AX.X, ALU.max))
                link(dve.tensor_tensor(v["a"], scores, wide(peak), ALU.is_equal))
                link(dve.tensor_tensor(v["a"], v["a"], rank[:, :, :], ALU.mult))
                link(dve.tensor_reduce(c["top"], v["a"], AX.X, ALU.max))
                link(dve.tensor_tensor(out, v["a"], wide(c["top"]), ALU.is_equal))

            best(L, v["first"], c["m1"])
            link(dve.scalar_tensor_tensor(out=v["b"], in0=v["first"], scalar=3 * NEG, in1=L, op0=ALU.mult, op1=ALU.add))
            best(v["b"], v["second"], c["m2"])
            link(dve.tensor_tensor(c["e"], c["m2"], c["m1"], ALU.subtract))
            dve.sem_inc(s["gap_ready"], 1)
            link(dve.tensor_tensor(count[:, :, :], v["first"], v["second"], ALU.add))
            dve.sem_inc(s["counted"], 1)
            dve.wait_ge(s["share_ready"], 1)
            link(dve.tensor_scalar(c["top"], c["e"], 1.0, None, ALU.add))
            link(dve.reciprocal(weight[:, 0, :], c["top"]))
            link(dve.tensor_tensor(weight[:, 1, :], weight[:, 0, :], c["e"], ALU.mult))
            dve.wait_ge(s["prefix_ready"], 2)
            tot = CT[1][:, 0:NT * EXPERTS].rearrange("p (t e) -> p t e", e=EXPERTS)
            link(dve.tensor_copy(v["sa"], tot))
            a, b = "sa", "sb"
            gap = 1
            while gap < NT:
                link(dve.tensor_copy(v[b][:, 0:gap], v[a][:, 0:gap]))
                link(dve.tensor_tensor(v[b][:, gap:], v[a][:, gap:], v[a][:, 0:NT - gap], ALU.add))
                a, b = b, a
                gap *= 2
            n = v[a][:, NT - 1]
            link(dve.tensor_scalar(exi[:, :], n, (P - 1) / 1.0 - P / 2 + 0.5, 1.0 / P, ALU.add, ALU.mult))
            link(dve.tensor_copy(ex["tiles"][:, :], exi[:, :]))
            link(dve.tensor_copy(ex["end"][:, :], ex["tiles"][:, :]))
            p, q = "end", "end2"
            gap = 1
            while gap < EXPERTS:
                link(dve.tensor_copy(ex[q][:, 0:gap], ex[p][:, 0:gap]))
                link(dve.tensor_tensor(ex[q][:, gap:], ex[p][:, gap:], ex[p][:, 0:EXPERTS - gap], ALU.add))
                p, q = q, p
                gap *= 2
            link(dve.tensor_tensor(ex["start"][:, :], ex[p][:, :], ex["tiles"][:, :], ALU.subtract))
            link(dve.tensor_scalar(ex["start"][:, :], ex["start"][:, :], float(P), None, ALU.mult))
            link(dve.tensor_tensor(v["pos"], v[a], tot, ALU.subtract))
            pre = CT[0][:, 0:NT * EXPERTS].rearrange("p (t e) -> p t e", e=EXPERTS)
            link(dve.tensor_tensor(v["pos"], v["pos"], pre, ALU.add))
            link(dve.tensor_tensor(v["pos"], v["pos"], ex["start"][:, :].rearrange("p (a e) -> p a e", a=1).to_broadcast([P, NT, EXPERTS]),
                                   ALU.add))
            for k, pick in enumerate(("first", "second")):
                link(dve.tensor_tensor(v["a"], v["pos"], v[pick], ALU.mult))
                link(dve.tensor_reduce(c["top"], v["a"], AX.X, ALU.add))
                link(dve.tensor_copy(place[:, k, :], c["top"]))
            dve.sem_inc(s["placed"], 1)
            link(dve.tensor_tensor(cmp[:, :, :], slots[0:1, :].rearrange("p (t a) -> p t a", a=1).to_broadcast([1, SLOTS, EXPERTS - 1]),
                                   ex[p][0:1, 0:EXPERTS - 1].rearrange("p (a e) -> p a e", a=1).to_broadcast([1, SLOTS, EXPERTS - 1]),
                                   ALU.is_ge))
            link(dve.tensor_reduce(eidx[:, :], cmp[:, :, :], AX.X, ALU.add))
            link(dve.tensor_copy(expert_of, eidx[:, :]))


def experts(nc, sorted_rows, done_rows, W13, w13_in, w2, ln2, expert_of):
    with ExitStack() as ctx:
        sb = lambda name, shape, dt=F32: ctx.enter_context(nc.sbuf_tensor(name, shape, dt))
        ps = lambda name, shape, dt=F32: ctx.enter_context(nc.psum_tensor(name, shape, dt))
        sem = lambda name: ctx.enter_context(nc.semaphore(name))
        W2 = sb("e_W2", [P, EXPERTS, KF, D])
        ln = sb("e_ln", [P, KD])
        ident = sb("e_ident", [P, P])
        G = [sb(f"e_G{i}", [P, D]) for i in range(2)]
        hT = [sb(f"e_hT{i}", [P, KD, P]) for i in range(2)]
        gate = [sb(f"e_gate{i}", [P, FFN]) for i in range(2)]
        act_T = [sb(f"e_actT{i}", [P, KF, P]) for i in range(2)]
        out = [sb(f"e_out{i}", [P, D]) for i in range(2)]
        T = ps("e_T", [P, BANK])
        GU = [[ps(f"e_GU{i}{k}", [P, BANK]) for k in range(2)] for i in range(2)]
        AT = ps("e_AT", [P, BANK])
        Y = [ps(f"e_Y{i}", [P, BANK]) for i in range(2)]
        names = ("w2_in", "ln_in", "consts", "turned", "hT_ready", "gu_ready", "gated", "act_ready", "at_ready", "actT_ready",
                 "y_ready", "y_copied")
        s = {k: sem(f"e_{k}") for k in names}
        rows_in = [sem(f"e_rows_in{i}") for i in range(2)]
        stored = [sem(f"e_stored{i}") for i in range(2)]
        block = ctx.enter_context(nc.Block())

        def slot(t, n):
            return t.rearrange("(n p) d -> n p d", p=P)[bass.ds(n, 1)].rearrange("n p d -> (n p) d")

        @block.sync
        def _(sp):
            sp.dma_start(ln[:, :], ln2).then_inc(s["ln_in"], 16)
            for i in range(2):
                sp.dma_start(G[i][:, :], sorted_rows[i * P:(i + 1) * P, :]).then_inc(rows_in[i], 16)
            for e in range(EXPERTS):
                sp.dma_start(W2[:, e, :, :], w2[:, e, :, :]).then_inc(s["w2_in"], 16)
            with sp.Fori(0, SLOTS // 2) as g:
                for i in range(2):
                    sp.wait_ge(s["turned"], g * 2 + i + 1)
                    sp.dma_start(G[i][:, :], slot(sorted_rows, (g * 2 + (2 + i)) % SLOTS)).then_inc(rows_in[i], 16)
            for i in range(2):
                sp.wait_ge(stored[i], 16 * (SLOTS // 2) + 1)
                sp.wait_ge(rows_in[i], 16 * (SLOTS // 2 + 1))

        @block.gpsimd
        def _(pool):
            pool.memset(ident[:, :], 0.0).then_inc(s["consts"], 1)
            pool.wait_ge(s["consts"], 1)
            pool.affine_select(out=ident[:, :], in_=ident[:, :], compare_op=ALU.not_equal, fill=1.0, base=0,
                               pattern=[[-1, P]], channel_multiplier=1).then_inc(s["consts"], 1)

        @block.tensor
        def _(pe):
            pe.wait_ge(s["consts"], 2)
            pe.sem_inc(s["hT_ready"], 1)
            pe.sem_inc(s["gated"], 2)
            pe.sem_inc(s["actT_ready"], 1)
            pe.sem_inc(s["y_copied"], 2)

            def turn(n, i):
                pe.wait_ge(rows_in[i], (n - i) * 8 + 16)
                pe.wait_ge(s["hT_ready"], n * 2 + 1)
                for kt in range(KD):
                    last = pe.transpose(T[:, kt * P:(kt + 1) * P], G[i][:, kt * P:(kt + 1) * P], ident[:, :])
                last.then_inc(s["turned"], 1)

            def up(n, i, e):
                pe.wait_ge(s["hT_ready"], n * 2 + 3)
                pe.wait_ge(s["gated"], n + 1)
                for half in range(2):
                    for kt in range(KD):
                        last = pe.matmul(GU[i][half][:, :], hT[i][:, kt, :],
                                         W13[:, bass.ds(e, 1), kt, half * FFN:(half + 1) * FFN].rearrange("p a f -> p (a f)"),
                                         start=(kt == 0), stop=(kt == KD - 1))
                    last.then_inc(s["gu_ready"], 1)

            def turn_act(n, i):
                pe.wait_ge(s["gated"], n + 3)
                pe.wait_ge(s["actT_ready"], n + 1)
                for kt in range(KF):
                    last = pe.transpose(AT[:, kt * P:(kt + 1) * P], gate[i][:, kt * P:(kt + 1) * P], ident[:, :])
                last.then_inc(s["at_ready"], 1)

            def down(n, i, e):
                pe.wait_ge(s["actT_ready"], n + 2)
                pe.wait_ge(s["y_copied"], n + 1)
                for kt in range(KF):
                    last = pe.matmul(Y[i][:, 0:D], act_T[i][:, kt, :], W2[:, bass.ds(e, 1), kt, :].rearrange("p a d -> p (a d)"),
                                     start=(kt == 0), stop=(kt == KF - 1))
                last.then_inc(s["y_ready"], 1)

            def expert(n):
                return pe.value_load(expert_of[0:1, bass.ds(n, 1)], min_val=0, max_val=EXPERTS - 1)

            def half(m, i):
                e_down, e_up = expert(m - 1), expert(m + 1)
                turn(m + 1, 1 - i)
                down(m - 1, 1 - i, e_down)
                turn_act(m, i)
                up(m + 1, 1 - i, e_up)

            turn(0, 0)
            pe.wait_ge(w13_in, 16 * EXPERTS)
            up(0, 0, expert(0))
            turn(1, 1)
            turn_act(0, 0)
            up(1, 1, expert(1))
            pe.wait_ge(s["w2_in"], 16 * EXPERTS)
            with pe.Fori(0, SLOTS // 2 - 1) as g:
                half(g * 2 + 1, 1)
                half(g * 2 + 2, 0)
            down(SLOTS - 2, 0, expert(SLOTS - 2))
            turn_act(SLOTS - 1, 1)
            down(SLOTS - 1, 1, expert(SLOTS - 1))

        @block.scalar
        def _(act):
            act.wait_ge(s["ln_in"], 16)

            def feed(n, i):
                act.wait_ge(s["turned"], n + 1)
                for kt in range(KD):
                    act.activation(hT[i][:, kt, :], T[:, kt * P:(kt + 1) * P], ACT.Copy, scale=ln[:, kt:kt + 1]).then_inc(s["hT_ready"], 1)

            def silu(n, i):
                act.wait_ge(s["gu_ready"], n * 2 + 1)
                act.wait_ge(s["at_ready"], n + 1)
                act.activation(gate[i][:, :], GU[i][0][:, :], ACT.Silu).then_inc(s["act_ready"], 1)

            def rows(n, i):
                act.wait_ge(s["y_ready"], n + 1)
                act.wait_ge(stored[i], (n - i) * 8 + 1)
                act.activation(out[i][:, :], Y[i][:, 0:D], ACT.Copy).then_inc(s["y_copied"], 1)
                act.wait_ge(s["y_copied"], n + 3)
                act.dma_start(slot(done_rows, n), out[i][:, :]).then_inc(stored[i], 16)

            act.sem_inc(s["at_ready"], 2)
            act.sem_inc(stored[0], 1)
            act.sem_inc(stored[1], 1)
            feed(0, 0)
            silu(0, 0)
            feed(1, 1)
            silu(1, 1)
            with act.Fori(0, SLOTS // 2 - 1) as g:
                for i in range(2):
                    m = g * 2 + i + 1
                    feed(m + 1, i)
                    rows(m - 1, i)
                    silu(m + 1, i)
            rows(SLOTS - 2, 0)
            rows(SLOTS - 1, 1)

        @block.vector
        def _(dve):
            with dve.Fori(0, SLOTS // 2) as g:
                for i in range(2):
                    n = g * 2 + i
                    dve.wait_ge(s["act_ready"], n + 1)
                    dve.wait_ge(s["gu_ready"], n * 2 + 2)
                    dve.tensor_tensor(gate[i][:, :], gate[i][:, :], GU[i][1][:, :], ALU.mult).then_inc(s["gated"], 1)
                    dve.wait_ge(s["at_ready"], n + 3)
                    dve.tensor_copy(act_T[i][:, :, :].rearrange("p k q -> p (k q)"), AT[:, :]).then_inc(s["actT_ready"], 1)


def combine(nc, hold, A2, weight, place, done_rows, out):
    rows = hold.rearrange("p b k s -> p (b k s)").rearrange("p (t d) -> p t d", d=D)
    with ExitStack() as ctx:
        sb = lambda name, shape, dt=F32: ctx.enter_context(nc.sbuf_tensor(name, shape, dt))
        sem = lambda name: ctx.enter_context(nc.semaphore(name))
        E = [sb(f"c_E{k}", [P, NT, D]) for k in range(2)]
        stats = sb("c_stats", [P, NT, 6])
        small = {k: sb(f"c_{k}", [P, NT]) for k in ("mean2", "diff", "var", "std", "scale", "shift")}
        Y = [sb(f"c_Y{i}", [P, D]) for i in range(4)]
        s = {k: sem(f"c_{k}") for k in ("halfway", "mixed", "step", "var_ready", "std_ready", "y_ready", "row_ready", "stored")}
        fetched = [sem(f"c_fetched{i}") for i in range(4)]
        block = ctx.enter_context(nc.Block())

        def tile_of(t, n):
            return t[:, bass.ds(n, 1), :].rearrange("p a d -> p (a d)")

        @block.gpsimd
        def _(pool):
            for t in range(NT):
                for k in range(2):
                    pool.indirect_dma_start(out=E[k][:, t, :], out_offset=None, in_=done_rows,
                                            in_offset=bass.IndirectOffsetOnAxis(ap=place[:, k, t:t + 1], axis=0)).then_inc(fetched[t // 8], 16)

        @block.vector
        def _(dve):
            dve.sem_inc(s["row_ready"], 1)
            for i in range(4):
                dve.wait_ge(fetched[i], 16 * 2 * 8)
                with dve.Fori(4 * i, 4 * i + 4) as g:
                    for k in range(2):
                        for u in range(2):
                            t = g * 2 + u
                            if k:
                                dve.wait_ge(s["halfway"], t + 1)
                            dve.scalar_tensor_tensor(out=tile_of(A2, t), in0=tile_of(E[k], t), scalar=weight[:, k, bass.ds(t, 1)],
                                                     in1=tile_of(A2, t), op0=ALU.mult, op1=ALU.add).then_inc(s["mixed"] if k else s["halfway"], 1)
                    for u in range(2):
                        dve.wait_ge(s["mixed"], g * 2 + u + 1)
                        dve.bn_stats(tile_of(stats, g * 2 + u), tile_of(A2, g * 2 + u)).then_inc(s["step"], 1)
            dve.wait_ge(s["step"], NT)
            link = counted(dve, s["step"], NT)
            moments(dve, link, stats, small["mean2"], small["diff"], small["var"])
            dve.sem_inc(s["var_ready"], 1)
            dve.wait_ge(s["std_ready"], 1)
            link(dve.reciprocal(small["scale"][:, :], small["std"][:, :]))
            link(dve.scalar_tensor_tensor(out=small["shift"][:, :], in0=small["mean2"][:, :], scalar=-0.5, in1=small["scale"][:, :],
                                          op0=ALU.mult, op1=ALU.mult))
            dve.sem_inc(s["var_ready"], 1)
            with dve.Fori(0, NT // 4) as g:
                for k in range(4):
                    dve.wait_ge(s["y_ready"], g * 4 + k + 1)
                    dve.tensor_tensor(tile_of(rows, g * 4 + k), Y[k][:, :], tile_of(rows, g * 4 + k), ALU.add).then_inc(s["row_ready"], 1)

        @block.scalar
        def _(act):
            act.wait_ge(s["var_ready"], 1)
            act.activation(small["std"][:, :], small["var"][:, :], ACT.Sqrt).then_inc(s["std_ready"], 1)
            act.wait_ge(s["var_ready"], 2)
            act.sem_inc(s["row_ready"], 3)
            with act.Fori(0, NT // 4) as g:
                for k in range(4):
                    t = g * 4 + k
                    act.wait_ge(s["row_ready"], t + 1)
                    act.activation(Y[k][:, :], tile_of(A2, t), ACT.Identity, scale=small["scale"][:, bass.ds(t, 1)],
                                   bias=small["shift"][:, bass.ds(t, 1)]).then_inc(s["y_ready"], 1)

        @block.sync
        def _(sp):
            o = out.rearrange("(t p) d -> p t d", p=P)
            for i in range(8):
                sp.wait_ge(s["row_ready"], 4 * i + 8)
                sp.dma_start(o[:, 4 * i:4 * i + 4, :], rows[:, 4 * i:4 * i + 4, :]).then_inc(s["stored"], 16)
            sp.wait_ge(s["stored"], 16 * 8)


def layer(nc, x, w_pair, w_out1, w_qkv2, w_out2, ln1, ln2, w_gate, w13, w2, cos2, sin2, out):
    nc.disable_value_cache = True
    stack_dram = nc.dram_tensor("stack_rows", [NT, P, HEADS2 * STACK], BF16, kind="Internal").ap()
    sorted_rows = nc.dram_tensor("sorted_rows", [SLOTS * P, D], F32, kind="Internal").ap()
    done_rows = nc.dram_tensor("done_rows", [SLOTS * P, D], F32, kind="Internal").ap()
    with ExitStack() as ctx:
        sb = lambda name, shape, dt=F32: ctx.enter_context(nc.sbuf_tensor(name, shape, dt))
        hold = sb("hold", [P, B, KD, S])[:, :, :, :]
        norm_z, shift_z = sb("norm_z", [P, NT])[:, :], sb("shift_z", [P, NT])[:, :]
        normalise(nc, x, hold)
        attention_one(nc, hold, w_pair, w_out1)
        weight = sb("weight", [P, 2, NT])[:, :, :]
        place = sb("place", [P, 2, NT], mybir.dt.uint32)[:, :, :]
        expert_of = sb("expert_of", [1, SLOTS], mybir.dt.int32)[:, :]
        A2 = sb("A2", [P, NT, D])[:, :, :]
        with ExitStack() as inner:
            V2 = inner.enter_context(nc.sbuf_tensor("V2", [P, B, KV2, ST_N, 2 * DH2], F32))[:, :, :, :, :]
            project_two(nc, x, hold, w_qkv2, ln1, cos2, sin2, norm_z, shift_z, V2, stack_dram)
            attention_two(nc, stack_dram, V2, A2)
        with ExitStack() as inner:
            W13 = inner.enter_context(nc.sbuf_tensor("W13", [P, EXPERTS, KD, 2 * FFN], F32))[:, :, :, :]
            w13_in = inner.enter_context(nc.semaphore("w13_in"))
            route(nc, hold, norm_z, shift_z, A2, w_out2, ln2, w_gate, sorted_rows, weight, place, expert_of, W13, w13, w13_in)
            experts(nc, sorted_rows, done_rows, W13, w13_in, w2, ln2, expert_of)
        combine(nc, hold, A2, weight, place, done_rows, out)


def kernel(**inputs):
    import concourse.bacc as bacc
    from concourse.bass_utils import run_bass_kernel_spmd as run

    a = {k: np.asarray(v) for k, v in inputs.items()}

    def turned(w, cols=None):
        return np.ascontiguousarray(w.T.reshape(w.shape[1] // P, P, w.shape[0]).transpose(1, 0, 2))

    f = np.float32
    inv_freq = (f(1) / np.power(f(10000.0), np.arange(0, DH2, 2, dtype=f) / f(DH2))).astype(f)
    angle = np.arange(S, dtype=f)[:, None] * inv_freq[None, :]
    table = lambda left, right: np.ascontiguousarray(
        np.concatenate([left, right], 1).astype(f).reshape(ST_N, P, DH2).transpose(1, 0, 2))
    qkv = np.stack([a["L0_attn_w_q"].reshape(H1 * DH1, D), a["L0_attn_w_k"].reshape(H1 * DH1, D),
                    a["L0_attn_w_v"].reshape(H1 * DH1, D)])
    arrays = {
        "x": np.ascontiguousarray(a["L0_attn_x"].reshape(TOK, D)),
        "w_pair": np.ascontiguousarray(qkv.reshape(3, PAIRS, P, KD, P).transpose(1, 4, 3, 0, 2)),
        "w_out1": turned(a["L0_attn_w_o"]),
        "w_qkv2": turned(a["L0_ffn_wqkv"]),
        "w_out2": turned(a["L0_ffn_wo"]),
        "ln1": np.ascontiguousarray(a["L0_ffn_ln1_w"].reshape(KD, P).T),
        "ln2": np.ascontiguousarray(a["L0_ffn_ln2_w"].reshape(KD, P).T),
        "w_gate": turned(a["L0_ffn_gate_w"]),
        "w13": np.ascontiguousarray(a["L0_ffn_w13"].reshape(EXPERTS, 2 * FFN, KD, P).transpose(3, 0, 2, 1)),
        "w2": np.ascontiguousarray(a["L0_ffn_w2"].reshape(EXPERTS, D, KF, P).transpose(3, 0, 2, 1)),
        "cos2": table(np.cos(angle), np.cos(angle)),
        "sin2": table(-np.sin(angle), np.sin(angle)),
    }
    nc = bacc.Bacc("TRN2", target_bir_lowering=False, num_devices=1)
    args = {k: nc.dram_tensor(f"in_{k}", v.shape, mybir.dt.from_np(v.dtype), kind="ExternalInput").ap()
            for k, v in arrays.items()}
    out = nc.dram_tensor("out_rows", (TOK, D), F32, kind="ExternalOutput").ap()
    layer(nc, out=out, **args)
    r = run(nc, [{f"in_{k}": v for k, v in arrays.items()}], core_ids=[0])
    return r.results[0]["out_rows"].reshape(B, S, D)
```

```python
from contextlib import ExitStack

import numpy as np

import concourse.bass as bass
from concourse import mybir

F32 = mybir.dt.float32
F32R = mybir.dt.float32r
BF16 = mybir.dt.bfloat16
ALU = mybir.AluOpType
ACT = mybir.ActivationFunctionType
AX = mybir.AxisListType

P = 128
BANK = 512
B, S, D = 4, 1024, 256
TOK = B * S
NT = TOK // P
KD = D // P
ST_N = S // P
EPS = 1e-5
NEG = -1e30

H1, DH1 = 16, 64
PAIRS = H1 // 2

UNITS = [(c, j) for c in range(S // BANK) for j in range((c + 1) * BANK // P)]
NU = len(UNITS)
LAST = [n for n, (c, j) in enumerate(UNITS) if j == (c + 1) * BANK // P - 1]
MAXU = [(i, c) for i in range(ST_N) for c in range(i * P // BANK + 1)]


def first_col(c, j):
    return max(0, j * P - c * BANK)


def is_diag(c, j):
    return j * P >= c * BANK


def normalise(nc, x, hold):
    with ExitStack() as ctx:
        sb = lambda name, shape, dt=F32: ctx.enter_context(nc.sbuf_tensor(name, shape, dt))
        sem = lambda name: ctx.enter_context(nc.semaphore(name))
        X = sb("n_x", [P, NT, D])
        XN = sb("n_xn", [P, 4, D])
        stats = sb("n_stats", [P, NT, 6])
        scale = sb("n_scale", [P, NT])
        shift = sb("n_shift", [P, NT])
        mean2 = sb("n_mean2", [P, NT])
        diff = sb("n_diff", [P, NT])
        var = sb("n_var", [P, NT])
        std = sb("n_std", [P, NT])
        ident = sb("n_ident", [P, P])
        T = [ctx.enter_context(nc.psum_tensor(f"n_T{i}", [P, KD, 2, P], F32)) for i in range(2)]
        x_in = [sem(f"n_x_in{i}") for i in range(4)]
        id_set = sem("n_id_set")
        step = sem("n_step")
        var_ready = sem("n_var_ready")
        std_ready = sem("n_std_ready")
        xn_ready = sem("n_xn_ready")
        turned = sem("n_turned")
        stored = sem("n_stored")
        block = ctx.enter_context(nc.Block())

        @block.sync
        def _(sp):
            xt = x.rearrange("(t p) d -> p t d", p=P)
            for i in range(4):
                sp.dma_start(X[:, 8 * i:8 * i + 8, :], xt[:, 8 * i:8 * i + 8, :]).then_inc(x_in[i], 16)

        @block.gpsimd
        def _(pool):
            pool.memset(ident[:, :], 0.0).then_inc(id_set, 1)
            pool.wait_ge(id_set, 1)
            pool.affine_select(out=ident[:, :], in_=ident[:, :], compare_op=ALU.not_equal, fill=1.0, base=0,
                               pattern=[[-1, P]], channel_multiplier=1).then_inc(id_set, 1)

        Q4 = NT // 4

        def part(t, i):
            return t[:, Q4 * i:Q4 * (i + 1)]

        @block.vector
        def _(dve):
            for i in range(4):
                dve.wait_ge(x_in[i], 16)
                for t in range(Q4 * i, Q4 * (i + 1)):
                    dve.bn_stats(stats[:, t, :], X[:, t, :]).then_inc(step, 1)
                base = (Q4 + 8) * i + Q4
                dve.wait_ge(step, base)
                link = counted(dve, step, base)
                moments(dve, link, stats[:, Q4 * i:Q4 * (i + 1), :], part(mean2, i), part(diff, i), part(var, i))
                dve.sem_inc(var_ready, 1)
                dve.wait_ge(std_ready, i + 1)
                link(dve.reciprocal(part(scale, i), part(std, i)))
                link(dve.scalar_tensor_tensor(out=part(shift, i), in0=part(mean2, i), scalar=-0.5, in1=part(scale, i),
                                              op0=ALU.mult, op1=ALU.mult))
                for t in range(Q4 * i, Q4 * (i + 1)):
                    if t % 2 == 0:
                        dve.wait_ge(turned, t // 2 + 1)
                    dve.tensor_scalar(XN[:, t % 4, :], X[:, t, :], scale[:, t:t + 1], shift[:, t:t + 1],
                                      ALU.mult, ALU.add).then_inc(xn_ready, 1)

        @block.scalar
        def _(act):
            act.sem_inc(stored, 2)
            for i in range(4):
                act.wait_ge(var_ready, i + 1)
                act.activation(part(std, i), part(var, i), ACT.Sqrt).then_inc(std_ready, 1)
                for u in range(Q4 // 4):
                    for k in range(2):
                        turn = i * (Q4 // 2) + u * 2 + k
                        tile = u * 4 + 2 * k
                        act.wait_ge(turned, turn + 3)
                        act.activation(hold[:, i, :, tile * P:(tile + 2) * P], T[k][:, :, :, :].rearrange("p a b q -> p a (b q)"),
                                       ACT.Copy).then_inc(stored, 1)

        @block.tensor
        def _(pe):
            pe.wait_ge(id_set, 2)
            pe.sem_inc(turned, 2)
            with pe.Fori(0, NT // 4) as g:
                for k in range(2):
                    pe.wait_ge(xn_ready, g * 4 + 2 * k + 2)
                    pe.wait_ge(stored, g * 2 + k + 1)
                    for u in range(2):
                        for kt in range(KD):
                            last = pe.transpose(T[k][:, kt, u, :], XN[:, 2 * k + u, kt * P:(kt + 1) * P], ident[:, :])
                    last.then_inc(turned, 1)


def moments(dve, link, stats, mean2, diff, var):
    link(dve.tensor_tensor(mean2[:, :], stats[:, :, 1], stats[:, :, 4], ALU.add))
    link(dve.tensor_tensor(diff[:, :], stats[:, :, 1], stats[:, :, 4], ALU.subtract))
    link(dve.tensor_tensor(var[:, :], stats[:, :, 2], stats[:, :, 5], ALU.add))
    link(dve.scalar_tensor_tensor(out=diff[:, :], in0=diff[:, :], scalar=0.25, in1=diff[:, :],
                                  op0=ALU.mult, op1=ALU.mult))
    link(dve.scalar_tensor_tensor(out=var[:, :], in0=var[:, :], scalar=1.0 / D, in1=diff[:, :],
                                  op0=ALU.mult, op1=ALU.add))
    link(dve.tensor_scalar(var[:, :], var[:, :], EPS, None, ALU.add))


MAXN = [(h, i, c) for early in (True, False) for h in range(2) for i, c in MAXU if (i < BANK // P) == early]
NMAX = len(MAXN)
FILL = {n: [] for n in range(NU)}
for _n, _item in ((0, ("q", 0)), (2, ("k", 0)), (3, ("q", 1)), (4, ("v", 0)), (5, ("k", 1)), (8, ("v", 1))):
    FILL[_n].append(_item)
for _n in range(NMAX):
    FILL[(4, 4, 4, 4, 5, 5, 6, 6, 7, 7, 7, 7, 8, 8, 8, 8, 9, 9, 9, 9, 10, 10, 10, 10)[_n]].append(("max", _n))
FILL[11].append(("turn", 0))
LAG = 2
RING = 5
ADDS = [n for n, (c, j) in enumerate(UNITS) if j > 0]
SUM_SLOT = (6, 0)
COPY_SLOT = (7, 1)
WO_SLOT, WO_GROUPS = 7, ST_N // 2
PIECES = 4


def attention_one(nc, hold, w_pair, w_out):
    rows = hold.rearrange("p b k s -> p b (k s)").rearrange("p b (t d) -> p (b t) d", d=D)
    with ExitStack() as ctx:
        sb = lambda name, shape, dt=F32: ctx.enter_context(nc.sbuf_tensor(name, shape, dt))
        ps = lambda name, shape, dt=F32: ctx.enter_context(nc.psum_tensor(name, shape, dt))
        sem = lambda name: ctx.enter_context(nc.semaphore(name))
        xT = sb("a_xT", [P, KD, S])
        W = [sb(f"a_W{i}", [P, KD, 3, P]) for i in range(2)]
        Wo = sb("a_Wo", [P, PAIRS, D])
        QR = [[sb(f"a_QR{i}{h}", [P, S], F32R) for h in range(2)] for i in range(2)]
        KR = [[sb(f"a_KR{i}{h}", [P, S], F32R) for h in range(2)] for i in range(2)]
        QS = [[sb(f"a_QS{i}{h}", [DH1 + 1, S], F32R) for h in range(2)] for i in range(2)]
        KS = [[sb(f"a_KS{i}{h}", [DH1 + 1, S], F32R) for h in range(2)] for i in range(2)]
        V = [[sb(f"a_V{i}{h}", [P, ST_N, DH1]) for h in range(2)] for i in range(2)]
        cat = sb("a_cat", [P, PAIRS, S])
        ring = [[sb(f"a_P{h}{i}", [P, BANK]) for i in range(RING)] for h in range(2)]
        acc = [[sb(f"a_A{h}{c}", [P, BANK]) for c in range(2)] for h in range(2)]
        total = [sb(f"a_total{c}", [P, BANK]) for c in range(2)]
        inv = [sb(f"a_inv{c}", [P, BANK]) for c in range(2)]
        peak = sb("a_peak", [P, 2, ST_N, 2])
        minus = sb("a_minus", [P, 2 * ST_N])
        minusT = sb("a_minusT", [2 * ST_N, P], F32R)
        ident = sb("a_ident", [P, P])
        ones = sb("a_ones", [P, DH1])
        identb = sb("a_identb", [P, P], BF16)
        maskb = sb("a_maskb", [P, P], BF16)
        SC = [ps(f"a_SC{h}", [P, BANK]) for h in range(2)]
        MX = [ps(f"a_MX{i}", [P, BANK]) for i in range(2)]
        O = [ps(f"a_O{c}", [P, BANK]) for c in range(2)]
        PR = [ps(f"a_PR{i}", [P, BANK]) for i in range(2)]

        names = ("consts", "dve_consts", "x_in", "wo_in", "q_ready", "q_copied", "q_split", "k_ready", "k_copied", "k_split",
                 "v_ready", "v_copied", "max_ready", "max_used", "minus_ready", "turn_ready", "turn_copied", "minus_in",
                 "scores_ready", "exp_done", "mask_due", "masked", "pv_done", "sums_ready", "sums_copied", "inv_ready", "out_done",
                 "proj_ready", "proj_copied")
        s = {k: sem(f"a_{k}") for k in names}
        w_in = [sem(f"a_w_in{i}") for i in range(2)]
        added = [sem(f"a_added{h}") for h in range(2)]
        block = ctx.enter_context(nc.Block())

        N2 = 2 * NU
        NA = len(ADDS)

        def buffer(n, h):
            c, j = UNITS[n]
            return acc[h][c] if j == 0 else ring[h][ADDS.index(n) % RING]

        N = B * PAIRS

        def run(eng, step, end=lambda: None):
            def six(first):
                with eng.Fori(0, PAIRS // 2 - 1) as u:
                    m = first + u * 2
                    step(m + 2, m + 1, m, 0)
                    step(m + 3, m + 2, m + 1, 1)

            step(0, None, None, 0, begins=True)
            step(1, 0, None, 1)
            with eng.Fori(0, B - 1) as b:
                n = b * PAIRS
                six(n)
                step(n + PAIRS, n + (PAIRS - 1), n + (PAIRS - 2), 0, begins=True)
                step(n + (PAIRS + 1), n + PAIRS, n + (PAIRS - 1), 1, wo=b)
            six(N - PAIRS)
            step(None, N - 1, N - 2, 0)
            step(None, None, N - 1, 1)
            end()

        def add(eng, n2, n, h):
            c, j = UNITS[n]
            a = first_col(c, j)
            if is_diag(c, j):
                eng.wait_ge(s["masked"], n2 * (2 * ST_N) + 2 * j + h + 1)
            else:
                eng.wait_ge(s["exp_done"], n2 * N2 + 2 * n + h + 3)
            if j == 1:
                eng.wait_ge(s["pv_done"], n2 * N2 + N2 + 2 * (n - 1) + h + 1)
            else:
                eng.wait_ge(added[h], n2 * NA + NA + ADDS.index(n))
            eng.tensor_tensor(acc[h][c][:, a:], acc[h][c][:, a:], buffer(n, h)[:, a:], ALU.add).then_inc(added[h], 1)

        @block.gpsimd
        def _(pool):
            for m, fill in ((ident, 0.0), (identb, 0.0), (maskb, 0.0)):
                pool.memset(m[:, :], fill).then_inc(s["consts"], 1)
            pool.wait_ge(s["consts"], 3)
            for m in (ident, identb):
                pool.affine_select(out=m[:, :], in_=m[:, :], compare_op=ALU.not_equal, fill=1.0, base=0,
                                   pattern=[[-1, P]], channel_multiplier=1).then_inc(s["consts"], 1)
            pool.affine_select(out=maskb[:, :], in_=maskb[:, :], compare_op=ALU.is_ge, fill=NEG, base=0,
                               pattern=[[-1, P]], channel_multiplier=1).then_inc(s["consts"], 1)

            def step(n1, n2, n3, p, begins=False, wo=None):
                if n2 is None:
                    return
                for n, (c, j) in enumerate(UNITS):
                    for h in range(2):
                        if is_diag(c, j):
                            a = first_col(c, j)
                            t = buffer(n, h)[:, a:a + P]
                            pool.wait_ge(s["exp_done"], n2 * N2 + 2 * n + h + 3)
                            pool.sem_inc(s["mask_due"], 1)
                            pool.affine_select(out=t, in_=t, compare_op=ALU.is_ge, fill=0.0, base=0, pattern=[[1, P]],
                                               channel_multiplier=-1).then_inc(s["masked"], 1)
                    if n - 1 in ADDS:
                        add(pool, n2, n - 1, 1)
                add(pool, n2, NU - 1, 1)

            pool.sem_inc(added[1], NA)
            run(pool, step)

        @block.sync
        def _(sp):
            sp.dma_start(Wo[:, :, :], w_out).then_inc(s["wo_in"], 16)
            for i in range(2):
                sp.dma_start(W[i][:, :, :, :], w_pair[i]).then_inc(w_in[i], 16)

            def step(n1, n2, n3, p, begins=False, wo=None):
                if begins:
                    sp.wait_ge(s["v_ready"], n1 * 2 + 1)
                    sp.dma_start(xT[:, :, :], hold[:, bass.ds(n1 // PAIRS, 1), :, :].rearrange("p b k s -> p (b k) s")).then_inc(s["x_in"], 16)
                if n1 is not None:
                    sp.wait_ge(s["turn_copied"], n1 + 2)
                    for h in range(2):
                        sp.dma_start(QS[p][h][DH1:DH1 + 1, :].bitcast(F32),
                                     minusT[ST_N * h:ST_N * (h + 1), :].bitcast(F32)).then_inc(s["minus_in"], 16)
                    sp.dma_start(W[p][:, :, :, :], w_pair[bass.ds((n1 + 2) % PAIRS, 1)].rearrange(
                        "a p k w c -> p (a k) w c")).then_inc(w_in[p], 16)

            run(sp, step)
            for i in range(2):
                sp.wait_ge(w_in[i], 16 * (B * PAIRS // 2 + 1))

        @block.scalar
        def _(act):
            act.sem_inc(s["exp_done"], 2)
            act.sem_inc(s["v_copied"], 1)

            def feed(n1, p, what, c):
                cols = slice(c * BANK, (c + 1) * BANK)
                if what == "q":
                    act.wait_ge(s["q_ready"], n1 * 2 + c + 1)
                    for h in range(2):
                        for half in (h, 1 - h):
                            act.activation(QR[p][h][DH1 * half:DH1 * (half + 1), cols],
                                           PR[c][DH1 * h:DH1 * (h + 1), :], ACT.Copy).then_inc(s["q_copied"], 1)
                elif what == "k":
                    act.wait_ge(s["k_ready"], n1 * 2 + c + 1)
                    for h in range(2):
                        for dst in (KR[p][h][DH1 * h:DH1 * (h + 1), cols], KS[p][h][0:DH1, cols]):
                            act.activation(dst, PR[c][DH1 * h:DH1 * (h + 1), :], ACT.Copy).then_inc(s["k_copied"], 1)
                elif what == "v":
                    act.wait_ge(s["v_ready"], n1 * 2 + c + 2)
                    for h in range(2):
                        act.activation(V[p][h][:, 4 * c:4 * c + 4, :],
                                       PR[c][:, :].rearrange("p (t w) -> p t w", t=4)[:, :, DH1 * h:DH1 * (h + 1)],
                                       ACT.Copy).then_inc(s["v_copied"], 1)

            def step(n1, n2, n3, p, begins=False, wo=None):
                for n, (ch, j) in enumerate(UNITS):
                    if n == 0 and n1 is not None:
                        feed(n1, p, *FILL[0][0])
                    if n2 is not None:
                        a = first_col(ch, j)
                        for h in range(2):
                            act.wait_ge(s["scores_ready"], n2 * N2 + 2 * n + h + 1)
                            if j == 0:
                                act.wait_ge(s["sums_ready"], n2 * 2 + ch + 1)
                            else:
                                m = ADDS.index(n) - RING
                                k = 2 * ADDS[m] + h + (N2 if m >= 0 else 0)
                                act.wait_ge(s["pv_done"], n2 * N2 + k + 1)
                                act.wait_ge(added[h], n2 * NA + NA + m + 1)
                            act.activation(buffer(n, h)[:, a:], SC[h][:, a:], ACT.Exp, scale=DH1 ** -0.5).then_inc(s["exp_done"], 1)
                    if n1 is not None and n > 0:
                        for what, c in FILL[n]:
                            feed(n1, p, what, c)
                    for c, m in ((0, n2), (1, n3)):
                        if m is not None and n == COPY_SLOT[c]:
                            act.wait_ge(s["sums_ready"], m * 2 + c + 3)
                            act.wait_ge(s["inv_ready"], (m * 2 + c + 1) * PIECES)
                            act.activation(total[c][:, :], PR[c][:, :], ACT.Copy).then_inc(s["sums_copied"], 1)
                    if wo is not None and 0 <= n - WO_SLOT < WO_GROUPS:
                        rows_out(wo, n - WO_SLOT)

            def rows_out(b, g):
                act.wait_ge(s["proj_ready"], b * WO_GROUPS + g + (WO_GROUPS + 1))
                act.activation(rows[:, bass.ds(b * ST_N + 2 * g, 2), :].rearrange("p t d -> p (t d)"), PR[0][:, :],
                               ACT.Copy).then_inc(s["proj_copied"], 1)

            def end():
                for g in range(WO_GROUPS):
                    rows_out(B - 1, g)

            act.sem_inc(s["proj_copied"], 1)
            run(act, step, end)

        @block.vector
        def _(dve):
            dve.memset(peak[:, :, :, :], 3 * NEG).then_inc(s["dve_consts"], 1)
            dve.memset(ones[:, :], 1.0).then_inc(s["dve_consts"], 1)
            dve.memset(inv[0][DH1:DH1 + 1, :], 1.0).then_inc(s["dve_consts"], 1)
            dve.wait_ge(s["dve_consts"], 3)
            for i in range(2):
                for h in range(2):
                    for c in range(2):
                        dve.tensor_copy(KS[i][h][DH1:DH1 + 1, c * BANK:(c + 1) * BANK], inv[0][DH1:DH1 + 1, :]).then_inc(s["dve_consts"], 1)
            dve.wait_ge(s["dve_consts"], 11)
            dve.sem_inc(s["max_used"], 2)
            dve.sem_inc(s["minus_in"], 1)
            dve.sem_inc(s["turn_copied"], 1)
            dve.sem_inc(s["out_done"], 4)
            dve.sem_inc(added[0], NA)
            dve.sem_inc(s["sums_copied"], 4)
            dve.sem_inc(s["inv_ready"], 2 * PIECES)

            def inverse(n, c, i):
                if i == 0:
                    dve.wait_ge(s["sums_copied"], n * 2 + c + 5)
                    dve.wait_ge(s["out_done"], n * 2 + c + 3)
                cols = slice(i * BANK // PIECES, (i + 1) * BANK // PIECES)
                dve.reciprocal(inv[c][:, cols], total[c][:, cols]).then_inc(s["inv_ready"], 1)

            def output(n, c):
                dve.wait_ge(s["inv_ready"], (n * 2 + c + 3) * PIECES)
                dve.wait_ge(s["proj_ready"], n // PAIRS * WO_GROUPS + (c + 1) * (WO_GROUPS // 2))
                dve.tensor_tensor(cat[:, bass.ds(n % PAIRS, 1), c * BANK:(c + 1) * BANK].rearrange("p a s -> p (a s)"), O[c][:, :],
                                  inv[c][:, :], ALU.mult).then_inc(s["out_done"], 1)

            def reduce_max(n1, c):
                h, i, ch = MAXN[c]
                w = min(BANK, (i + 1) * P - ch * BANK)
                dve.wait_ge(s["max_ready"], n1 * NMAX + c + 1)
                dve.tensor_reduce(peak[:, h, i, ch:ch + 1], MX[c % 2][:, 0:w], AX.X, ALU.max).then_inc(s["max_used"], 1)
                if c == NMAX - 1:
                    dve.wait_ge(s["max_used"], n1 * NMAX + NMAX + 2)
                    dve.tensor_reduce(minus[:, :].rearrange("p (h i) -> p h i", h=2), peak[:, :, :, :],
                                      AX.X, ALU.max, negate=True).then_inc(s["minus_ready"], 1)

            def split(n1, p, what, c, h):
                own, cols = slice(DH1 * h, DH1 * (h + 1)), slice(c * BANK, (c + 1) * BANK)
                if what == "q":
                    dve.wait_ge(s["q_copied"], n1 * 8 + 4 * c + 4)
                    dve.tensor_tensor(QS[p][h][0:DH1, cols], PR[c][own, :], QR[p][h][own, cols],
                                      ALU.subtract).then_inc(s["q_split"], 1)
                else:
                    dve.wait_ge(s["k_copied"], n1 * 8 + 4 * c + 4)
                    dve.tensor_tensor(KR[p][h][DH1 * (1 - h):DH1 * (2 - h), cols], PR[c][own, :],
                                      KR[p][h][own, cols], ALU.subtract).then_inc(s["k_split"], 1)

            def turn(n1):
                dve.wait_ge(s["turn_ready"], n1 + 1)
                dve.wait_ge(s["minus_in"], n1 * 32 + 1)
                dve.tensor_copy(minusT[:, :], PR[1][0:2 * ST_N, 0:P]).then_inc(s["turn_copied"], 1)

            def step(n1, n2, n3, p, begins=False, wo=None):
                if n3 is not None:
                    add(dve, n3, NU - 1, 0)
                for n in range(NU):
                    maxima = [c for what, c in FILL[n] if n1 is not None and what == "max"]

                    def one_max():
                        if maxima:
                            reduce_max(n1, maxima.pop(0))

                    one_max()
                    if n1 is not None:
                        for what, c in (FILL[0] if n == 0 else []) + (FILL[n - 1] if n > 1 else []):
                            if what in "qk":
                                for h in range(2):
                                    split(n1, p, what, c, h)
                                    one_max()
                    if n2 is not None and n - 1 in ADDS:
                        one_max()
                        add(dve, n2, n - 1, 0)
                    one_max()
                    for c, m in ((0, n2), (1, n3)):
                        i = n - COPY_SLOT[c]
                        if m is not None and 0 <= i < PIECES:
                            inverse(m, c, i)
                            one_max()
                            if i == PIECES - 1:
                                output(m, c)
                    while maxima:
                        one_max()
                    if n1 is not None and ("turn", 0) in FILL[n]:
                        turn(n1)

            run(dve, step)

        @block.tensor
        def _(pe):
            pe.wait_ge(s["consts"], 6)
            pe.wait_ge(s["dve_consts"], 11)
            pe.wait_ge(s["wo_in"], 16)
            pe.sem_inc(s["pv_done"], N2)
            pe.sem_inc(s["sums_ready"], 2)
            pe.sem_inc(s["v_ready"], 1)
            pe.sem_inc(s["proj_ready"], WO_GROUPS)

            def scores(n2, p, n, h):
                c, j = UNITS[n]
                a = first_col(c, j)
                keys, queries = slice(j * P, (j + 1) * P), slice(c * BANK + a, (c + 1) * BANK)
                if n == 0:
                    pe.wait_ge(s["minus_in"], n2 * 32 + 33)
                pe.wait_ge(s["exp_done"], n2 * N2 + 2 * n + h + 1)
                pe.matmul(SC[h][:, a:], KR[p][h][:, keys], QR[p][h][:, queries], start=True, stop=False)
                pe.matmul(SC[h][:, a:], KS[p][h][:, keys], QS[p][h][:, queries], start=False,
                          stop=True).then_inc(s["scores_ready"], 1)

            def output(n2, p, n):
                c, j = UNITS[n]
                a = first_col(c, j)
                if j == 0:
                    pe.wait_ge(s["out_done"], n2 * 2 + c + 3)
                pe.wait_ge(s["exp_done"], n2 * N2 + 2 * n + 4)
                if is_diag(c, j):
                    pe.wait_ge(s["masked"], n2 * (2 * ST_N) + 2 * j + 2)
                for h in range(2):
                    pe.matmul(O[c][DH1 * h:DH1 * (h + 1), a:], V[p][h][:, j, :], buffer(n, h)[:, a:], start=(j == 0),
                              stop=(n in LAST)).then_inc(s["pv_done"], 1)

            def sums(n2, c):
                for h in range(2):
                    pe.wait_ge(added[h], n2 * NA + NA + ADDS.index(LAST[c]) + 1)
                pe.wait_ge(s["sums_copied"], n2 * 2 + c + 4)
                for h in range(2):
                    last = pe.matmul(PR[c][DH1 * h:DH1 * (h + 1), :], ones[:, :], acc[h][c][:, :], start=True, stop=True)
                last.then_inc(s["sums_ready"], 1)

            def fill(n1, p, what, c):
                if what in "qk":
                    if (what, c) == ("q", 0):
                        pe.wait_ge(w_in[p], (n1 - p) * 8 + 16)
                        pe.wait_ge(s["sums_copied"], n1 * 2 + 1)
                    elif (what, c) == ("q", 1):
                        pe.wait_ge(s["v_copied"], n1 * 4 + 1)
                        pe.wait_ge(s["sums_copied"], n1 * 2 + 2)
                    else:
                        pe.wait_ge(s["q_split"], n1 * 4 + 2 * c + 2)
                        pe.wait_ge(s["q_copied"], n1 * 8 + 4 * c + 4)
                    for kt in range(KD):
                        last = pe.matmul(PR[c][:, :], W[p][:, kt, "qk".index(what), :],
                                         hold[:, bass.ds(n1 // PAIRS, 1), kt, c * BANK:(c + 1) * BANK].rearrange("p b s -> p (b s)"),
                                         start=(kt == 0), stop=(kt == KD - 1))
                    last.then_inc(s["q_ready"] if what == "q" else s["k_ready"], 1)
                elif what == "v":
                    pe.wait_ge(s["k_split"], n1 * 4 + 2 * c + 2)
                    pe.wait_ge(s["k_copied"], n1 * 8 + 4 * c + 4)
                    if c == 0:
                        pe.wait_ge(s["x_in"], n1 // PAIRS * 16 + 16)
                    for t in range(4):
                        for kt in range(KD):
                            last = pe.matmul(PR[c][:, t * P:(t + 1) * P], xT[:, kt, (4 * c + t) * P:(4 * c + t + 1) * P],
                                             W[p][:, kt, 2, :], start=(kt == 0), stop=(kt == KD - 1))
                    last.then_inc(s["v_ready"], 1)
                elif what == "max":
                    h, i, ch = MAXN[c]
                    w = min(BANK, (i + 1) * P - ch * BANK)
                    diag = ch == i * P // BANK
                    own = slice(DH1 * h, DH1 * (h + 1))
                    if i * P // BANK == 1 or c == 0:
                        pe.wait_ge(s["q_copied"], n1 * 8 + 4 * (i * P // BANK) + 4)
                        pe.wait_ge(s["k_copied"], n1 * 8 + 4 * (i * P // BANK) + 4)
                    pe.wait_ge(s["max_used"], n1 * NMAX + c + 1)
                    last = pe.matmul(MX[c % 2][:, 0:w], QR[p][h][own, i * P:(i + 1) * P], KR[p][h][own, ch * BANK:ch * BANK + w],
                                     start=True, stop=not diag)
                    if diag:
                        last = pe.matmul(MX[c % 2][:, w - P:w], identb[:, :], maskb[:, :], start=False, stop=True)
                    last.then_inc(s["max_ready"], 1)
                elif what == "turn":
                    pe.wait_ge(s["minus_ready"], n1 + 1)
                    pe.wait_ge(s["v_copied"], n1 * 4 + 5)
                    pe.transpose(PR[1][0:2 * ST_N, 0:P], minus[:, :], ident[:, :]).then_inc(s["turn_ready"], 1)

            def step(n1, n2, n3, p, begins=False, wo=None):
                for n in range(NU):
                    if n3 is not None and n == 0:
                        output(n3, p, NU - 2)
                    if n1 is not None and n == 0:
                        fill(n1, p, *FILL[0][0])
                    if n3 is not None and n == 0:
                        output(n3, p, NU - 1)
                    maxima = [f for f in FILL[n] if n1 is not None and f[0] == "max"]
                    others = [f for f in FILL[n] if n1 is not None and n > 0 and f[0] != "max"]

                    def one_max():
                        if maxima:
                            fill(n1, p, *maxima.pop(0))

                    for h in range(2):
                        if n2 is not None:
                            scores(n2, 1 - p, n, h)
                        one_max()
                    if wo is not None and n == WO_SLOT + WO_GROUPS:
                        pe.wait_ge(s["proj_copied"], wo * WO_GROUPS + (WO_GROUPS + 1))
                    for f in others:
                        if f[0] != "turn":
                            fill(n1, p, *f)
                    if wo is not None and 0 <= n - WO_SLOT < WO_GROUPS:
                        if n == WO_SLOT:
                            pe.wait_ge(s["sums_copied"], n2 * 2 + 5)
                        project(wo, n3, n - WO_SLOT)
                    one_max()
                    if n2 is not None and n >= LAG:
                        output(n2, 1 - p, n - LAG)
                    one_max()
                    while maxima:
                        one_max()
                    if n1 is not None and ("turn", 0) in FILL[n]:
                        fill(n1, p, "turn", 0)
                    if n3 is not None and n == SUM_SLOT[1]:
                        pe.wait_ge(s["turn_copied"], n3 + 3 if n2 is not None else n3 + 2)
                        sums(n3, 1)
                    if n2 is not None and n == SUM_SLOT[0]:
                        if n1 is not None:
                            pe.wait_ge(s["v_copied"], n1 * 4 + 3)
                        sums(n2, 0)

            def project(b, last_pair, g):
                pe.wait_ge(s["out_done"], last_pair * 2 + 5 + g // (WO_GROUPS // 2))
                pe.wait_ge(s["proj_copied"], b * WO_GROUPS + g + 1)
                for u in range(2):
                    for pair in range(PAIRS):
                        last = pe.matmul(PR[0][:, u * D:(u + 1) * D], cat[:, pair, (2 * g + u) * P:(2 * g + u + 1) * P], Wo[:, pair, :],
                                         start=(pair == 0), stop=(pair == PAIRS - 1))
                last.then_inc(s["proj_ready"], 1)

            def end():
                pe.wait_ge(s["sums_copied"], 2 * N + 3)
                for g in range(WO_GROUPS):
                    project(B - 1, N - 1, g)

            run(pe, step, end)


H2, KV2, DH2 = 16, 4, 16
GROUP = H2 // KV2
QK2 = (H2 + KV2) * DH2
QKV2 = QK2 + KV2 * DH2
Q_PARTS = (0, 0, 0, 1, 1, 2)
K_PARTS = (0, 1, 2, 0, 1, 0)
PARTS = len(Q_PARTS)
STACK = PARTS * DH2
HEADS2 = H2 + KV2


def counted(eng, sem, base):
    n = [0]

    def link(ins):
        n[0] += 1
        ins.then_inc(sem, 1)
        eng.wait_ge(sem, base + n[0])

    return link


def project_two(nc, x, hold, w_qkv, ln1, cos2, sin2, norm_z, shift_z, V2, stack_dram):
    rows = hold.rearrange("p b k s -> p (b k s)").rearrange("p (t d) -> p t d", d=D)
    with ExitStack() as ctx:
        sb = lambda name, shape, dt=F32: ctx.enter_context(nc.sbuf_tensor(name, shape, dt))
        ps = lambda name, shape, dt=F32: ctx.enter_context(nc.psum_tensor(name, shape, dt))
        sem = lambda name: ctx.enter_context(nc.semaphore(name))
        X = sb("p_x", [P, NT, D])
        Y = sb("p_y", [P, 4, D])
        Wq = sb("p_w", [P, KD, QKV2])
        ln = sb("p_ln", [P, KD])
        cos = sb("p_cos", [P, ST_N, DH2])
        sin = sb("p_sin", [P, ST_N, DH2])
        stats = sb("p_stats", [P, NT, 6])
        small = {k: sb(f"p_{k}", [P, NT]) for k in ("mean2", "diff", "var", "std", "scale", "shift", "ratio", "hscale", "hshift")}
        ident = sb("p_ident", [P, P])
        HN = [sb(f"p_hn{i}", [P, 2, D]) for i in range(2)]
        hT = [sb(f"p_hT{i}", [P, KD, 2, P]) for i in range(2)]
        T = [ps(f"p_T{i}", [P, KD, 2, P]) for i in range(2)]
        rot = [sb(f"p_rot{i}", [P, QK2]) for i in range(4)]
        crs = [sb(f"p_crs{i}", [P, QK2]) for i in range(4)]
        stk = [sb(f"p_stk{i}", [P, HEADS2, PARTS, DH2], BF16) for i in range(4)]
        QKV = [ps(f"p_QKV{i}", [P, BANK]) for i in range(4)]
        names = ("x_in", "w_in", "id_set", "step", "ones_set", "var_ready", "std_ready", "y_ready", "y_used", "hn_ready",
                 "turned", "hT_ready", "qkv_ready", "v_copied", "crossed", "rotated", "first_set", "rest_set", "second_set",
                 "third_set")
        s = {k: sem(f"p_{k}") for k in names}
        x_in = [sem(f"p_x_in{i}") for i in range(4)]
        stored = [sem(f"p_stored{i}") for i in range(4)]
        block = ctx.enter_context(nc.Block())

        NR = NT // 2

        def pairs(eng, step):
            step(0, 0)
            with eng.Fori(0, NR // 2 - 1) as u:
                step(u * 2 + 1, 1)
                step(u * 2 + 2, 0)
            step(NR - 1, 1)

        @block.sync
        def _(sp):
            xt = x.rearrange("(t p) d -> p t d", p=P)
            for i in range(4):
                sp.dma_start(X[:, 8 * i:8 * i + 8, :], xt[:, 8 * i:8 * i + 8, :]).then_inc(x_in[i], 16)
            for dst, src in ((Wq, w_qkv), (cos, cos2), (sin, sin2)):
                sp.dma_start(dst[:, :, :], src).then_inc(s["w_in"], 16)
            sp.dma_start(ln[:, :], ln1).then_inc(s["w_in"], 16)
            with sp.Fori(0, NT // 4) as g:
                for i in range(4):
                    sp.wait_ge(s["third_set"], g * 8 + 2 * i + 10)
                    sp.dma_start(stack_dram[bass.ds(g * 4 + i, 1), :, :].rearrange("t p w -> (t p) w"),
                                 stk[i][:, :, :, :].rearrange("p h a d -> p (h a d)")).then_inc(stored[i], 16)
            for i in range(4):
                sp.wait_ge(stored[i], 16 * (NT // 4) + 1)

        @block.gpsimd
        def _(pool):
            pool.memset(ident[:, :], 0.0).then_inc(s["id_set"], 1)
            pool.wait_ge(s["id_set"], 1)
            pool.affine_select(out=ident[:, :], in_=ident[:, :], compare_op=ALU.not_equal, fill=1.0, base=0,
                               pattern=[[-1, P]], channel_multiplier=1).then_inc(s["id_set"], 1)
            pool.memset(V2, 1.0).then_inc(s["ones_set"], 1)
            with pool.Fori(0, NT // 4) as g:
                for i in range(4):
                    pool.wait_ge(s["second_set"], (g * 4 + i) * 2 + 2)
                    r = rot[i][:, :].rearrange("p (h d) -> p h d", d=DH2)
                    for lo, hi, parts in ((0, H2, Q_PARTS), (H2, HEADS2, K_PARTS)):
                        pool.tensor_tensor(stk[i][:, lo:hi, parts.index(2), :], r[:, lo:hi, :],
                                           stk[i][:, lo:hi, parts.index(1), :], ALU.subtract).then_inc(s["third_set"], 1)

        def tile_of(t, n):
            return t[:, bass.ds(n, 1), :].rearrange("p a d -> p (a d)")

        @block.vector
        def _(dve):
            sm = {k: v[:, :] for k, v in small.items()}
            for t in range(NT):
                dve.bn_stats(stats[:, t, :], rows[:, t, :]).then_inc(s["step"], 1)
            dve.wait_ge(s["step"], NT)
            link = counted(dve, s["step"], NT)
            moments(dve, link, stats, small["mean2"], small["diff"], small["var"])
            dve.sem_inc(s["var_ready"], 1)
            dve.wait_ge(s["std_ready"], 1)
            link(dve.reciprocal(sm["scale"], sm["std"]))
            link(dve.scalar_tensor_tensor(out=sm["shift"], in0=sm["mean2"], scalar=-0.5, in1=sm["scale"],
                                          op0=ALU.mult, op1=ALU.mult))
            dve.sem_inc(s["var_ready"], 1)
            dve.sem_inc(s["y_used"], 4)
            base = NT + 8
            for i in range(4):
                dve.wait_ge(x_in[i], 16)
                for f in range(2 * i, 2 * i + 2):
                    for t in range(4 * f, 4 * f + 4):
                        dve.wait_ge(s["y_ready"], t + 1)
                        dve.tensor_tensor(rows[:, t, :], Y[:, t % 4, :], X[:, t, :], ALU.add).then_inc(s["y_used"], 1)
                    for t in range(4 * f, 4 * f + 4):
                        dve.wait_ge(s["y_used"], t + 5)
                        dve.bn_stats(stats[:, t, :], rows[:, t, :]).then_inc(s["step"], 1)
            dve.wait_ge(s["step"], base + NT)
            link = counted(dve, s["step"], base + NT)
            moments(dve, link, stats, small["mean2"], small["diff"], small["var"])
            dve.sem_inc(s["var_ready"], 1)
            dve.wait_ge(s["std_ready"], 2)
            link(dve.reciprocal(norm_z, sm["std"]))
            link(dve.scalar_tensor_tensor(out=shift_z, in0=sm["mean2"], scalar=-0.5, in1=norm_z,
                                          op0=ALU.mult, op1=ALU.mult))
            link(dve.tensor_scalar(sm["diff"], sm["var"], -EPS, None, ALU.add))
            link(dve.tensor_tensor(sm["diff"], sm["diff"], norm_z, ALU.mult))
            link(dve.tensor_tensor(sm["diff"], sm["diff"], norm_z, ALU.mult))
            link(dve.tensor_scalar(sm["var"], sm["diff"], EPS, None, ALU.add))
            dve.sem_inc(s["var_ready"], 1)
            dve.wait_ge(s["std_ready"], 3)
            link(dve.reciprocal(sm["ratio"], sm["std"]))
            link(dve.tensor_tensor(sm["hscale"], norm_z, sm["ratio"], ALU.mult))
            link(dve.tensor_tensor(sm["hshift"], shift_z, sm["ratio"], ALU.mult))
            dve.wait_ge(s["w_in"], 64)
            dve.wait_ge(s["ones_set"], 1)
            for i in range(4):
                dve.sem_inc(stored[i], 1)
            dve.sem_inc(s["rotated"], 4)
            dve.sem_inc(s["third_set"], 8)

            def narrow(r, p):
                for u in range(2):
                    t = r * 2 + u
                    dve.tensor_scalar(HN[p][:, u, :], tile_of(rows, t),
                                      small["hscale"][:, bass.ds(t, 1)], small["hshift"][:, bass.ds(t, 1)],
                                      ALU.mult, ALU.add).then_inc(s["hn_ready"], 1)

            def cross(t, i):
                dve.wait_ge(s["v_copied"], t + 5)
                dve.wait_ge(s["third_set"], t * 2 + 2)
                C = cos[:, bass.ds(t % ST_N, 1), :].to_broadcast([P, HEADS2, DH2])
                qk = QKV[i][:, 0:QK2].rearrange("p (h d) -> p h d", d=DH2)
                X4 = crs[i][:, :].rearrange("p (h d) -> p h d", d=DH2)
                half = DH2 // 2
                dve.tensor_tensor(rot[i][:, :].rearrange("p (h d) -> p h d", d=DH2), qk, C, ALU.mult).then_inc(s["crossed"], 1)
                for a in range(2):
                    dve.tensor_tensor(X4[:, :, a * half:(a + 1) * half], qk[:, :, (1 - a) * half:(2 - a) * half],
                                      sin[:, bass.ds(t % ST_N, 1), a * half:(a + 1) * half].to_broadcast([P, HEADS2, half]),
                                      ALU.mult).then_inc(s["crossed"], 1)

            def rest(t, i):
                dve.wait_ge(s["first_set"], t * 3 + 3)
                r = rot[i][:, :].rearrange("p (h d) -> p h d", d=DH2)
                dve.tensor_tensor(r[:, 0:H2, :], r[:, 0:H2, :], stk[i][:, 0:H2, Q_PARTS.index(0), :], ALU.subtract).then_inc(s["rest_set"], 1)
                dve.tensor_tensor(r[:, H2:, :], r[:, H2:, :], stk[i][:, H2:, K_PARTS.index(0), :], ALU.subtract).then_inc(s["rest_set"], 1)

            def step(r, p):
                first = isinstance(r, int) and r == 0
                if not first:
                    for u in range(2):
                        rest((r - 1) * 2 + u, 2 * (1 - p) + u)
                for u in range(2):
                    cross(r * 2 + u, 2 * p + u)
                for u in range(2):
                    dve.wait_ge(s["crossed"], (r * 2 + u) * 3 + 3)
                    dve.tensor_tensor(rot[2 * p + u][:, :], rot[2 * p + u][:, :], crs[2 * p + u][:, :], ALU.add).then_inc(s["rotated"], 1)
                dve.wait_ge(s["turned"], r + 1)
                narrow((r + 2) % NR, p)

            for i in range(2):
                narrow(i, i)
            pairs(dve, step)
            for u in range(2):
                rest(NT - 2 + u, 2 + u)

        @block.scalar
        def _(act):
            act.wait_ge(s["var_ready"], 1)
            act.activation(small["std"][:, :], small["var"][:, :], ACT.Sqrt).then_inc(s["std_ready"], 1)
            act.wait_ge(s["var_ready"], 2)
            for t in range(NT):
                act.wait_ge(s["y_used"], t + 1)
                act.activation(Y[:, t % 4, :], rows[:, t, :], ACT.Identity, scale=small["scale"][:, t:t + 1],
                               bias=small["shift"][:, t:t + 1]).then_inc(s["y_ready"], 1)
            for n in range(2):
                act.wait_ge(s["var_ready"], 3 + n)
                act.activation(small["std"][:, :], small["var"][:, :], ACT.Sqrt).then_inc(s["std_ready"], 1)
            act.wait_ge(s["w_in"], 64)
            act.wait_ge(s["ones_set"], 1)
            act.sem_inc(s["v_copied"], 4)

            def feed(r, p):
                act.wait_ge(s["turned"], r + 1)
                for kt in range(KD):
                    act.activation(hT[p][:, kt, :, :], T[p][:, kt, :, :], ACT.Copy, scale=ln[:, kt:kt + 1]).then_inc(s["hT_ready"], 1)

            def values(t, i):
                act.wait_ge(s["qkv_ready"], t + 1)
                act.activation(V2[:, bass.ds(t // ST_N, 1), :, bass.ds(t % ST_N, 1), 0:DH2].rearrange("p a g b d -> p (a g) (b d)"),
                               QKV[i][:, QK2:].rearrange("p (g d) -> p g d", d=DH2)[:, 0:KV2, :], ACT.Copy).then_inc(s["v_copied"], 1)

            def first_part(t, i, turn):
                act.wait_ge(s["rotated"], t + 5)
                act.wait_ge(stored[i], turn * 16 + 1)
                r = rot[i][:, :].rearrange("p (h a d) -> p h a d", a=1, d=DH2)
                act.activation(stk[i][:, 0:H2, 0:3, :], r[:, 0:H2].to_broadcast([P, H2, 3, DH2]), ACT.Copy).then_inc(s["first_set"], 1)
                act.activation(stk[i][:, H2:, 0:4:3, :], r[:, H2:].to_broadcast([P, KV2, 2, DH2]), ACT.Copy).then_inc(s["first_set"], 1)
                act.activation(stk[i][:, H2:, 5:6, :], r[:, H2:], ACT.Copy).then_inc(s["first_set"], 1)

            def second_part(t, i):
                act.wait_ge(s["rest_set"], t * 2 + 2)
                r = rot[i][:, :].rearrange("p (h a d) -> p h a d", a=1, d=DH2)
                act.activation(stk[i][:, 0:H2, 3:5, :], r[:, 0:H2].to_broadcast([P, H2, 2, DH2]), ACT.Copy).then_inc(s["second_set"], 1)
                act.activation(stk[i][:, H2:, 1:5:3, :], r[:, H2:].to_broadcast([P, KV2, 2, DH2]), ACT.Copy).then_inc(s["second_set"], 1)

            def step(r, p):
                first = isinstance(r, int) and r == 0
                last = isinstance(r, int) and r == NR - 1
                if not first:
                    for u in range(2):
                        first_part((r - 1) * 2 + u, 2 * (1 - p) + u, (r - 1) // 2)
                for u in range(2):
                    values(r * 2 + u, 2 * p + u)
                if not last:
                    feed(r + 1, 1 - p)
                if not first:
                    for u in range(2):
                        second_part((r - 1) * 2 + u, 2 * (1 - p) + u)

            feed(0, 0)
            pairs(act, step)
            for u in range(2):
                first_part(NT - 2 + u, 2 + u, NT // 4 - 1)
            for u in range(2):
                second_part(NT - 2 + u, 2 + u)

        @block.tensor
        def _(pe):
            pe.wait_ge(s["id_set"], 2)
            pe.wait_ge(s["w_in"], 64)
            pe.sem_inc(s["hT_ready"], 2 * KD)

            def turn(r, p):
                pe.wait_ge(s["hn_ready"], r * 2 + 2)
                pe.wait_ge(s["hT_ready"], (r + 1) * KD)
                for u in range(2):
                    for kt in range(KD):
                        last = pe.transpose(T[p][:, kt, u, :], HN[p][:, u, kt * P:(kt + 1) * P], ident[:, :])
                last.then_inc(s["turned"], 1)

            def step(r, p):
                pe.wait_ge(s["hT_ready"], (r + 3) * KD)
                for u in range(2):
                    pe.wait_ge(s["rotated"], r * 2 + u + 1)
                    pe.wait_ge(s["v_copied"], r * 2 + u + 1)
                    for kt in range(KD):
                        last = pe.matmul(QKV[2 * p + u][:, 0:QKV2], hT[p][:, kt, u, :], Wq[:, kt, :], start=(kt == 0), stop=(kt == KD - 1))
                    last.then_inc(s["qkv_ready"], 1)
                if not (isinstance(r, int) and r == NR - 1):
                    turn(r + 1, 1 - p)

            pe.wait_ge(s["ones_set"], 1)
            turn(0, 0)
            pairs(pe, step)


STEPS2 = B * KV2
UNITS2 = [(c, j, h) for c, j in UNITS for h in range(GROUP)]
NU2 = len(UNITS2)
MAX2 = [(h, i, c) for h in range(GROUP) for i, c in MAXU]
LAG2 = 10
RING2 = 16
STACK_SLOTS = (0, 2, 8, 17, 26)
SCORE_BANKS, MAX_BANKS = 2, 3
TURN_SLOT, OUT_SLOTS = NU2 - 8, (16 + LAG2 + 5, LAG2 + 3)
assert STACK_SLOTS[-1] < OUT_SLOTS[0] < TURN_SLOT
FILL2 = {k: [] for k in range(NU2)}
for _n, _k in enumerate(STACK_SLOTS):
    FILL2[_k].append(("stack", _n))
for _n in range(NU2):
    FILL2[4 + _n * (TURN_SLOT - 5) // NU2].append(("max", _n))


def attention_two(nc, stack_dram, V2, A2):
    with ExitStack() as ctx:
        sb = lambda name, shape, dt=F32: ctx.enter_context(nc.sbuf_tensor(name, shape, dt))
        ps = lambda name, shape, dt=F32: ctx.enter_context(nc.psum_tensor(name, shape, dt))
        sem = lambda name: ctx.enter_context(nc.semaphore(name))
        stk = [sb(f"b_stk{i}", [P, ST_N, GROUP + 1, STACK], BF16) for i in range(2)]
        V = [sb(f"b_V{i}", [P, ST_N, 2 * DH2]) for i in range(2)]
        Q = [sb(f"b_Q{i}", [STACK + 2, GROUP, S], BF16) for i in range(2)]
        K = [sb(f"b_K{i}", [STACK + 2, S], BF16) for i in range(2)]
        probs = [sb(f"b_P{i}", [P, BANK]) for i in range(RING2)]
        OT = [sb(f"b_OT{i}", [P, BANK]) for i in range(2)]
        inv = sb("b_inv", [P, 2, GROUP, GROUP])
        peak = sb("b_peak", [P, GROUP, ST_N, 2])
        minus = sb("b_minus", [P, GROUP * ST_N])
        hi = sb("b_hi", [GROUP * ST_N, P], BF16)
        lo = sb("b_lo", [GROUP * ST_N, P], BF16)
        ident = sb("b_ident", [P, P])
        identb = sb("b_identb", [P, P], BF16)
        maskb = sb("b_maskb", [P, P], BF16)
        SC = [ps(f"b_SC{i}", [P, BANK]) for i in range(SCORE_BANKS)]
        MX = [ps(f"b_MX{i}", [P, BANK]) for i in range(MAX_BANKS)]
        O = [ps(f"b_O{i}", [P, BANK]) for i in range(2)]
        SM = ps("b_SM", [P, BANK])
        TR = SM[0:STACK, :].bitcast(BF16)
        names = ("consts", "dve_consts", "stack_ready", "stack_copied", "max_ready", "max_used", "minus_ready",
                 "turn_ready", "turn_copied", "minus_in", "scores_ready", "exp_done", "masked", "pv_done",
                 "OT_copied", "OT_ready", "inv_ready", "A2_done", "v_in", "mask_due")
        s = {k: sem(f"b_{k}") for k in names}
        loaded = [sem(f"b_loaded{i}") for i in range(2)]
        block = ctx.enter_context(nc.Block())

        def run(eng, step):
            step(0, None, None, 0)
            step(1, 0, None, 1)
            with eng.Fori(0, STEPS2 // 2 - 1) as u:
                step(u * 2 + 2, u * 2 + 1, u * 2, 0)
                step(u * 2 + 3, u * 2 + 2, u * 2 + 1, 1)
            step(None, STEPS2 - 1, STEPS2 - 2, 0)
            step(None, None, STEPS2 - 1, 1)

        @block.gpsimd
        def _(pool):
            for m in (ident, identb, maskb):
                pool.memset(m[:, :], 0.0).then_inc(s["consts"], 1)
            pool.wait_ge(s["consts"], 3)
            for m in (ident, identb):
                pool.affine_select(out=m[:, :], in_=m[:, :], compare_op=ALU.not_equal, fill=1.0, base=0,
                                   pattern=[[-1, P]], channel_multiplier=1).then_inc(s["consts"], 1)
            pool.affine_select(out=maskb[:, :], in_=maskb[:, :], compare_op=ALU.is_ge, fill=NEG, base=0,
                               pattern=[[-1, P]], channel_multiplier=1).then_inc(s["consts"], 1)

            def step(n1, n2, n3, p):
                if n2 is None:
                    return
                for k, (c, j, h) in enumerate(UNITS2):
                    if is_diag(c, j):
                        a = first_col(c, j)
                        pool.wait_ge(s["exp_done"], n2 * NU2 + k + 1 + SCORE_BANKS)
                        pool.sem_inc(s["mask_due"], 1)
                        pool.affine_select(out=probs[k % RING2][:, a:a + P], in_=probs[k % RING2][:, a:a + P],
                                           compare_op=ALU.is_ge, fill=0.0, base=0, pattern=[[1, P]],
                                           channel_multiplier=-1).then_inc(s["masked"], 1)

            run(pool, step)

        @block.sync
        def _(sp):
            def load(n, p):
                b, g = n // KV2, n % KV2
                src = stack_dram.rearrange("(b t) p (h w) -> b p t h w", b=B, w=STACK)[bass.ds(b, 1)].rearrange("b p t h w -> (b p) t h w")
                for t in range(ST_N):
                    sp.dma_start(stk[p][:, t, 0:GROUP, :], src[:, t, bass.ds(g * GROUP, GROUP), :]).then_inc(loaded[p], 16)
                sp.dma_start(stk[p][:, :, GROUP:, :].rearrange("p t h w -> p t (h w)"), src[:, :, bass.ds(g + H2, 1), :].rearrange("p t h w -> p t (h w)")).then_inc(loaded[p], 16)

            load(0, 0)

            def step(n1, n2, n3, p):
                if n1 is not None:
                    sp.wait_ge(s["stack_ready"], n1 * (GROUP + 1) + 1)
                    b, g = n1 // KV2, n1 % KV2
                    if n3 is not None:
                        sp.wait_ge(s["pv_done"], n3 * NU2 + NU2 + RING2)
                    sp.dma_start(V[p][:, :, :], V2[:, bass.ds(b, 1), bass.ds(g, 1), :, :].rearrange(
                        "p b g t w -> p (b g t) w")).then_inc(s["v_in"], 16)
                    load((n1 + 1) % STEPS2, 1 - p)
                    sp.wait_ge(s["turn_copied"], n1 * 2 + 3)
                    for n, part in enumerate((hi, lo)):
                        sp.dma_start(Q[p][STACK + n:STACK + n + 1, :, :].rearrange("p h s -> p (h s)"), part[:, :]).then_inc(s["minus_in"], 16)

            run(sp, step)
            sp.wait_ge(loaded[0], 144 * (STEPS2 // 2 + 1))

        @block.scalar
        def _(act):
            act.sem_inc(s["exp_done"], SCORE_BANKS)
            act.sem_inc(s["stack_copied"], 1)
            act.sem_inc(s["OT_copied"], 2)

            def turn_out(n2, c):
                act.wait_ge(s["pv_done"], n2 * NU2 + (16 if c == 0 else NU2) + RING2)
                act.wait_ge(s["OT_ready"], n2 * 2 + c + 1)
                act.activation(OT[c][:, :], O[c][:, :], ACT.Copy).then_inc(s["OT_copied"], 1)

            def step(n1, n2, n3, p):
                for k, (c, j, h) in enumerate(UNITS2):
                    if n2 is not None:
                        a = first_col(c, j)
                        act.wait_ge(s["scores_ready"], n2 * NU2 + k + 1)
                        act.wait_ge(s["pv_done"], n2 * NU2 + k + 1)
                        act.activation(probs[k % RING2][:, a:], SC[k % SCORE_BANKS][:, a:], ACT.Exp,
                                       scale=DH2 ** -0.5).then_inc(s["exp_done"], 1)
                        if k == 16 + LAG2:
                            turn_out(n2, 0)
                    if n1 is not None:
                        for what, n in FILL2[k]:
                            if what == "stack":
                                act.wait_ge(s["stack_ready"], n1 * (GROUP + 1) + n + 1)
                                dst = K[p][0:STACK, :] if n == 0 else Q[p][0:STACK, n - 1, :]
                                act.activation(dst, TR, ACT.Copy).then_inc(s["stack_copied"], 1)
                    if n3 is not None and k == LAG2 + 1:
                        turn_out(n3, 1)

            run(act, step)

        @block.vector
        def _(dve):
            dve.memset(peak[:, :, :, :], 3 * NEG).then_inc(s["dve_consts"], 1)
            for i in range(2):
                dve.memset(K[i][STACK:, :], 1.0).then_inc(s["dve_consts"], 1)
            dve.wait_ge(s["dve_consts"], 3)
            dve.sem_inc(s["max_used"], MAX_BANKS)
            dve.sem_inc(s["turn_copied"], 1)
            dve.sem_inc(s["minus_in"], 1)
            dve.sem_inc(s["A2_done"], 1)

            def rows_out(n2, c):
                b, g = n2 // KV2, n2 % KV2
                dve.wait_ge(s["OT_ready"], n2 * 2 + c + 3)
                O4 = SM[:, :].rearrange("p (t h w) -> p t h w", t=4, h=GROUP)
                dve.reciprocal(inv[:, c, :, :], O4[:, :, :, DH2]).then_inc(s["inv_ready"], 1)
                dve.wait_ge(s["inv_ready"], n2 * 2 + c + 1)
                dve.tensor_tensor(A2[:, bass.ds(b * ST_N + 4 * c, 4), bass.ds(g * (GROUP * DH2), GROUP * DH2)].rearrange(
                    "p t (h d) -> p t h d", h=GROUP), O4[:, :, :, 0:DH2],
                    inv[:, c, :, :].rearrange("p t (h a) -> p t h a", a=1).to_broadcast([P, 4, GROUP, DH2]), ALU.mult).then_inc(s["A2_done"], 1)

            def step(n1, n2, n3, p):
                for k in range(NU2):
                    if n1 is not None:
                        for what, n in FILL2[k]:
                            if what == "max":
                                h, i, ch = MAX2[n]
                                w = min(BANK, (i + 1) * P - ch * BANK)
                                dve.wait_ge(s["max_ready"], n1 * NU2 + n + 1)
                                dve.tensor_reduce(peak[:, h, i, ch:ch + 1], MX[n % MAX_BANKS][:, 0:w], AX.X, ALU.max).then_inc(s["max_used"], 1)
                    for c, m in ((0, n2), (1, n3)):
                        if m is not None and k == OUT_SLOTS[c] + 2:
                            rows_out(m, c)
                    if n1 is not None and k == TURN_SLOT - 1:
                        dve.wait_ge(s["max_used"], n1 * NU2 + NU2 + MAX_BANKS)
                        dve.tensor_reduce(minus[:, :].rearrange("p (h i) -> p h i", h=GROUP), peak[:, :, :, :],
                                          AX.X, ALU.max, negate=True).then_inc(s["minus_ready"], 1)
                    if n1 is not None and k == TURN_SLOT:
                        dve.wait_ge(s["turn_ready"], n1 + 1)
                        dve.wait_ge(s["minus_in"], n1 * 32 + 1)
                        T = SM[0:GROUP * ST_N, 0:P]
                        dve.tensor_copy(hi[:, :], T).then_inc(s["turn_copied"], 1)
                        dve.wait_ge(s["turn_copied"], n1 * 2 + 2)
                        dve.tensor_tensor(lo[:, :], T, hi[:, :], ALU.subtract).then_inc(s["turn_copied"], 1)

            run(dve, step)

        @block.tensor
        def _(pe):
            pe.wait_ge(s["consts"], 6)
            pe.wait_ge(s["dve_consts"], 3)
            pe.sem_inc(s["pv_done"], RING2)
            pe.sem_inc(s["OT_ready"], 2)

            def scores(n2, p2, k):
                c, j, h = UNITS2[k]
                a = first_col(c, j)
                if k == 0:
                    pe.wait_ge(s["minus_in"], n2 * 32 + 33)
                    pe.wait_ge(s["v_in"], n2 * 16 + 16)
                pe.wait_ge(s["exp_done"], n2 * NU2 + k + 1)
                pe.matmul(SC[k % SCORE_BANKS][:, a:], K[p2][:, j * P:(j + 1) * P], Q[p2][:, h, c * BANK + a:(c + 1) * BANK],
                          start=True, stop=True).then_inc(s["scores_ready"], 1)

            def output(n2, p2, k):
                c, j, h = UNITS2[k]
                a = first_col(c, j)
                if (j, h) == (0, 0):
                    pe.wait_ge(s["OT_copied"], n2 * 2 + c + 1)
                pe.wait_ge(s["exp_done"], n2 * NU2 + k + 1 + SCORE_BANKS)
                if is_diag(c, j):
                    pe.wait_ge(s["masked"], n2 * (GROUP * ST_N) + j * GROUP + h + 1)
                pe.matmul(O[c][32 * h:32 * h + 32, a:], V[p2][:, j, :], probs[k % RING2][:, a:], start=(j == 0),
                          stop=(j == (c + 1) * 4 - 1)).then_inc(s["pv_done"], 1)

            def turn_out(n, c, turned, stacks):
                pe.wait_ge(s["OT_copied"], n * 2 + c + 3)
                pe.wait_ge(s["turn_copied"], turned * 2 + 1)
                if stacks is not None:
                    pe.wait_ge(s["stack_copied"], stacks + 1)
                pe.wait_ge(s["A2_done"], n * 2 + c + 1)
                for t in range(4):
                    last = pe.transpose(SM[:, t * P:(t + 1) * P], OT[c][:, t * P:(t + 1) * P], ident[:, :])
                last.then_inc(s["OT_ready"], 1)

            def fill(n1, n3, p, what, n):
                if what == "stack":
                    if n == 0:
                        pe.wait_ge(loaded[p], (n1 - p) * 72 + 144)
                    pe.wait_ge(s["stack_copied"], n1 * (GROUP + 1) + n + 1)
                    if n == 0:
                        pe.wait_ge(s["turn_copied"], n1 * 2 + 1)
                    if n3 is not None and STACK_SLOTS[n] > OUT_SLOTS[1] > STACK_SLOTS[n - 1]:
                        pe.wait_ge(s["A2_done"], n3 * 2 + 3)
                    for t in range(ST_N):
                        last = pe.transpose(TR[:, t * P:(t + 1) * P], stk[p][:, t, (n - 1) % (GROUP + 1), :], identb[:, :])
                    last.then_inc(s["stack_ready"], 1)
                else:
                    h, i, ch = MAX2[n]
                    w = min(BANK, (i + 1) * P - ch * BANK)
                    diag = ch == i * P // BANK
                    if (i, ch) == MAXU[0]:
                        pe.wait_ge(s["stack_copied"], n1 * (GROUP + 1) + h + 3)
                    pe.wait_ge(s["max_used"], n1 * NU2 + n + 1)
                    last = pe.matmul(MX[n % MAX_BANKS][:, 0:w], Q[p][0:STACK, h, i * P:(i + 1) * P],
                                     K[p][0:STACK, ch * BANK:ch * BANK + w], start=True, stop=not diag)
                    if diag:
                        last = pe.matmul(MX[n % MAX_BANKS][:, w - P:w], identb[:, :], maskb[:, :], start=False, stop=True)
                    last.then_inc(s["max_ready"], 1)

            def step(n1, n2, n3, p):
                for k in range(NU2):
                    if n3 is not None and k < LAG2:
                        output(n3, p, NU2 - LAG2 + k)
                    if n2 is not None and k > 0:
                        scores(n2, 1 - p, k)
                    if n1 is not None:
                        for f in FILL2[k]:
                            fill(n1, n3, p, *f)
                    if n2 is not None:
                        if k == 0:
                            scores(n2, 1 - p, 0)
                        if k >= LAG2:
                            output(n2, 1 - p, k - LAG2)
                        if k == OUT_SLOTS[0]:
                            turn_out(n2, 0, n2 + 1, None if n1 is None else (n1 + 1) * (GROUP + 1))
                    if n3 is not None and k == OUT_SLOTS[1]:
                        turn_out(n3, 1, n3 + 2 if n2 is not None else n3 + 1,
                                 None if n1 is None else n1 * (GROUP + 1) + sum(x < OUT_SLOTS[1] for x in STACK_SLOTS))
                    if n1 is not None and k == TURN_SLOT:
                        pe.wait_ge(s["minus_ready"], n1 + 1)
                        pe.wait_ge(s["stack_copied"], (n1 + 1) * (GROUP + 1) + 1)
                        if n2 is not None:
                            pe.wait_ge(s["A2_done"], n2 * 2 + 2)
                        pe.transpose(SM[0:GROUP * ST_N, 0:P], minus[:, :], ident[:, :]).then_inc(s["turn_ready"], 1)

            run(pe, step)


EXPERTS, FFN = 8, 512
KF = FFN // P
SLOTS = (2 * TOK + EXPERTS * (P - 1)) // P
SLOTS += SLOTS % 2
ZEROS = 12


def route(nc, hold, norm_z, shift_z, A2, w_out, ln2, w_gate, sorted_rows, weight, place, expert_of, W13, w13,
          w13_in):
    rows = hold.rearrange("p b k s -> p (b k s)").rearrange("p (t d) -> p t d", d=D)
    with ExitStack() as ctx:
        sb = lambda name, shape, dt=F32: ctx.enter_context(nc.sbuf_tensor(name, shape, dt))
        ps = lambda name, shape, dt=F32: ctx.enter_context(nc.psum_tensor(name, shape, dt))
        sem = lambda name: ctx.enter_context(nc.semaphore(name))
        Wo = sb("r_Wo", [P, KD, D])
        Wg = sb("r_Wg", [P, KD, EXPERTS])
        ln = sb("r_ln", [P, KD])
        ident = sb("r_ident", [P, P])
        before = sb("r_before", [P, P], BF16)
        ones = sb("r_ones", [P, P], BF16)
        H = sb("r_H", [P, NT, D])
        zeros = sb("r_zeros", [P, ZEROS, D])
        stage = [sb(f"r_stage{i}", [P, 2, D]) for i in range(2)]
        HN = [sb(f"r_HN{i}", [P, 2, D]) for i in range(2)]
        hT = [sb(f"r_hT{i}", [P, KD, 2, P]) for i in range(2)]
        Z = [sb(f"r_Z{i}", [P, 2, D]) for i in range(2)]
        square = sb("r_square", [P, D])
        total = sb("r_total", [P, NT])
        std = sb("r_std", [P, NT])
        logits = sb("r_logits", [P, NT, EXPERTS])
        rank = sb("r_rank", [P, NT, EXPERTS])
        slots = sb("r_slots", [P, SLOTS])
        small = {k: sb(f"r_{k}", [P, NT, EXPERTS]) for k in ("a", "b", "first", "second", "sa", "sb", "pos")}
        count = sb("r_count", [P, NT, EXPERTS], BF16)
        col = {k: sb(f"r_c_{k}", [P, NT]) for k in ("m1", "m2", "top", "e")}
        ex = {k: sb(f"r_e_{k}", [P, EXPERTS]) for k in ("tiles", "end", "end2", "start")}
        exi = sb("r_exi", [P, EXPERTS], mybir.dt.int32)
        cmp = sb("r_cmp", [1, SLOTS, EXPERTS - 1])
        eidx = sb("r_eidx", [1, SLOTS])
        T = [ps(f"r_T{i}", [P, KD, 2, P]) for i in range(2)]
        Y = [ps(f"r_Y{i}", [P, 2, D]) for i in range(2)]
        CT = [ps(f"r_CT{i}", [P, BANK]) for i in range(2)]
        names = ("w_in", "consts", "zeros_set", "zeroed", "turned", "hT_ready", "y_ready", "x2_ready", "z_ready", "summed", "var_ready", "std_ready",
                 "h_ready", "lg_ready", "lg_copied", "step", "counted", "prefix_ready", "gap_ready", "share_ready", "placed", "scattered")
        s = {k: sem(f"r_{k}") for k in names}
        staged = [sem(f"r_staged{i}") for i in range(2)]
        kept = [sem(f"r_kept{i}") for i in range(2)]
        block = ctx.enter_context(nc.Block())

        def tile_of(t, n):
            return t[:, bass.ds(n, 1), :].rearrange("p a d -> p (a d)")

        def pair_of(t, n):
            return t[:, bass.ds(n * 2, 2), :]

        NR = NT // 2

        @block.sync
        def _(sp):
            for i in range(2):
                sp.dma_start(stage[i][:, :, :], A2[:, 2 * i:2 * i + 2, :]).then_inc(staged[i], 16)
            for dst, src in ((Wo, w_out), (Wg, w_gate)):
                sp.dma_start(dst[:, :, :], src).then_inc(s["w_in"], 16)
            sp.dma_start(ln[:, :], ln2).then_inc(s["w_in"], 16)
            sp.wait_ge(s["zeros_set"], 1)

            def stage_in(g):
                for i in range(2):
                    sp.wait_ge(s["turned"], g * 2 + i + 1)
                    sp.dma_start(stage[i][:, :, :], pair_of(A2, g * 2 + (2 + i))).then_inc(staged[i], 16)

            with sp.Fori(0, SLOTS // ZEROS) as g:
                stage_in(g)
                sp.dma_start(sorted_rows.rearrange("(n p) d -> p n d", p=P)[:, bass.ds(g * ZEROS, ZEROS), :],
                             zeros[:, :, :]).then_inc(s["zeroed"], 16)
            with sp.Fori(SLOTS // ZEROS, NR // 2 - 1) as g:
                stage_in(g)
            with sp.Fori(0, NR // 2) as g:
                for i in range(2):
                    sp.wait_ge(s["h_ready"], (g * 2 + i) * 2 + 2)
                    sp.dma_start(pair_of(H, g * 2 + i), HN[i][:, :, :]).then_inc(kept[i], 16)
            for e in range(EXPERTS):
                sp.dma_start(W13[:, e, :, :], w13[:, e, :, :]).then_inc(w13_in, 16)

        @block.gpsimd
        def _(pool):
            pool.memset(zeros[:, :, :], 0.0).then_inc(s["zeros_set"], 1)
            pool.memset(ident[:, :], 0.0).then_inc(s["consts"], 1)
            pool.memset(before[:, :], 1.0).then_inc(s["consts"], 1)
            pool.memset(ones[:, :], 1.0).then_inc(s["consts"], 1)
            pool.iota(slots[:, :], pattern=[[1, SLOTS]], base=0, channel_multiplier=0,
                      allow_small_or_imprecise_dtypes=True).then_inc(s["consts"], 1)
            for e in range(EXPERTS):
                pool.memset(rank[:, :, e:e + 1], float(EXPERTS - e)).then_inc(s["consts"], 1)
            pool.wait_ge(s["consts"], 4 + EXPERTS)
            pool.affine_select(out=ident[:, :], in_=ident[:, :], compare_op=ALU.not_equal, fill=1.0, base=0,
                               pattern=[[-1, P]], channel_multiplier=1).then_inc(s["consts"], 1)
            pool.affine_select(out=before[:, :], in_=before[:, :], compare_op=ALU.is_gt, fill=0.0, base=0,
                               pattern=[[1, P]], channel_multiplier=-1).then_inc(s["consts"], 1)
            pool.wait_ge(s["placed"], 1)
            pool.wait_ge(s["zeroed"], 16 * (SLOTS // ZEROS))
            for i in range(2):
                pool.wait_ge(kept[i], 16 * (NR // 2) + 1)
            for t in range(NT):
                for k in range(2):
                    pool.indirect_dma_start(out=sorted_rows, out_offset=bass.IndirectOffsetOnAxis(ap=place[:, k, t:t + 1], axis=0),
                                            in_=H[:, t, :], in_offset=None).then_inc(s["scattered"], 16)
            pool.wait_ge(s["scattered"], 16 * 2 * NT)

        @block.tensor
        def _(pe):
            pe.wait_ge(s["consts"], 6 + EXPERTS)
            pe.wait_ge(s["w_in"], 48)
            pe.sem_inc(s["hT_ready"], 4)
            pe.sem_inc(s["x2_ready"], 2)
            def turn(src, i):
                for u in range(2):
                    for kt in range(KD):
                        last = pe.transpose(T[i][:, kt, u, :], src[i][:, u, kt * P:(kt + 1) * P], ident[:, :])
                last.then_inc(s["turned"], 1)

            with pe.Fori(0, NR // 2) as g:
                for i in range(2):
                    r = g * 2 + i
                    pe.wait_ge(staged[i], g * 16 + 16)
                    pe.wait_ge(s["hT_ready"], r * 2 + 2)
                    turn(stage, i)
                for i in range(2):
                    r = g * 2 + i
                    pe.wait_ge(s["hT_ready"], r * 2 + 6)
                    pe.wait_ge(s["x2_ready"], r + 1)
                    for u in range(2):
                        for kt in range(KD):
                            last = pe.matmul(Y[i][:, u, :], hT[i][:, kt, u, :], Wo[:, kt, :], start=(kt == 0), stop=(kt == KD - 1))
                    last.then_inc(s["y_ready"], 1)
            with pe.Fori(0, NR // 2) as g:
                for i in range(2):
                    r = g * 2 + i
                    pe.wait_ge(s["h_ready"], r * 2 + 2)
                    pe.wait_ge(s["hT_ready"], r * 2 + (2 * NR + 2))
                    turn(HN, i)
                for i in range(2):
                    r = g * 2 + i
                    pe.wait_ge(s["hT_ready"], r * 2 + (2 * NR + 6))
                    pe.wait_ge(s["x2_ready"], NR + 2)
                    pe.wait_ge(s["lg_copied"], r + 1)
                    for u in range(2):
                        for kt in range(KD):
                            last = pe.matmul(Y[i][:, u, 0:EXPERTS], hT[i][:, kt, u, :], Wg[:, kt, :], start=(kt == 0),
                                             stop=(kt == KD - 1))
                    last.then_inc(s["lg_ready"], 1)
            pe.wait_ge(s["counted"], 1)
            flat = count[:, :, :].rearrange("p t e -> p (t e)")
            pe.matmul(CT[0][:, 0:NT * EXPERTS], before[:, :], flat, start=True, stop=True).then_inc(s["prefix_ready"], 1)
            pe.matmul(CT[1][:, 0:NT * EXPERTS], ones[:, :], flat, start=True, stop=True).then_inc(s["prefix_ready"], 1)

        @block.scalar
        def _(act):
            act.wait_ge(s["w_in"], 48)
            act.activation(square[:, 0:KD], ln[:, :], ACT.Square).then_inc(s["summed"], 1)
            with act.Fori(0, NR // 2) as g:
                for i in range(2):
                    act.wait_ge(s["turned"], g * 2 + i + 1)
                    act.activation(hT[i][:, :, :, :], T[i][:, :, :, :], ACT.Copy).then_inc(s["hT_ready"], 2)
                for i in range(2):
                    r = g * 2 + i
                    act.wait_ge(s["x2_ready"], r + 3)
                    for u in range(2):
                        act.wait_ge(s["summed"], r * 2 + u + 1)
                        act.activation(square[:, :], tile_of(A2, r * 2 + u), ACT.Square,
                                       accum_out=total[:, bass.ds(r * 2 + u, 1)]).then_inc(s["summed"], 1)
            act.wait_ge(s["var_ready"], 1)
            act.activation(std[:, :], total[:, :], ACT.Sqrt).then_inc(s["std_ready"], 1)
            with act.Fori(0, NR // 2) as g:
                for i in range(2):
                    act.wait_ge(s["turned"], g * 2 + i + (NR + 1))
                    for kt in range(KD):
                        act.activation(hT[i][:, kt, :, :], T[i][:, kt, :, :], ACT.Copy,
                                       scale=ln[:, kt:kt + 1]).then_inc(s["hT_ready"], 1)
                for i in range(2):
                    act.wait_ge(s["lg_ready"], g * 2 + i + 1)
                    act.activation(pair_of(logits, g * 2 + i), Y[i][:, :, 0:EXPERTS], ACT.Copy).then_inc(s["lg_copied"], 1)
            act.wait_ge(s["gap_ready"], 1)
            act.activation(col["e"][:, :], col["e"][:, :], ACT.Exp).then_inc(s["share_ready"], 1)

        @block.vector
        def _(dve):
            dve.sem_inc(s["lg_copied"], 2)
            for i in range(2):
                dve.sem_inc(kept[i], 1)
            with dve.Fori(0, NR // 2) as g:
                for i in range(2):
                    r = g * 2 + i
                    dve.wait_ge(s["x2_ready"], r + 1)
                    for u in range(2):
                        t = r * 2 + u
                        dve.tensor_scalar(Z[i][:, u, :], tile_of(rows, t), norm_z[:, bass.ds(t, 1)], shift_z[:, bass.ds(t, 1)],
                                          ALU.mult, ALU.add).then_inc(s["z_ready"], 1)
                for i in range(2):
                    r = g * 2 + i
                    dve.wait_ge(s["z_ready"], r * 2 + 2)
                    dve.wait_ge(s["y_ready"], r + 1)
                    dve.tensor_tensor(pair_of(A2, r), Z[i][:, :, :], Y[i][:, :, :], ALU.add).then_inc(s["x2_ready"], 1)
            link = counted(dve, s["step"], 0)
            dve.wait_ge(s["summed"], NT + 1)
            link(dve.tensor_scalar(total[:, :], total[:, :], 1.0 / D, EPS, ALU.mult, ALU.add))
            dve.sem_inc(s["var_ready"], 1)
            dve.wait_ge(s["std_ready"], 1)
            link(dve.reciprocal(std[:, :], std[:, :]))
            with dve.Fori(0, NR // 2) as g:
                for i in range(2):
                    r = g * 2 + i
                    dve.wait_ge(s["turned"], r + (NR - 1))
                    dve.wait_ge(kept[i], g * 16 + 1)
                    for u in range(2):
                        dve.tensor_scalar(HN[i][:, u, :], tile_of(A2, r * 2 + u), std[:, bass.ds(r * 2 + u, 1)], None,
                                          ALU.mult).then_inc(s["h_ready"], 1)
            dve.wait_ge(s["lg_copied"], NR + 2)
            dve.wait_ge(s["consts"], 6 + EXPERTS)
            v = {k: x[:, :, :] for k, x in small.items()}
            c = {k: x[:, :] for k, x in col.items()}
            L = logits[:, :, :]

            def wide(x):
                return x.rearrange("p (t a) -> p t a", a=1).to_broadcast([P, NT, EXPERTS])

            def best(scores, out, peak):
                link(dve.tensor_reduce(peak, scores, AX.X, ALU.max))
                link(dve.tensor_tensor(v["a"], scores, wide(peak), ALU.is_equal))
                link(dve.tensor_tensor(v["a"], v["a"], rank[:, :, :], ALU.mult))
                link(dve.tensor_reduce(c["top"], v["a"], AX.X, ALU.max))
                link(dve.tensor_tensor(out, v["a"], wide(c["top"]), ALU.is_equal))

            best(L, v["first"], c["m1"])
            link(dve.scalar_tensor_tensor(out=v["b"], in0=v["first"], scalar=3 * NEG, in1=L, op0=ALU.mult, op1=ALU.add))
            best(v["b"], v["second"], c["m2"])
            link(dve.tensor_tensor(c["e"], c["m2"], c["m1"], ALU.subtract))
            dve.sem_inc(s["gap_ready"], 1)
            link(dve.tensor_tensor(count[:, :, :], v["first"], v["second"], ALU.add))
            dve.sem_inc(s["counted"], 1)
            dve.wait_ge(s["share_ready"], 1)
            link(dve.tensor_scalar(c["top"], c["e"], 1.0, None, ALU.add))
            link(dve.reciprocal(weight[:, 0, :], c["top"]))
            link(dve.tensor_tensor(weight[:, 1, :], weight[:, 0, :], c["e"], ALU.mult))
            dve.wait_ge(s["prefix_ready"], 2)
            tot = CT[1][:, 0:NT * EXPERTS].rearrange("p (t e) -> p t e", e=EXPERTS)
            link(dve.tensor_copy(v["sa"], tot))
            a, b = "sa", "sb"
            gap = 1
            while gap < NT:
                link(dve.tensor_copy(v[b][:, 0:gap], v[a][:, 0:gap]))
                link(dve.tensor_tensor(v[b][:, gap:], v[a][:, gap:], v[a][:, 0:NT - gap], ALU.add))
                a, b = b, a
                gap *= 2
            n = v[a][:, NT - 1]
            link(dve.tensor_scalar(exi[:, :], n, (P - 1) / 1.0 - P / 2 + 0.5, 1.0 / P, ALU.add, ALU.mult))
            link(dve.tensor_copy(ex["tiles"][:, :], exi[:, :]))
            link(dve.tensor_copy(ex["end"][:, :], ex["tiles"][:, :]))
            p, q = "end", "end2"
            gap = 1
            while gap < EXPERTS:
                link(dve.tensor_copy(ex[q][:, 0:gap], ex[p][:, 0:gap]))
                link(dve.tensor_tensor(ex[q][:, gap:], ex[p][:, gap:], ex[p][:, 0:EXPERTS - gap], ALU.add))
                p, q = q, p
                gap *= 2
            link(dve.tensor_tensor(ex["start"][:, :], ex[p][:, :], ex["tiles"][:, :], ALU.subtract))
            link(dve.tensor_scalar(ex["start"][:, :], ex["start"][:, :], float(P), None, ALU.mult))
            link(dve.tensor_tensor(v["pos"], v[a], tot, ALU.subtract))
            pre = CT[0][:, 0:NT * EXPERTS].rearrange("p (t e) -> p t e", e=EXPERTS)
            link(dve.tensor_tensor(v["pos"], v["pos"], pre, ALU.add))
            link(dve.tensor_tensor(v["pos"], v["pos"], ex["start"][:, :].rearrange("p (a e) -> p a e", a=1).to_broadcast([P, NT, EXPERTS]),
                                   ALU.add))
            for k, pick in enumerate(("first", "second")):
                link(dve.tensor_tensor(v["a"], v["pos"], v[pick], ALU.mult))
                link(dve.tensor_reduce(c["top"], v["a"], AX.X, ALU.add))
                link(dve.tensor_copy(place[:, k, :], c["top"]))
            dve.sem_inc(s["placed"], 1)
            link(dve.tensor_tensor(cmp[:, :, :], slots[0:1, :].rearrange("p (t a) -> p t a", a=1).to_broadcast([1, SLOTS, EXPERTS - 1]),
                                   ex[p][0:1, 0:EXPERTS - 1].rearrange("p (a e) -> p a e", a=1).to_broadcast([1, SLOTS, EXPERTS - 1]),
                                   ALU.is_ge))
            link(dve.tensor_reduce(eidx[:, :], cmp[:, :, :], AX.X, ALU.add))
            link(dve.tensor_copy(expert_of, eidx[:, :]))


def experts(nc, sorted_rows, done_rows, W13, w13_in, w2, ln2, expert_of):
    with ExitStack() as ctx:
        sb = lambda name, shape, dt=F32: ctx.enter_context(nc.sbuf_tensor(name, shape, dt))
        ps = lambda name, shape, dt=F32: ctx.enter_context(nc.psum_tensor(name, shape, dt))
        sem = lambda name: ctx.enter_context(nc.semaphore(name))
        W2 = sb("e_W2", [P, EXPERTS, KF, D])
        ln = sb("e_ln", [P, KD])
        ident = sb("e_ident", [P, P])
        G = [sb(f"e_G{i}", [P, D]) for i in range(2)]
        hT = [sb(f"e_hT{i}", [P, KD, P]) for i in range(2)]
        gate = [sb(f"e_gate{i}", [P, FFN]) for i in range(2)]
        act_T = [sb(f"e_actT{i}", [P, KF, P]) for i in range(2)]
        out = [sb(f"e_out{i}", [P, D]) for i in range(2)]
        T = ps("e_T", [P, BANK])
        GU = [[ps(f"e_GU{i}{k}", [P, BANK]) for k in range(2)] for i in range(2)]
        AT = ps("e_AT", [P, BANK])
        Y = [ps(f"e_Y{i}", [P, BANK]) for i in range(2)]
        names = ("w2_in", "ln_in", "consts", "turned", "hT_ready", "gu_ready", "gated", "act_ready", "at_ready", "actT_ready",
                 "y_ready", "y_copied")
        s = {k: sem(f"e_{k}") for k in names}
        rows_in = [sem(f"e_rows_in{i}") for i in range(2)]
        stored = [sem(f"e_stored{i}") for i in range(2)]
        block = ctx.enter_context(nc.Block())

        def slot(t, n):
            return t.rearrange("(n p) d -> n p d", p=P)[bass.ds(n, 1)].rearrange("n p d -> (n p) d")

        @block.sync
        def _(sp):
            sp.dma_start(ln[:, :], ln2).then_inc(s["ln_in"], 16)
            for i in range(2):
                sp.dma_start(G[i][:, :], sorted_rows[i * P:(i + 1) * P, :]).then_inc(rows_in[i], 16)
            for e in range(EXPERTS):
                sp.dma_start(W2[:, e, :, :], w2[:, e, :, :]).then_inc(s["w2_in"], 16)
            with sp.Fori(0, SLOTS // 2) as g:
                for i in range(2):
                    sp.wait_ge(s["turned"], g * 2 + i + 1)
                    sp.dma_start(G[i][:, :], slot(sorted_rows, (g * 2 + (2 + i)) % SLOTS)).then_inc(rows_in[i], 16)
            for i in range(2):
                sp.wait_ge(stored[i], 16 * (SLOTS // 2) + 1)
                sp.wait_ge(rows_in[i], 16 * (SLOTS // 2 + 1))

        @block.gpsimd
        def _(pool):
            pool.memset(ident[:, :], 0.0).then_inc(s["consts"], 1)
            pool.wait_ge(s["consts"], 1)
            pool.affine_select(out=ident[:, :], in_=ident[:, :], compare_op=ALU.not_equal, fill=1.0, base=0,
                               pattern=[[-1, P]], channel_multiplier=1).then_inc(s["consts"], 1)

        @block.tensor
        def _(pe):
            pe.wait_ge(s["consts"], 2)
            pe.sem_inc(s["hT_ready"], 1)
            pe.sem_inc(s["gated"], 2)
            pe.sem_inc(s["actT_ready"], 1)
            pe.sem_inc(s["y_copied"], 2)

            def turn(n, i):
                pe.wait_ge(rows_in[i], (n - i) * 8 + 16)
                pe.wait_ge(s["hT_ready"], n * 2 + 1)
                for kt in range(KD):
                    last = pe.transpose(T[:, kt * P:(kt + 1) * P], G[i][:, kt * P:(kt + 1) * P], ident[:, :])
                last.then_inc(s["turned"], 1)

            def up(n, i, e):
                pe.wait_ge(s["hT_ready"], n * 2 + 3)
                pe.wait_ge(s["gated"], n + 1)
                for half in range(2):
                    for kt in range(KD):
                        last = pe.matmul(GU[i][half][:, :], hT[i][:, kt, :],
                                         W13[:, bass.ds(e, 1), kt, half * FFN:(half + 1) * FFN].rearrange("p a f -> p (a f)"),
                                         start=(kt == 0), stop=(kt == KD - 1))
                    last.then_inc(s["gu_ready"], 1)

            def turn_act(n, i):
                pe.wait_ge(s["gated"], n + 3)
                pe.wait_ge(s["actT_ready"], n + 1)
                for kt in range(KF):
                    last = pe.transpose(AT[:, kt * P:(kt + 1) * P], gate[i][:, kt * P:(kt + 1) * P], ident[:, :])
                last.then_inc(s["at_ready"], 1)

            def down(n, i, e):
                pe.wait_ge(s["actT_ready"], n + 2)
                pe.wait_ge(s["y_copied"], n + 1)
                for kt in range(KF):
                    last = pe.matmul(Y[i][:, 0:D], act_T[i][:, kt, :], W2[:, bass.ds(e, 1), kt, :].rearrange("p a d -> p (a d)"),
                                     start=(kt == 0), stop=(kt == KF - 1))
                last.then_inc(s["y_ready"], 1)

            def expert(n):
                return pe.value_load(expert_of[0:1, bass.ds(n, 1)], min_val=0, max_val=EXPERTS - 1)

            def half(m, i):
                e_down, e_up = expert(m - 1), expert(m + 1)
                turn(m + 1, 1 - i)
                down(m - 1, 1 - i, e_down)
                turn_act(m, i)
                up(m + 1, 1 - i, e_up)

            turn(0, 0)
            pe.wait_ge(w13_in, 16 * EXPERTS)
            up(0, 0, expert(0))
            turn(1, 1)
            turn_act(0, 0)
            up(1, 1, expert(1))
            pe.wait_ge(s["w2_in"], 16 * EXPERTS)
            with pe.Fori(0, SLOTS // 2 - 1) as g:
                half(g * 2 + 1, 1)
                half(g * 2 + 2, 0)
            down(SLOTS - 2, 0, expert(SLOTS - 2))
            turn_act(SLOTS - 1, 1)
            down(SLOTS - 1, 1, expert(SLOTS - 1))

        @block.scalar
        def _(act):
            act.wait_ge(s["ln_in"], 16)

            def feed(n, i):
                act.wait_ge(s["turned"], n + 1)
                for kt in range(KD):
                    act.activation(hT[i][:, kt, :], T[:, kt * P:(kt + 1) * P], ACT.Copy, scale=ln[:, kt:kt + 1]).then_inc(s["hT_ready"], 1)

            def silu(n, i):
                act.wait_ge(s["gu_ready"], n * 2 + 1)
                act.wait_ge(s["at_ready"], n + 1)
                act.activation(gate[i][:, :], GU[i][0][:, :], ACT.Silu).then_inc(s["act_ready"], 1)

            def rows(n, i):
                act.wait_ge(s["y_ready"], n + 1)
                act.wait_ge(stored[i], (n - i) * 8 + 1)
                act.activation(out[i][:, :], Y[i][:, 0:D], ACT.Copy).then_inc(s["y_copied"], 1)
                act.wait_ge(s["y_copied"], n + 3)
                act.dma_start(slot(done_rows, n), out[i][:, :]).then_inc(stored[i], 16)

            act.sem_inc(s["at_ready"], 2)
            act.sem_inc(stored[0], 1)
            act.sem_inc(stored[1], 1)
            feed(0, 0)
            silu(0, 0)
            feed(1, 1)
            silu(1, 1)
            with act.Fori(0, SLOTS // 2 - 1) as g:
                for i in range(2):
                    m = g * 2 + i + 1
                    feed(m + 1, i)
                    rows(m - 1, i)
                    silu(m + 1, i)
            rows(SLOTS - 2, 0)
            rows(SLOTS - 1, 1)

        @block.vector
        def _(dve):
            with dve.Fori(0, SLOTS // 2) as g:
                for i in range(2):
                    n = g * 2 + i
                    dve.wait_ge(s["act_ready"], n + 1)
                    dve.wait_ge(s["gu_ready"], n * 2 + 2)
                    dve.tensor_tensor(gate[i][:, :], gate[i][:, :], GU[i][1][:, :], ALU.mult).then_inc(s["gated"], 1)
                    dve.wait_ge(s["at_ready"], n + 3)
                    dve.tensor_copy(act_T[i][:, :, :].rearrange("p k q -> p (k q)"), AT[:, :]).then_inc(s["actT_ready"], 1)


def combine(nc, hold, A2, weight, place, done_rows, out):
    rows = hold.rearrange("p b k s -> p (b k s)").rearrange("p (t d) -> p t d", d=D)
    with ExitStack() as ctx:
        sb = lambda name, shape, dt=F32: ctx.enter_context(nc.sbuf_tensor(name, shape, dt))
        sem = lambda name: ctx.enter_context(nc.semaphore(name))
        E = [sb(f"c_E{k}", [P, NT, D]) for k in range(2)]
        stats = sb("c_stats", [P, NT, 6])
        small = {k: sb(f"c_{k}", [P, NT]) for k in ("mean2", "diff", "var", "std", "scale", "shift")}
        Y = [sb(f"c_Y{i}", [P, D]) for i in range(4)]
        s = {k: sem(f"c_{k}") for k in ("halfway", "mixed", "step", "var_ready", "std_ready", "y_ready", "row_ready", "stored")}
        fetched = [sem(f"c_fetched{i}") for i in range(4)]
        block = ctx.enter_context(nc.Block())

        @block.gpsimd
        def _(pool):
            for t in range(NT):
                for k in range(2):
                    pool.indirect_dma_start(out=E[k][:, t, :], out_offset=None, in_=done_rows,
                                            in_offset=bass.IndirectOffsetOnAxis(ap=place[:, k, t:t + 1], axis=0)).then_inc(fetched[t // 8], 16)

        Q4 = NT // 4

        def part(name, i):
            return small[name][:, Q4 * i:Q4 * (i + 1)]

        @block.vector
        def _(dve):
            dve.sem_inc(s["row_ready"], 1)
            for i in range(4):
                dve.wait_ge(fetched[i], 16 * 2 * Q4)
                for k in range(2):
                    for t in range(Q4 * i, Q4 * (i + 1)):
                        if k:
                            dve.wait_ge(s["halfway"], t + 1)
                        dve.scalar_tensor_tensor(out=A2[:, t, :], in0=E[k][:, t, :], scalar=weight[:, k, t:t + 1], in1=A2[:, t, :],
                                                 op0=ALU.mult, op1=ALU.add).then_inc(s["mixed"] if k else s["halfway"], 1)
                for t in range(Q4 * i, Q4 * (i + 1)):
                    dve.wait_ge(s["mixed"], t + 1)
                    dve.bn_stats(stats[:, t, :], A2[:, t, :]).then_inc(s["step"], 1)
                base = (Q4 + 8) * i + Q4
                dve.wait_ge(s["step"], base)
                link = counted(dve, s["step"], base)
                moments(dve, link, stats[:, Q4 * i:Q4 * (i + 1), :], part("mean2", i), part("diff", i), part("var", i))
                dve.sem_inc(s["var_ready"], 1)
                dve.wait_ge(s["std_ready"], i + 1)
                link(dve.reciprocal(part("scale", i), part("std", i)))
                link(dve.scalar_tensor_tensor(out=part("shift", i), in0=part("mean2", i), scalar=-0.5, in1=part("scale", i),
                                              op0=ALU.mult, op1=ALU.mult))
                dve.sem_inc(s["var_ready"], 1)
                for t in range(Q4 * i, Q4 * (i + 1)):
                    dve.wait_ge(s["y_ready"], t + 1)
                    dve.tensor_tensor(rows[:, t, :], Y[t % 4][:, :], rows[:, t, :], ALU.add).then_inc(s["row_ready"], 1)

        @block.scalar
        def _(act):
            act.sem_inc(s["row_ready"], 3)
            for i in range(4):
                act.wait_ge(s["var_ready"], 2 * i + 1)
                act.activation(part("std", i), part("var", i), ACT.Sqrt).then_inc(s["std_ready"], 1)
                act.wait_ge(s["var_ready"], 2 * i + 2)
                for t in range(Q4 * i, Q4 * (i + 1)):
                    act.wait_ge(s["row_ready"], t + 1)
                    act.activation(Y[t % 4][:, :], A2[:, t, :], ACT.Identity, scale=small["scale"][:, t:t + 1],
                                   bias=small["shift"][:, t:t + 1]).then_inc(s["y_ready"], 1)

        @block.sync
        def _(sp):
            o = out.rearrange("(t p) d -> p t d", p=P)
            for i in range(8):
                sp.wait_ge(s["row_ready"], 4 * i + 8)
                sp.dma_start(o[:, 4 * i:4 * i + 4, :], rows[:, 4 * i:4 * i + 4, :]).then_inc(s["stored"], 16)
            sp.wait_ge(s["stored"], 16 * 8)


def layer(nc, x, w_pair, w_out1, w_qkv2, w_out2, ln1, ln2, w_gate, w13, w2, cos2, sin2, out):
    nc.disable_value_cache = True
    stack_dram = nc.dram_tensor("stack_rows", [NT, P, HEADS2 * STACK], BF16, kind="Internal").ap()
    sorted_rows = nc.dram_tensor("sorted_rows", [SLOTS * P, D], F32, kind="Internal").ap()
    done_rows = nc.dram_tensor("done_rows", [SLOTS * P, D], F32, kind="Internal").ap()
    with ExitStack() as ctx:
        sb = lambda name, shape, dt=F32: ctx.enter_context(nc.sbuf_tensor(name, shape, dt))
        hold = sb("hold", [P, B, KD, S])[:, :, :, :]
        norm_z, shift_z = sb("norm_z", [P, NT])[:, :], sb("shift_z", [P, NT])[:, :]
        normalise(nc, x, hold)
        attention_one(nc, hold, w_pair, w_out1)
        weight = sb("weight", [P, 2, NT])[:, :, :]
        place = sb("place", [P, 2, NT], mybir.dt.uint32)[:, :, :]
        expert_of = sb("expert_of", [1, SLOTS], mybir.dt.int32)[:, :]
        A2 = sb("A2", [P, NT, D])[:, :, :]
        with ExitStack() as inner:
            V2 = inner.enter_context(nc.sbuf_tensor("V2", [P, B, KV2, ST_N, 2 * DH2], F32))[:, :, :, :, :]
            project_two(nc, x, hold, w_qkv2, ln1, cos2, sin2, norm_z, shift_z, V2, stack_dram)
            attention_two(nc, stack_dram, V2, A2)
        with ExitStack() as inner:
            W13 = inner.enter_context(nc.sbuf_tensor("W13", [P, EXPERTS, KD, 2 * FFN], F32))[:, :, :, :]
            w13_in = inner.enter_context(nc.semaphore("w13_in"))
            route(nc, hold, norm_z, shift_z, A2, w_out2, ln2, w_gate, sorted_rows, weight, place, expert_of, W13, w13, w13_in)
            experts(nc, sorted_rows, done_rows, W13, w13_in, w2, ln2, expert_of)
        combine(nc, hold, A2, weight, place, done_rows, out)


def kernel(**inputs):
    import concourse.bacc as bacc
    from concourse.bass_utils import run_bass_kernel_spmd as run

    a = {k: np.asarray(v) for k, v in inputs.items()}

    def turned(w, cols=None):
        return np.ascontiguousarray(w.T.reshape(w.shape[1] // P, P, w.shape[0]).transpose(1, 0, 2))

    f = np.float32
    inv_freq = (f(1) / np.power(f(10000.0), np.arange(0, DH2, 2, dtype=f) / f(DH2))).astype(f)
    angle = np.arange(S, dtype=f)[:, None] * inv_freq[None, :]
    table = lambda left, right: np.ascontiguousarray(
        np.concatenate([left, right], 1).astype(f).reshape(ST_N, P, DH2).transpose(1, 0, 2))
    qkv = np.stack([a["L0_attn_w_q"].reshape(H1 * DH1, D), a["L0_attn_w_k"].reshape(H1 * DH1, D),
                    a["L0_attn_w_v"].reshape(H1 * DH1, D)])
    arrays = {
        "x": np.ascontiguousarray(a["L0_attn_x"].reshape(TOK, D)),
        "w_pair": np.ascontiguousarray(qkv.reshape(3, PAIRS, P, KD, P).transpose(1, 4, 3, 0, 2)),
        "w_out1": turned(a["L0_attn_w_o"]),
        "w_qkv2": turned(a["L0_ffn_wqkv"]),
        "w_out2": turned(a["L0_ffn_wo"]),
        "ln1": np.ascontiguousarray(a["L0_ffn_ln1_w"].reshape(KD, P).T),
        "ln2": np.ascontiguousarray(a["L0_ffn_ln2_w"].reshape(KD, P).T),
        "w_gate": turned(a["L0_ffn_gate_w"]),
        "w13": np.ascontiguousarray(a["L0_ffn_w13"].reshape(EXPERTS, 2 * FFN, KD, P).transpose(3, 0, 2, 1)),
        "w2": np.ascontiguousarray(a["L0_ffn_w2"].reshape(EXPERTS, D, KF, P).transpose(3, 0, 2, 1)),
        "cos2": table(np.cos(angle), np.cos(angle)),
        "sin2": table(-np.sin(angle), np.sin(angle)),
    }
    nc = bacc.Bacc("TRN2", target_bir_lowering=False, num_devices=1)
    args = {k: nc.dram_tensor(f"in_{k}", v.shape, mybir.dt.from_np(v.dtype), kind="ExternalInput").ap()
            for k, v in arrays.items()}
    out = nc.dram_tensor("out_rows", (TOK, D), F32, kind="ExternalOutput").ap()
    layer(nc, out=out, **args)
    r = run(nc, [{f"in_{k}": v for k, v in arrays.items()}], core_ids=[0])
    return r.results[0]["out_rows"].reshape(B, S, D)
```
